# Optimizing a Trainium2 kernel written in Bass

```python
import numpy as np
import jax
import jax.numpy as jnp

def _softmax(x, axis=-1):
    return jax.nn.softmax(x, axis=axis)

def _gelu(x):
    return jax.nn.gelu(x, approximate=True)

def _silu(x):
    return jax.nn.silu(x)

def _sigmoid(x):
    return jax.nn.sigmoid(x)

def _layernorm(x, axis=-1, eps=1e-05):
    m = jnp.mean(x, axis=axis, keepdims=True)
    v = jnp.var(x, axis=axis, keepdims=True)
    return (x - m) / jnp.sqrt(v + eps)

def _scatter_add(tgt, idx, src, axis=0):
    return tgt.at[idx].add(src)

def _segment_sum(src, seg, n):
    return jax.ops.segment_sum(src, seg, n)
kernel_name = 'mk_gps_d1_gnn_r16_40a5b1'

def setup_inputs(seed: int=0):
    np.random.seed(seed)
    _w = jnp.asarray

    def _rec_inputs():
        import jax
        import jax.numpy as jnp
        _gk = jax.random.key(seed)
        x = -0.0003713 + 1 * jax.random.normal(jax.random.fold_in(_gk, 1), (6250, 256), jnp.float32)
        src = jax.random.randint(jax.random.fold_in(_gk, 2), (100000,), 0, 6250, jnp.int32)
        dst = jax.random.randint(jax.random.fold_in(_gk, 3), (100000,), 0, 6250, jnp.int32)
        _o = jnp.argsort(dst, stable=True)
        src = src[_o]
        dst = dst[_o]
        return (x, src, dst)
    x, src, dst = _rec_inputs()

    def _L0_gnn_setup():
        import jax, jax.numpy as jnp
        import numpy as np
        N_NODES = 3125
        N_EDGES = 50000
        IN_DIM = 256
        OUT_DIM = 32
        NUM_HEADS = 8
        key = jax.random.key(seed)
        ks = jax.random.split(key, 9)
        h = jax.random.normal(ks[0], (N_NODES, IN_DIM), dtype=jnp.float32)
        src = jax.random.randint(ks[1], (N_EDGES,), 0, N_NODES, dtype=jnp.int32)
        dst = jax.random.randint(ks[2], (N_EDGES,), 0, N_NODES, dtype=jnp.int32)
        s = 1.0 / np.sqrt(IN_DIM)
        W_lin = jax.random.uniform(ks[3], (IN_DIM, IN_DIM), jnp.float32, -s, s)
        b_lin = jax.random.uniform(ks[4], (IN_DIM,), jnp.float32, -s, s)
        W_gat = jax.random.normal(ks[5], (IN_DIM, NUM_HEADS * OUT_DIM), dtype=jnp.float32) * s
        attn_l = jax.random.normal(ks[6], (NUM_HEADS, OUT_DIM), dtype=jnp.float32) * 0.1
        attn_r = jax.random.normal(ks[7], (NUM_HEADS, OUT_DIM), dtype=jnp.float32) * 0.1
        gat_bias = jnp.zeros((NUM_HEADS * OUT_DIM,), dtype=jnp.float32)
        return {'h': h, 'src': src, 'dst': dst, 'W_lin': W_lin, 'b_lin': b_lin, 'W_gat': W_gat, 'attn_l': attn_l, 'attn_r': attn_r, 'gat_bias': gat_bias}
    _L0_gnn_all = _L0_gnn_setup()
    _L0_gnn_in = {k: v for k, v in _L0_gnn_all.items() if k in ('W_lin', 'b_lin', 'W_gat', 'attn_l', 'attn_r', 'gat_bias')}
    del _L0_gnn_all

    def _L0_mix_setup():
        import jax, jax.numpy as jnp
        import numpy as np
        BN_EPS = 1e-05
        key = jax.random.key(seed)
        ks = jax.random.split(key, 4)
        B, N, D = (8, 512, 256)
        outD = 256
        s = 1.0 / np.sqrt(D)
        return {'feature': jax.random.normal(ks[0], (B, N, D), dtype=jnp.float32), 'W_qk': jax.random.normal(ks[1], (2, D, D), dtype=jnp.float32) * s, 'b_qk': jnp.zeros((2, D), dtype=jnp.float32), 'W_v': jax.random.normal(ks[2], (D, outD), dtype=jnp.float32) * s, 'b_v': jnp.zeros((outD,), dtype=jnp.float32), 'gamma': jnp.ones((D,), dtype=jnp.float32), 'beta': jnp.zeros((D,), dtype=jnp.float32)}
    _L0_mix_all = _L0_mix_setup()
    _L0_mix_in = {k: v for k, v in _L0_mix_all.items() if k in ('W_qk', 'b_qk', 'W_v', 'b_v', 'gamma', 'beta')}
    del _L0_mix_all

    def _L0_ffn_setup():
        import jax, jax.numpy as jnp
        import numpy as np
        B, S, D, F, E, K = (8, 128, 256, 1024, 8, 2)
        key = jax.random.key(seed)
        ks = jax.random.split(key, 10)
        s = 0.02
        return {'x': jax.random.normal(ks[0], (B, S, D), dtype=jnp.float32), 'Wr': jax.random.normal(ks[1], (D, E), dtype=jnp.float32) * s, 'W1s': jax.random.normal(ks[2], (D, F), dtype=jnp.float32) * s, 'b1s': jnp.zeros((F,), dtype=jnp.float32), 'W2s': jax.random.normal(ks[3], (F, D), dtype=jnp.float32) * s, 'b2s': jnp.zeros((D,), dtype=jnp.float32), 'W1p': jax.random.normal(ks[4], (E, D, F), dtype=jnp.float32) * s, 'b1p': jnp.zeros((E, F), dtype=jnp.float32), 'W2p': jax.random.normal(ks[5], (E, F, D), dtype=jnp.float32) * s, 'b2p': jnp.zeros((E, D), dtype=jnp.float32)}
    _L0_ffn_all = _L0_ffn_setup()
    _L0_ffn_in = {k: v for k, v in _L0_ffn_all.items() if k in ('Wr', 'W1s', 'b1s', 'W2s', 'b2s', 'W1p', 'b1p', 'W2p', 'b2p')}
    del _L0_ffn_all
    return {'x': x, 'src': src, 'dst': dst, 'L0_gnn_W_lin': _L0_gnn_in['W_lin'], 'L0_gnn_b_lin': _L0_gnn_in['b_lin'], 'L0_gnn_W_gat': _L0_gnn_in['W_gat'], 'L0_gnn_attn_l': _L0_gnn_in['attn_l'], 'L0_gnn_attn_r': _L0_gnn_in['attn_r'], 'L0_gnn_gat_bias': _L0_gnn_in['gat_bias'], 'L0_mix_W_qk': _L0_mix_in['W_qk'], 'L0_mix_b_qk': _L0_mix_in['b_qk'], 'L0_mix_W_v': _L0_mix_in['W_v'], 'L0_mix_b_v': _L0_mix_in['b_v'], 'L0_mix_gamma': _L0_mix_in['gamma'], 'L0_mix_beta': _L0_mix_in['beta'], 'L0_ffn_Wr': _L0_ffn_in['Wr'], 'L0_ffn_W1s': _L0_ffn_in['W1s'], 'L0_ffn_b1s': _L0_ffn_in['b1s'], 'L0_ffn_W2s': _L0_ffn_in['W2s'], 'L0_ffn_b2s': _L0_ffn_in['b2s'], 'L0_ffn_W1p': _L0_ffn_in['W1p'], 'L0_ffn_b1p': _L0_ffn_in['b1p'], 'L0_ffn_W2p': _L0_ffn_in['W2p'], 'L0_ffn_b2p': _L0_ffn_in['b2p']}

def reference(x, src, dst, L0_gnn_W_lin, L0_gnn_b_lin, L0_gnn_W_gat, L0_gnn_attn_l, L0_gnn_attn_r, L0_gnn_gat_bias, L0_mix_W_qk, L0_mix_b_qk, L0_mix_W_v, L0_mix_b_v, L0_mix_gamma, L0_mix_beta, L0_ffn_Wr, L0_ffn_W1s, L0_ffn_b1s, L0_ffn_W2s, L0_ffn_b2s, L0_ffn_W1p, L0_ffn_b1p, L0_ffn_W2p, L0_ffn_b2p):
    import jax
    import jax.numpy as jnp

    def _L0_gnn_ref(h, src, dst, W_lin, b_lin, W_gat, attn_l, attn_r, gat_bias):
        import jax, jax.numpy as jnp
        import numpy as np
        N_NODES = 3125
        N_EDGES = 50000
        IN_DIM = 256
        OUT_DIM = 32
        NUM_HEADS = 8
        N = h.shape[0]
        h = h @ W_lin + b_lin
        h_in = h
        feat = (h @ W_gat).reshape(N, NUM_HEADS, OUT_DIM)
        el = jnp.sum(feat * attn_l, axis=-1)
        er = jnp.sum(feat * attn_r, axis=-1)
        e = jax.nn.leaky_relu(el[src] + er[dst], 0.2)
        m = jax.ops.segment_max(e, dst, num_segments=N)
        m = jnp.where(jnp.isfinite(m), m, 0.0)
        e = jnp.exp(e - m[dst])
        s = jax.ops.segment_sum(e, dst, num_segments=N)
        a = e / s[dst]
        msg = feat[src] * a[:, :, None]
        out = jax.ops.segment_sum(msg, dst, num_segments=N)
        out = out.reshape(N, NUM_HEADS * OUT_DIM) + gat_bias
        out = jax.nn.leaky_relu(out, 0.01)
        return h_in + out

    def _L0_mix_ref(feature, W_qk, b_qk, W_v, b_v, gamma, beta):
        import jax, jax.numpy as jnp
        import numpy as np
        BN_EPS = 1e-05
        QK = jnp.einsum('bnd,kde->bkne', feature, W_qk) + b_qk[None, :, None, :]
        value = jnp.einsum('bnd,de->bne', feature, W_v) + b_v
        query = QK[:, 0]
        key = QK[:, 1]
        sm = jax.nn.softmax(key, axis=1)
        lam = jnp.einsum('bnd,bne->bde', sm, value)
        mean = jnp.mean(lam, axis=(0, 2), keepdims=True)
        var = jnp.var(lam, axis=(0, 2), keepdims=True)
        bn = (lam - mean) * jax.lax.rsqrt(var + BN_EPS)
        bn = bn * gamma[None, :, None] + beta[None, :, None]
        return jnp.einsum('bnd,bde->bne', query, bn)

    def _L0_ffn_ref(x, Wr, W1s, b1s, W2s, b2s, W1p, b1p, W2p, b2p):
        import jax, jax.numpy as jnp
        import numpy as np
        B, S, D, F, E, K = (8, 128, 256, 1024, 8, 2)
        gelu = lambda t: jax.nn.gelu(t, approximate=False)
        shared = gelu(x @ W1s + b1s) @ W2s + b2s
        rw = jax.nn.softmax(x @ Wr, axis=-1)
        topw, topi = jax.lax.top_k(rw, K)
        topw = topw / jnp.sum(topw, axis=-1, keepdims=True)
        mask = jnp.sum(jax.nn.one_hot(topi, E, dtype=topw.dtype) * topw[..., None], axis=-2)
        h = gelu(jnp.einsum('bsd,edf->bsef', x, W1p) + b1p)
        priv = jnp.einsum('bsef,efd->bsed', h, W2p) + b2p
        routed = jnp.einsum('bsed,bse->bsd', priv, mask)
        return shared + routed
    xn = _layernorm(x, axis=-1)
    x = x + _L0_gnn_ref(xn, src, dst, L0_gnn_W_lin, L0_gnn_b_lin, L0_gnn_W_gat, L0_gnn_attn_l, L0_gnn_attn_r, L0_gnn_gat_bias) + _L0_mix_ref(xn[None], L0_mix_W_qk, L0_mix_b_qk, L0_mix_W_v, L0_mix_b_v, L0_mix_gamma, L0_mix_beta)[0]
    x = x + _L0_ffn_ref(_layernorm(x, axis=-1)[None], L0_ffn_Wr, L0_ffn_W1s, L0_ffn_b1s, L0_ffn_W2s, L0_ffn_b2s, L0_ffn_W1p, L0_ffn_b1p, L0_ffn_W2p, L0_ffn_b2p)[0]
    return x

_drawn_inputs = setup_inputs


def setup_inputs(seed=0):
    import zlib

    import numpy as np

    out = dict(_drawn_inputs(seed))
    spreads = {'L0_gnn_gat_bias': (0.0, 0.8),
     'L0_mix_b_qk': (0.0, 0.1),
     'L0_mix_b_v': (0.0, 0.1),
     'L0_mix_gamma': (1.0, 0.2),
     'L0_mix_beta': (0.0, 0.1),
     'L0_ffn_b1s': (0.0, 0.8),
     'L0_ffn_b2s': (0.0, 0.8),
     'L0_ffn_b1p': (0.0, 0.8),
     'L0_ffn_b2p': (0.0, 0.8)}
    factors = {'L0_gnn_b_lin': 8.0,
     'L0_gnn_W_gat': 8.0,
     'L0_gnn_attn_l': 8.0,
     'L0_gnn_attn_r': 8.0,
     'L0_ffn_Wr': 8.0,
     'L0_ffn_W1s': 8.0,
     'L0_ffn_W2s': 8.0,
     'L0_ffn_W1p': 8.0,
     'L0_ffn_W2p': 8.0}
    for name, (base, spread) in spreads.items():
        noise = np.random.default_rng([zlib.crc32(name.encode()), seed]).standard_normal(out[name].shape)
        drawn = base * np.exp(spread * noise) if base else spread * noise
        out[name] = jnp.asarray(drawn.astype(out[name].dtype))
    for name, factor in factors.items():
        out[name] = (out[name] * factor).astype(out[name].dtype)
    return out
```

```python
from contextlib import ExitStack

import numpy as np

import concourse.bass as bass
from concourse import mybir

F32 = mybir.dt.float32
BF16 = mybir.dt.bfloat16
I32 = mybir.dt.int32
ALU = mybir.AluOpType
ACT = mybir.ActivationFunctionType
AX = mybir.AxisListType
ds = bass.ds
IndexOn = bass.IndirectOffsetOnAxis

P = 128
N, D = 6250, 256
E = 100000
H, HD = 8, 32
X, F = 8, 1024
DK = D // P
FK = F // P
NT = -(-N // P)
LAST = N - (NT - 1) * P
NP = NT * P
STRIP = -(-E // P)
ES = STRIP * P
EL_LAST = E - (P - 1) * STRIP
COLS = 17
STEPS = STRIP // COLS
assert STEPS * COLS == STRIP and STEPS % 2 == 0
GJ = 2
GE = GJ * P
NG = E // GE + NT
NG += -NG % 8
EROWS = E + GE + P * 2
GF = D + H
CH = 512
BLK = P
NRB = (2 * N) // BLK + X
NB = NT + NRB
NB += NB % 2
SLOTS = (NB - NT) * BLK
BIG = 1.0e30
EPS = 1.0e-5
PAD_DST = 8191
CREDIT = 2


def done(t):
    return t + 1 + CREDIT


def freed(t):
    return t + 1


def each_tile(eng):
    with eng.Fori(0, NT // 2) as i:
        for b in range(2):
            yield 2 * i + b, b, P, i
    yield NT - 1, 0, LAST, NT // 2


def pipeline(eng, *stages):
    most = max(lag for lag, _ in stages)

    def step(s, b, i):
        for lag, stage in stages:
            at = (b - lag) % 2
            if isinstance(s, int) and not 0 <= s - lag < NT:
                continue
            rows = LAST if isinstance(s, int) and s - lag == NT - 1 else P
            stage(s - lag, at, rows, i + (b - lag - at) // 2)

    head = most + most % 2
    for s in range(head):
        step(s, s % 2, s // 2)
    with eng.Fori(head // 2, NT // 2) as i:
        for b in range(2):
            step(2 * i + b, b, i)
    for s in range(NT - 1, NT + most):
        step(s, s % 2, s // 2)


def settle(eng, sem):
    eng.sem_inc(sem, 1)


def prime(k, queue, sems, n=1):
    for s in sems:
        for _ in range(n):
            queue.dma_start(k.scrap_d[k.scraps:k.scraps + 1, :], k.ones[0:1, 0:32]).then_inc(s, 16)
            k.scraps += 1


class Chain:

    def __init__(self, eng, sem, start=0):
        self.eng, self.sem, self.start, self.n = eng, sem, start, 0

    def __call__(self, ins):
        ins.then_inc(self.sem, 1)
        self.n += 1
        self.eng.wait_ge(self.sem, self.start + self.n)


class Kernel:
    def __init__(self, nc, ins, out):
        self.nc, self.ins, self.out = nc, ins, out
        self.stack = ExitStack()
        self.names = {}
        self.passed = self.stack.enter_context(nc.semaphore("waits_passed"))
        nc_ = nc
        d = lambda name, shape, dt=F32: nc_.dram_tensor(name, shape, dt).ap()
        self.feat_d = d("feat_rows", (N, D))
        self.el_d = d("el_rows", (N, H))
        self.scan_d = d("scan_rows", (ES, H))
        self.fill_d = d("fill_rows", (ES + NP, 2 * H))
        self.edge_d = d("edge_rows", (EROWS, H + 2))
        self.table_d = d("group_table", (2, 512), I32)
        self.scrap_d, self.scraps = d("scrap_rows", (32, 32)), 0
        self.x2_d = d("x2_rows", (NP, D))
        self.x2n_d = d("x2n_rows", (N, D))
        self.token_d = d("slot_tokens", (NB * BLK + 2 * NP, 1), I32)
        self.block_d = d("block_table", (1, 2 * P), I32)
        self.y_d = d("expert_rows", (NB * BLK, D))

    def sem(self, name):
        return self.stack.enter_context(self.nc.semaphore(name))

    def sb(self, stack, name, shape, dt=F32):
        return stack.enter_context(self.nc.sbuf_tensor(self.unique(name), shape, dt))

    def ps(self, stack, name, shape, dt=F32):
        return stack.enter_context(self.nc.psum_tensor(self.unique(name), shape, dt))

    def unique(self, name):
        self.names[name] = self.names.get(name, 0) + 1
        return name if self.names[name] == 1 else f"{name}_{self.names[name]}"


def prepare(k):
    nc, ins = k.nc, k.ins
    st = ExitStack()
    sb = lambda *a: k.sb(st, *a)
    w_gat = sb("w_gat", [P, DK, D])
    ext = sb("w_ext", [P, DK, D + 2 * H])
    attn = sb("attn_rows", [P, 2, D])
    prod = sb("attn_prod", [P, D])
    w_linT = sb("w_linT", [P, DK, D])
    blin_rep = sb("blin_rep", [P, DK, P])
    blin_col = sb("blin_col", [P, DK])
    idx = sb("idx", [P, P], I32)
    zeros = sb("zeros", [P, 2048])
    ip = k.ps(st, "pT", [P, 2, 2, P])
    pw = k.ps(st, "pW", [P, 2, 512])
    pb = k.ps(st, "pB", [P, 512])
    s_ld, s_c, s_pe, s_cp, s_ch, s_z, s_g, s_ex = (k.sem("p0_" + x) for x in
                                     ("load", "const", "pe", "copied", "dve", "zeros", "pool", "ext"))
    with nc.Block() as block:
        @block.sync
        def _(sp):
            w3 = lambda a: a.rearrange("(k p) n -> p k n", p=P)
            sp.dma_start(k.w_lin[:, :, :], w3(ins["L0_gnn_W_lin"])).then_inc(s_ld, 16)
            sp.dma_start(w_gat[:, :, :], w3(ins["L0_gnn_W_gat"])).then_inc(s_ld, 16)
            sp.dma_start(ext[:, :, 0:D], w3(ins["L0_gnn_W_gat"])).then_inc(s_ld, 16)
            for j, a in enumerate(("L0_gnn_attn_l", "L0_gnn_attn_r")):
                sp.dma_start(attn[:, j, :], ins[a].rearrange("h c -> (h c)").partition_broadcast(P)).then_inc(s_ld, 16)
            with nc.allow_non_contiguous_dma("a short bias column"):
                sp.dma_start(blin_col[:, :], ins["L0_gnn_b_lin"].rearrange("(k p) -> p k", p=P)).then_inc(s_ld, 16)
            sp.wait_ge(s_ld, 96)
            sp.wait_ge(s_z, 1)
            fr = k.fill_d[0:ES, :].rearrange("(p c) h -> p (c h)", p=P)
            w = STRIP * 2 * H
            n = 0
            for a in range(0, w, 2048):
                m = min(2048, w - a)
                sp.dma_start(fr[:, a:a + m], zeros[:, 0:m]).then_inc(s_z, 16)
                n += 1
            tk = k.token_d[0:NB * BLK, :].rearrange("(p c) o -> p (c o)", p=P)
            sp.dma_start(tk, zeros[:, 0:NB].bitcast(I32)).then_inc(s_z, 16)
            sp.wait_ge(s_z, 1 + 16 * (n + 1))

        @block.gpsimd
        def _(pool):
            link = Chain(pool, s_g)
            link(pool.memset(zeros[:, :], 0.0))
            pool.sem_inc(s_z, 1)
            link(pool.memset(k.ident[:, :], 0.0))
            link(pool.affine_select(out=k.ident[:, :], in_=k.ident[:, :], compare_op=ALU.not_equal, fill=1.0,
                                    base=0, pattern=[[-1, P]], channel_multiplier=1))
            link(pool.memset(k.upper[:, :], 1.0))
            link(pool.affine_select(out=k.upper[:, :], in_=k.upper[:, :], compare_op=ALU.is_gt, fill=0.0,
                                    base=0, pattern=[[1, P]], channel_multiplier=-1))
            link(pool.memset(k.ones[:, :], 1.0))
            link(pool.memset(k.eps[:, :], EPS))
            link(pool.iota(idx[:, :], [[1, P]], base=0, channel_multiplier=0))
            pool.tensor_copy(k.iota[:, :], idx[:, :]).then_inc(s_c, 1)

        @block.vector
        def _(dve):
            link = Chain(dve, s_ch)
            dve.wait_ge(s_ld, 96)
            for j in range(2):
                for c in range(DK):
                    link(dve.tensor_tensor(prod[:, :], w_gat[:, c, :], attn[:, j, :], ALU.mult))
                    link(dve.tensor_reduce(ext[:, c, D + j * H:D + (j + 1) * H],
                                           prod[:, :].rearrange("p (h c) -> p h c", h=H), AX.X, ALU.add))
            for c in range(DK):
                last = dve.tensor_copy(blin_rep[:, c, :], blin_col[:, c:c + 1].broadcast_to([P, P]))
            last.then_inc(s_ex, 1)
            dve.wait_ge(s_pe, 1)
            for c in range(DK):
                last = dve.tensor_copy(w_linT[:, c, :].rearrange("p (a b) -> p a b", a=2), ip[:, c, :, :])
            last.then_inc(s_cp, 1)
            dve.wait_ge(s_pe, 2)
            for m in range(2):
                link(dve.tensor_copy(k.w_feat[:, m, :], pw[:, m, 0:D + 2 * H]))
            link(dve.tensor_copy(k.b_feat[:, :], pb[:, 0:D + 2 * H]))

        @block.tensor
        def _(pe):
            pe.wait_ge(s_ld, 96)
            pe.wait_ge(s_c, 1)
            for m in range(2):
                for c in range(DK):
                    last = nc.tensor.transpose(ip[:, c, m, :], k.w_lin[:, m, c * P:(c + 1) * P], k.ident[:, :])
            last.then_inc(s_pe, 1)
            pe.wait_ge(s_cp, 1)
            pe.wait_ge(s_ex, 1)
            for m in range(2):
                for c in range(DK):
                    nc.tensor.matmul(pw[:, m, 0:D + 2 * H], w_linT[:, c, m * P:(m + 1) * P], ext[:, c, :],
                                     start=c == 0, stop=c == DK - 1)
            for c in range(DK):
                last = nc.tensor.matmul(pb[:, 0:D + 2 * H], blin_rep[:, c, :], ext[:, c, :],
                                        start=c == 0, stop=c == DK - 1)
            last.then_inc(s_pe, 1)
    st.close()


def project(k):
    nc, ins = k.nc, k.ins
    st = ExitStack()
    sb = lambda *a: k.sb(st, *a)
    xs, xn, fs = sb("x_in", [P, 2, D]), sb("xn_stage", [P, 2, D]), sb("feat_stage", [P, 2, D + 2 * H])
    stats, mv, sd, rs = (sb(n, [P, 2, w]) for n, w in (("stats", 6), ("mv", 2), ("sd", 1), ("rs", 1)))
    xt = sb("xT_stage", [P, 2, DK, P])
    pt = [k.ps(st, f"pT{b}", [P, 512]) for b in range(2)]
    pf = [k.ps(st, f"pF{b}", [P, 512]) for b in range(2)]
    x_in = [k.sem(f"p1_x_in{b}") for b in range(2)]
    stored = [k.sem(f"p1_stored{b}") for b in range(2)]
    (mv_done, sd_done, xn_done, keep_done, tr_done, xt_done, xtk_done, feat_done, fs_done, er_done, own, own_r, z) = (
        k.sem("p1_" + n) for n in ("mv", "sd", "xn", "xn_kept", "transposed", "xT", "xT_kept", "feat", "fs",
                                   "er", "dve", "dve_rs", "zero"))
    with nc.Block() as block:
        @block.sync
        def _(sp):
            prime(k, sp, stored, 2)

            def load(t, b, rows, i):
                sp.wait_ge(xn_done, freed(t))
                sp.dma_start(xs[:rows, b, :], ins["x"][ds(t * P, rows), :]).then_inc(x_in[b], 16)

            def store(t, b, rows, i):
                sp.wait_ge(fs_done, done(t))
                sp.dma_start(k.feat_d[ds(t * P, rows), :], fs[:rows, b, 0:D]).then_inc(stored[b], 16)
                sp.dma_start(k.el_d[ds(t * P, rows), :], fs[:rows, b, D:D + H]).then_inc(stored[b], 16)

            pipeline(sp, (0, load), (4, store))
            for b in range(2):
                sp.wait_ge(stored[b], 32 * (NT // 2 + 2 - b))

        @block.gpsimd
        def _(pool):
            pool.sem_inc(keep_done, CREDIT)
            pool.memset(k.er[:, :, :], 0.0).then_inc(z, 1)

            def keep(t, b, rows, i):
                pool.wait_ge(xn_done, done(t))
                pool.tensor_copy(k.xn[:rows, ds(t, 1), :], xn[:rows, b:b + 1, :]).then_inc(keep_done, 1)

            pipeline(pool, (0, keep))

        @block.vector
        def _(dve):
            dve.sem_inc(xn_done, CREDIT)
            dve.sem_inc(fs_done, CREDIT)

            def moments(t, b, rows, i):
                dve.wait_ge(x_in[b], 16 * i + 16)
                Chain(dve, own, t)(dve.bn_stats(stats[:rows, b, :], xs[:rows, b, :]))
                settle(dve, k.passed)
                dve.bn_aggr(mv[:rows, b, :], stats[:rows, b, :]).then_inc(mv_done, 1)

            def normalise(t, b, rows, i):
                dve.wait_ge(sd_done, t + 1)
                Chain(dve, own_r, t)(dve.reciprocal(rs[:rows, b, :], sd[:rows, b, :]))
                dve.wait_ge(keep_done, freed(t))
                dve.wait_ge(tr_done, freed(t))
                dve.tensor_scalar(xn[:rows, b, :], xs[:rows, b, :], mv[:rows, b, 0:1], rs[:rows, b, :],
                                  ALU.subtract, ALU.mult).then_inc(xn_done, 1)

            def features(t, b, rows, i):
                dve.wait_ge(feat_done, done(t))
                dve.wait_ge(stored[b], 32 * i + 32)
                dve.wait_ge(er_done, freed(t))
                dve.tensor_tensor(fs[:rows, b, :], pf[b][:rows, 0:D + 2 * H], k.b_feat[:rows, :],
                                  ALU.add).then_inc(fs_done, 1)

            pipeline(dve, (0, moments), (3, features), (1, normalise))

        @block.scalar
        def _(act):
            act.sem_inc(xt_done, CREDIT)
            act.sem_inc(xtk_done, CREDIT)
            act.sem_inc(er_done, CREDIT)
            act.wait_ge(z, 1)

            def deviation(t, b, rows, i):
                act.wait_ge(mv_done, t + 1)
                nc.scalar.activation(sd[:rows, b, :], mv[:rows, b, 1:2], ACT.Sqrt,
                                     bias=k.eps[:rows, :]).then_inc(sd_done, 1)

            def turned(t, b, rows, i):
                act.wait_ge(tr_done, done(t))
                act.wait_ge(feat_done, freed(t))
                src = pt[b][:, 0:DK * P].rearrange("p (k n) -> p k n", k=DK)[:, :, 0:rows]
                nc.scalar.activation(xt[:, b, :, 0:rows], src, ACT.Copy).then_inc(xt_done, 1)
                nc.scalar.activation(k.xnT[:, :, ds(t * P, rows)], src, ACT.Copy).then_inc(xtk_done, 1)

            def keep_er(t, b, rows, i):
                act.wait_ge(fs_done, done(t))
                nc.scalar.activation(k.er[:rows, ds(t, 1), :], fs[:rows, b:b + 1, D + H:D + 2 * H],
                                     ACT.Copy).then_inc(er_done, 1)

            pipeline(act, (0, deviation), (2, turned), (4, keep_er))

        @block.tensor
        def _(pe):
            pe.sem_inc(tr_done, CREDIT)
            pe.sem_inc(feat_done, CREDIT)

            def turn(t, b, rows, i):
                pe.wait_ge(xn_done, done(t))
                pe.wait_ge(xtk_done, freed(t))
                for c in range(DK):
                    last = nc.tensor.transpose(pt[b][:, c * P:c * P + rows], xn[:rows, b, c * P:(c + 1) * P],
                                               k.ident[:rows, :rows])
                last.then_inc(tr_done, 1)

            def product(t, b, rows, i):
                pe.wait_ge(xt_done, done(t))
                pe.wait_ge(fs_done, freed(t))
                for c in range(DK):
                    last = nc.tensor.matmul(pf[b][:rows, 0:D + 2 * H], xt[:, b, c, 0:rows], k.w_feat[:, c, :],
                                            start=c == 0, stop=c == DK - 1)
                last.then_inc(feat_done, 1)

            pipeline(pe, (0, turn), (1, product))
    st.close()


def collect(k):
    nc, ins = k.nc, k.ins
    st = ExitStack()
    sb = lambda *a: k.sb(st, *a)
    src = sb("src_strips", [P, STRIP], I32)
    idx, got = sb("gather_index", [P, 2, COLS], I32), sb("gathered_el", [P, 2, COLS, H])
    dst_i, lo_i = sb("dst_int", [P, STRIP], I32), sb("dst_part", [P, STRIP], I32)
    lo, hi = sb("dst_lo", [P, STRIP]), sb("dst_hi", [P, STRIP])
    oh_lo, oh_hi = sb("onehot_lo", [P, 2, COLS, P], BF16), sb("onehot_hi", [P, 2, COLS, NT], BF16)
    wk, wq, wv = (sb(n, [P, DK, D]) for n in ("w_k", "w_q", "w_v"))
    cols = sb("mix_columns", [P, 4, DK])
    bv, blin = sb("b_v_rows", [P, D]), sb("b_lin_rows", [P, D])
    NC = -(-N // CH)
    kmax = sb("key_max_chunks", [P, DK, NC])
    nb = sb("exp_bias", [P, 3, DK])
    es = sb("expT_stage", [P, 2, DK, P])
    e2 = sb("exp_stage", [P, 2, D])
    pn, pnT, lam, bn, wqT = (sb(n, [P, DK, D]) for n in ("pool_mean", "pool_meanT", "lam", "bn", "w_qT"))
    rden, stats, mv, rg = (sb(n, [P, DK, w]) for n, w in (("rden", 1), ("lam_stats", 6), ("lam_mv", 2), ("lam_rg", 2)))
    bq_rep = sb("b_q_rep", [P, DK, P])
    zf, zb = sb("zero_f32", [P, 512]), sb("zero_bf16", [P, P], BF16)
    pk = [k.ps(st, f"pK{b}", [P, 512]) for b in range(2)]
    pe_ = [k.ps(st, f"pE{b}", [P, 512]) for b in range(2)]
    pp = [k.ps(st, f"pP{b}", [P, 512]) for b in range(2)]
    ph = k.ps(st, "pHist", [P, 512])
    px = k.ps(st, "pX", [P, 512])
    g_land = [k.sem(f"p2_gathered{b}") for b in range(2)]
    (ld, pad, z, kt_mm, key_done, kt_mx, nb_s, exp_done, et_done, e2_done, acc_done, oh_done, hist_mm, kept, own, own_p,
     own_a, tail_pe, tail_v, idx_done, sd_s) = (
        k.sem("p2_" + n) for n in ("loaded", "padded", "zeros", "keys", "keys_again", "keys_max", "bias", "exp",
                                   "exp_transposed", "exp_staged", "accumulated", "onehots", "histogram", "el_kept",
                                   "dve", "pool", "act", "tail_pe", "tail_dve", "index", "lam_sd"))

    def chunks(eng):
        with eng.Fori(0, NC - 1) as c:
            yield c, CH
        yield NC - 1, N - (NC - 1) * CH

    with nc.Block() as block:
        @block.sync
        def _(sp):
            w3 = lambda a: a.rearrange("(k p) n -> p k n", p=P)
            sp.dma_start(wk[:, :, :], w3(ins["L0_mix_W_qk"][1])).then_inc(ld, 16)
            sp.dma_start(wq[:, :, :], w3(ins["L0_mix_W_qk"][0])).then_inc(ld, 16)
            sp.dma_start(wv[:, :, :], w3(ins["L0_mix_W_v"])).then_inc(ld, 16)
            with nc.allow_non_contiguous_dma("short bias columns"):
                for j, a in enumerate((ins["L0_mix_b_qk"][0], ins["L0_mix_b_qk"][1], ins["L0_mix_gamma"],
                                       ins["L0_mix_beta"])):
                    sp.dma_start(cols[:, j, :], a.rearrange("(k p) -> p k", p=P)).then_inc(ld, 16)
            sp.dma_start(bv[:, :], ins["L0_mix_b_v"].partition_broadcast(P)).then_inc(ld, 16)
            sp.dma_start(blin[:, :], ins["L0_gnn_b_lin"].partition_broadcast(P)).then_inc(ld, 16)
            sp.wait_ge(pad, 2)
            sp.dma_start(dst_i[0:P - 1, :], ins["dst"][0:(P - 1) * STRIP].rearrange("(p c) -> p c", c=STRIP)).then_inc(ld, 16)
            sp.dma_start(dst_i[P - 1:P, 0:EL_LAST], ins["dst"][(P - 1) * STRIP:E].rearrange("(p c) -> p c", p=1)).then_inc(ld, 16)

        @block.gpsimd
        def _(pool):
            link = Chain(pool, own_p)
            link(pool.memset(src[:, :], 0))
            pool.sem_inc(pad, 1)
            pool.dma_start(src[0:P - 1, :], ins["src"][0:(P - 1) * STRIP].rearrange("(p c) -> p c", c=STRIP)).then_inc(idx_done, 16)
            pool.dma_start(src[P - 1:P, 0:EL_LAST], ins["src"][(P - 1) * STRIP:E].rearrange("(p c) -> p c", p=1)).then_inc(idx_done, 16)
            pool.wait_ge(idx_done, 32)

            def gathers(s, b):
                pool.tensor_copy(idx[:, b, :], src[:, ds(s * COLS, COLS)]).then_inc(own_p, 1)
                pool.wait_ge(own_p, s + 2)
                settle(pool, k.passed)
                for c in range(COLS):
                    pool.indirect_dma_start(got[:, b, c, :], None, k.el_d[:, :],
                                            IndexOn(ap=idx[:, b, c:c + 1], axis=0)).then_inc(g_land[b], 16)

            def keep(s, b, n):
                pool.wait_ge(g_land[b], 16 * COLS * n)
                pool.tensor_copy(k.el_e[:, ds(s * COLS, COLS), :], got[:, b, :, :]).then_inc(kept, 1)
                pool.wait_ge(kept, s + 1)

            for b in range(2):
                gathers(b, b)
            with pool.Fori(1, STEPS // 2) as i:
                for b in range(2):
                    keep(2 * i + b - 2, b, i)
                    gathers(2 * i + b, b)
            for b in range(2):
                keep(STEPS - 2 + b, b, STEPS // 2)

        @block.vector
        def _(dve):
            link = Chain(dve, own)
            link(dve.memset(dst_i[:, :], PAD_DST))
            dve.sem_inc(pad, 1)
            link(dve.memset(zf[:, :], 0.0))
            link(dve.memset(zb[:, :], 0.0))
            dve.sem_inc(z, 1)
            dve.wait_ge(ld, 16 * 11)
            link(dve.tensor_single_scalar(lo_i[:, :], dst_i[:, :], P - 1, ALU.bitwise_and))
            link(dve.tensor_copy(lo[:, :], lo_i[:, :]))
            link(dve.tensor_single_scalar(lo_i[:, :], dst_i[:, :], 7, ALU.logical_shift_right))
            link(dve.tensor_copy(hi[:, :], lo_i[:, :]))
            for c in range(DK):
                link(dve.tensor_copy(bq_rep[:, c, :], cols[:, 0, c:c + 1].broadcast_to([P, P])))
            dve.sem_inc(kt_mx, 1)
            for c, w in chunks(dve):
                dve.wait_ge(kt_mm, c + 1)
                for m in range(DK):
                    last = dve.reduce_max(kmax[:, m, ds(c, 1)], pk[m][:, 0:w], AX.X)
                last.then_inc(kt_mx, 1)
            dve.wait_ge(kt_mx, NC + 1)
            for m in range(DK):
                link(dve.reduce_max(nb[:, 0, m:m + 1], kmax[:, m, :], AX.X))
            link(dve.tensor_tensor(nb[:, 1, :], nb[:, 0, :], cols[:, 1, :], ALU.add))
            dve.tensor_tensor(nb[:, 2, :], cols[:, 1, :], nb[:, 1, :], ALU.subtract).then_inc(nb_s, 1)
            dve.sem_inc(e2_done, CREDIT)
            for t, b, rows, i in each_tile(dve):
                dve.wait_ge(et_done, done(t))
                dve.wait_ge(acc_done, freed(t))
                dve.tensor_copy(e2[:rows, b, :], pe_[b][:rows, 0:D]).then_inc(e2_done, 1)
            dve.sem_inc(oh_done, CREDIT)
            with dve.Fori(0, STEPS // 2) as i:
                for b in range(2):
                    s = 2 * i + b
                    dve.wait_ge(hist_mm, freed(s))
                    dve.tensor_tensor(oh_lo[:, b, :, :], k.iota[:, :].unsqueeze(1).broadcast_to([P, COLS, P]),
                                      lo[:, ds(s * COLS, COLS)].unsqueeze(2).broadcast_to([P, COLS, P]), ALU.is_equal)
                    dve.tensor_tensor(oh_hi[:, b, :, :], k.iota[:, 0:NT].unsqueeze(1).broadcast_to([P, COLS, NT]),
                                      hi[:, ds(s * COLS, COLS)].unsqueeze(2).broadcast_to([P, COLS, NT]),
                                      ALU.is_equal).then_inc(oh_done, 1)
            dve.wait_ge(hist_mm, done(STEPS))
            link(dve.tensor_copy(k.count[:, :], ph[:, 0:NT]))
            dve.wait_ge(tail_pe, 1)
            for m in range(DK):
                link(dve.reciprocal(rden[:, m, :], pp[m][:, D:D + 1]))
                link(dve.tensor_scalar(pn[:, m, :], pp[m][:, 0:D], rden[:, m, :], None, ALU.mult))
            dve.sem_inc(tail_v, 1)
            dve.wait_ge(tail_pe, 2)
            for m in range(DK):
                link(dve.tensor_copy(pnT[:, :, m * P:(m + 1) * P], pk[m][:, 0:D].rearrange("p (c n) -> p c n", c=DK)))
                link(dve.tensor_copy(wqT[:, :, m * P:(m + 1) * P], pe_[m][:, 0:D].rearrange("p (c n) -> p c n", c=DK)))
            dve.sem_inc(tail_v, 1)
            dve.wait_ge(tail_pe, 3)
            for m in range(DK):
                link(dve.tensor_tensor(lam[:, m, :], pp[m][:, 0:D], bv[:, :], ALU.add))
                link(dve.bn_stats(stats[:, m, :], lam[:, m, :]))
                link(dve.bn_aggr(mv[:, m, :], stats[:, m, :]))
            dve.sem_inc(tail_v, 1)
            dve.wait_ge(sd_s, 1)
            for m in range(DK):
                link(dve.reciprocal(rg[:, m, 1:2], rg[:, m, 0:1]))
                link(dve.tensor_scalar(bn[:, m, :], lam[:, m, :], mv[:, m, 0:1], rg[:, m, 1:2], ALU.subtract, ALU.mult))
                link(dve.tensor_scalar(bn[:, m, :], bn[:, m, :], cols[:, 2, m:m + 1], cols[:, 3, m:m + 1],
                                       ALU.mult, ALU.add))
            dve.sem_inc(tail_v, 1)
            dve.wait_ge(tail_pe, 4)
            for m in range(DK):
                link(dve.tensor_tensor(k.w_lin[:, m, :], pk[m][:, 0:D], k.w_lin[:, m, :], ALU.add))
            link(dve.tensor_tensor(k.cb[:, :], px[:, 0:D], blin[:, :], ALU.add))

        @block.scalar
        def _(act):
            act.sem_inc(exp_done, CREDIT)
            act.wait_ge(nb_s, 1)
            for t, b, rows, i in each_tile(act):
                act.wait_ge(key_done, done(t))
                act.wait_ge(et_done, freed(t))
                for m in range(DK):
                    last = nc.scalar.activation(es[:, b, m, 0:rows], pk[b][:, m * P:m * P + rows], ACT.Exp,
                                                bias=nb[:, 2, m:m + 1])
                last.then_inc(exp_done, 1)
            act.wait_ge(tail_v, 3)
            for m in range(DK):
                last = nc.scalar.activation(rg[:, m, 0:1], mv[:, m, 1:2], ACT.Sqrt, bias=k.eps[:, :])
            last.then_inc(sd_s, 1)

        @block.tensor
        def _(pe):
            pe.wait_ge(ld, 16 * 11)
            pe.wait_ge(z, 1)
            for c, w in chunks(pe):
                pe.wait_ge(kt_mx, c + 1)
                for m in range(DK):
                    for q in range(DK):
                        last = nc.tensor.matmul(pk[m][:, 0:w], wk[:, q, m * P:(m + 1) * P],
                                                k.xnT[:, q, ds(c * CH, w)], start=q == 0, stop=q == DK - 1)
                last.then_inc(kt_mm, 1)
            pe.wait_ge(kt_mx, NC + 1)
            pe.sem_inc(key_done, CREDIT)
            pe.sem_inc(et_done, CREDIT)
            pe.sem_inc(acc_done, CREDIT)
            for m in range(DK):
                nc.tensor.matmul(pp[m][:, 0:D + 1], zf[:, 0:P], zf[:, 0:D + 1], start=True, stop=False)
            nc.tensor.matmul(ph[:, 0:NT], zb[:, :], zb[:, 0:NT], start=True, stop=False)
            for t, b, rows, i in each_tile(pe):
                pe.wait_ge(exp_done, freed(t))
                for m in range(DK):
                    for q in range(DK):
                        last = nc.tensor.matmul(pk[b][:, m * P:m * P + rows], wk[:, q, m * P:(m + 1) * P],
                                                k.xnT[:, q, ds(t * P, rows)], start=q == 0, stop=q == DK - 1)
                last.then_inc(key_done, 1)
                pe.wait_ge(exp_done, done(t))
                pe.wait_ge(e2_done, freed(t))
                for m in range(DK):
                    last = nc.tensor.transpose(pe_[b][:rows, m * P:(m + 1) * P], es[:, b, m, 0:rows], k.ident[:, :])
                last.then_inc(et_done, 1)
                pe.wait_ge(e2_done, done(t))
                for m in range(DK):
                    nc.tensor.matmul(pp[m][:, 0:D], e2[:rows, b, m * P:(m + 1) * P], k.xn[:rows, ds(t, 1), :],
                                     start=False, stop=False)
                    last = nc.tensor.matmul(pp[m][:, D:D + 1], e2[:rows, b, m * P:(m + 1) * P], k.ones[:rows, 0:1],
                                            start=False, stop=False)
                last.then_inc(acc_done, 1)
            for m in range(DK):
                last = nc.tensor.matmul(pp[m][:, 0:D + 1], zf[:, 0:P], zf[:, 0:D + 1], start=False, stop=True)
            last.then_inc(tail_pe, 1)
            pe.sem_inc(hist_mm, CREDIT)
            with pe.Fori(0, STEPS // 2) as i:
                for b in range(2):
                    pe.wait_ge(oh_done, done(2 * i + b))
                    for c in range(COLS):
                        last = nc.tensor.matmul(ph[:, 0:NT], oh_lo[:, b, c, :], oh_hi[:, b, c, :], start=False, stop=False)
                    last.then_inc(hist_mm, 1)
            nc.tensor.matmul(ph[:, 0:NT], zb[:, :], zb[:, 0:NT], start=False, stop=True).then_inc(hist_mm, 1)
            pe.wait_ge(tail_v, 1)
            for m in range(DK):
                for c in range(DK):
                    nc.tensor.transpose(pk[m][:, c * P:(c + 1) * P], pn[:, m, c * P:(c + 1) * P], k.ident[:, :])
                    last = nc.tensor.transpose(pe_[m][:, c * P:(c + 1) * P], wq[:, m, c * P:(c + 1) * P], k.ident[:, :])
            last.then_inc(tail_pe, 1)
            pe.wait_ge(tail_v, 2)
            for m in range(DK):
                for c in range(DK):
                    last = nc.tensor.matmul(pp[m][:, 0:D], pnT[:, c, m * P:(m + 1) * P], wv[:, c, :],
                                            start=c == 0, stop=c == DK - 1)
            last.then_inc(tail_pe, 1)
            pe.wait_ge(tail_v, 4)
            for m in range(DK):
                for c in range(DK):
                    nc.tensor.matmul(pk[m][:, 0:D], wqT[:, c, m * P:(m + 1) * P], bn[:, c, :],
                                     start=c == 0, stop=c == DK - 1)
            for c in range(DK):
                last = nc.tensor.matmul(px[:, 0:D], bq_rep[:, c, :], bn[:, c, :], start=c == 0, stop=c == DK - 1)
            last.then_inc(tail_pe, 1)
    st.close()


def scan_max(k):
    nc, ins = k.nc, k.ins
    st = ExitStack()
    sb = lambda *a: k.sb(st, *a)
    prev = sb("dst_before", [P, STRIP], I32)
    neg = sb("run_starts", [P, STRIP])
    run = sb("running_max", [P, STRIP, H])
    a8, bA, bB, ci, carry = (sb(n, s) for n, s in (("starts8", [P, H]), ("startsT", [H, P]), ("lastT", [H, P]),
                                                    ("carryT", [H, P + 1]), ("carry", [P, H])))
    T1 = NT + 1
    total, base, gk, gkf, val = (sb(n, [P, T1]) for n in ("tile_edges", "tile_start", "group_start", "groups", "offset"))
    gi = sb("groups_int", [P, T1], I32)
    start, has, node, t1, t2 = (sb(n, [P, NT]) for n in ("node_start", "has_edges", "node_number", "tmp1", "tmp2"))
    node_i = sb("node_int", [P, NT], I32)
    sidx, eidx = sb("first_edge", [P, NT], I32), sb("last_edge", [P, NT], I32)
    G4 = 4
    gno_i, gno = sb("group_int", [P, G4], I32), sb("group_number", [P, G4])
    cmp_ = sb("group_compare", [P, G4, T1])
    tg, bs = sb("group_tile", [P, G4, 1]), sb("group_base", [P, G4, 1])
    tab = sb("table", [P, 2, G4], I32)
    mx, v16, zz = sb("node_max", [P, NT, H]), sb("node_er_m", [P, NT, 2 * H]), sb("node_sum", [P, NT, H])
    pa, pb, pc, pd = (k.ps(st, n, [P, 512]) for n in ("pA", "pB", "pC", "pD"))
    (ld, pad, own, carry_s, pe_s, v_s, stored, cons, g_in, m_s, sc) = (
        k.sem("p3_" + n) for n in ("loaded", "padded", "dve", "carry", "pe", "dve_to_pe", "stored", "const", "max_in",
                                   "node_max", "scattered"))
    with nc.Block() as block:
        @block.sync
        def _(sp):
            dst = ins["dst"]
            sp.wait_ge(pad, 1)
            body = (P - 1) * STRIP
            sp.dma_start(k.dst_i[0:P - 1, :], dst[0:body].rearrange("(p c) -> p c", c=STRIP)).then_inc(ld, 16)
            sp.dma_start(k.dst_i[P - 1:P, 0:EL_LAST], dst[body:E].rearrange("(p c) -> p c", p=1)).then_inc(ld, 16)
            sp.dma_start(prev[0:1, 1:STRIP], dst[0:STRIP - 1].rearrange("(p c) -> p c", p=1)).then_inc(ld, 16)
            sp.dma_start(prev[1:P - 1, :], dst[STRIP - 1:body - 1].rearrange("(p c) -> p c", c=STRIP)).then_inc(ld, 16)
            sp.dma_start(prev[P - 1:P, 0:EL_LAST + 1], dst[body - 1:E].rearrange("(p c) -> p c", p=1)).then_inc(ld, 16)
            sp.wait_ge(v_s, 4)
            with nc.allow_non_contiguous_dma("a small table, once"):
                for j in range(2):
                    sp.dma_start(k.table_d[j, :].rearrange("(c p) -> p c", p=P), tab[:, j, :]).then_inc(stored, 16)
            sp.wait_ge(v_s, 6)
            sp.dma_start(k.scan_d.rearrange("(p c) h -> p (c h)", p=P), run[:, :, :].rearrange("p c h -> p (c h)")).then_inc(stored, 16)
            sp.wait_ge(stored, 48)

        @block.gpsimd
        def _(pool):
            pool.iota(node_i[:, :], [[P, NT]], base=0, channel_multiplier=1).then_inc(cons, 1)
            pool.iota(gno_i[:, :], [[P, G4]], base=0, channel_multiplier=1).then_inc(cons, 1)
            pool.wait_ge(stored, 48)
            pool.wait_ge(v_s, 4)
            for t in range(NT):
                pool.indirect_dma_start(mx[:, t, :], None, k.scan_d[:, :], IndexOn(ap=eidx[:, t:t + 1], axis=0)).then_inc(g_in, 16)
            pool.wait_ge(m_s, 1)
            for t in range(NT):
                pool.indirect_dma_start(k.fill_d[:, :], IndexOn(ap=sidx[:, t:t + 1], axis=0), v16[:, t, :], None).then_inc(sc, 16)
            pool.wait_ge(sc, 16 * NT)

        @block.vector
        def _(dve):
            link = Chain(dve, own)
            link(dve.memset(k.dst_i[:, :], PAD_DST))
            link(dve.memset(prev[:, :], -1))
            dve.sem_inc(pad, 1)
            dve.wait_ge(pe_s, 1)
            link(dve.memset(total[:, :], 0.0))
            link(dve.tensor_copy(total[:, 0:NT], pb[:, 0:NT]))
            link(dve.memset(base[:, :], 0.0))
            link(dve.memset(gk[:, :], 0.0))
            link(dve.tensor_tensor_scan(base[:, 1:T1], k.ones[:, 0:NT], total[:, 0:NT], 0.0, ALU.mult, ALU.add))
            link(dve.tensor_tensor(start[:, :], pa[:, 0:NT], base[:, 0:NT], ALU.add))
            dve.wait_ge(cons, 2)
            link(dve.tensor_copy(node[:, :], node_i[:, :]))
            link(dve.tensor_copy(gno[:, :], gno_i[:, :]))
            link(dve.tensor_scalar(has[:, :], k.count[:, :], 0.0, None, ALU.is_gt))
            link(dve.tensor_tensor(t1[:, :], start[:, :], has[:, :], ALU.mult))
            link(dve.tensor_scalar(node[:, :], node[:, :], float(ES), None, ALU.add))
            link(dve.tensor_tensor(t2[:, :], node[:, :], has[:, :], ALU.mult))
            link(dve.tensor_tensor(t2[:, :], node[:, :], t2[:, :], ALU.subtract))
            link(dve.tensor_tensor(sidx[:, :], t1[:, :], t2[:, :], ALU.add))
            link(dve.tensor_tensor(t1[:, :], start[:, :], k.count[:, :], ALU.add))
            link(dve.tensor_scalar(eidx[:, :], t1[:, :], -1.0, 0.0, ALU.add, ALU.max))
            link(dve.tensor_scalar(t1[:, :], total[:, 0:NT], float(GE - 1), None, ALU.add))
            link(dve.tensor_copy(gi[:, 0:NT], t1[:, :]))
            link(dve.tensor_single_scalar(gi[:, 0:NT], gi[:, 0:NT], GE.bit_length() - 1, ALU.logical_shift_right))
            link(dve.tensor_copy(gkf[:, 0:NT], gi[:, 0:NT]))
            link(dve.tensor_tensor_scan(gk[:, 1:T1], k.ones[:, 0:NT], gkf[:, 0:NT], 0.0, ALU.mult, ALU.add))
            link(dve.scalar_tensor_tensor(val[:, :], gk[:, :], -float(GE), base[:, :], ALU.mult, ALU.add))
            b3 = lambda a, n: a.unsqueeze(1).broadcast_to([P, G4, n])
            link(dve.tensor_tensor(cmp_[:, :, 0:NT], b3(gk[:, 1:T1], NT), gno[:, :].unsqueeze(2).broadcast_to([P, G4, NT]), ALU.is_le))
            link(dve.tensor_reduce(tg[:, :, 0], cmp_[:, :, 0:NT], AX.X, ALU.add))
            link(dve.tensor_tensor(cmp_[:, :, :], b3(k.iota[:, 0:T1], T1), tg[:, :, :].broadcast_to([P, G4, T1]), ALU.is_equal))
            link(dve.tensor_tensor(cmp_[:, :, :], cmp_[:, :, :], b3(val[:, :], T1), ALU.mult))
            link(dve.tensor_reduce(bs[:, :, 0], cmp_[:, :, :], AX.X, ALU.add))
            link(dve.scalar_tensor_tensor(bs[:, :, 0], gno[:, :], float(GE), bs[:, :, 0], ALU.mult, ALU.add))
            link(dve.tensor_scalar(tab[:, 0, :], bs[:, :, 0], float(E), None, ALU.min))
            link(dve.tensor_scalar(tab[:, 1, :], tg[:, :, 0], float(NT - 1), None, ALU.min))
            dve.sem_inc(v_s, 4)
            dve.wait_ge(ld, 80)
            link(dve.tensor_tensor(k.cont[:, :], k.dst_i[:, :], prev[:, :], ALU.is_equal))
            link(dve.tensor_scalar(neg[:, :], k.cont[:, :], 1.0, BIG, ALU.subtract, ALU.mult))
            for h in range(H):
                link(dve.tensor_tensor_scan(run[:, :, h], neg[:, :], k.el_e[:, :, h], -BIG, ALU.add, ALU.max))
            link(dve.tensor_reduce(a8[:, 0:1], neg[:, :], AX.X, ALU.min))
            link(dve.tensor_copy(a8[:, 1:H], a8[:, 0:1].broadcast_to([P, H - 1])))
            dve.sem_inc(v_s, 1)
            dve.wait_ge(pe_s, 2)
            link(dve.tensor_copy(bA[:, :], pc[0:H, 0:P]))
            link(dve.tensor_copy(bB[:, :], pd[0:H, 0:P]))
            link(dve.memset(ci[:, :], -BIG))
            link(dve.tensor_tensor_scan(ci[:, 1:P + 1], bA[:, :], bB[:, :], -BIG, ALU.add, ALU.max))
            dve.sem_inc(carry_s, 1)
            dve.wait_ge(pe_s, 3)
            link(dve.tensor_copy(carry[:, :], pc[:, 0:H]))
            for h in range(H):
                link(dve.tensor_tensor_scan(run[:, :, h], neg[:, :], k.el_e[:, :, h], carry[:, h:h + 1], ALU.add, ALU.max))
            dve.sem_inc(v_s, 1)
            link(dve.tensor_copy(v16[:, :, 0:H], k.er[:, :, :]))
            dve.wait_ge(g_in, 16 * NT)
            link(dve.tensor_tensor(zz[:, :, :], mx[:, :, :], k.er[:, :, :], ALU.add))
            link(dve.scalar_tensor_tensor(v16[:, :, H:2 * H], zz[:, :, :], 0.2, zz[:, :, :], ALU.mult, ALU.max))
            dve.sem_inc(m_s, 1)

        @block.tensor
        def _(pe):
            nc.tensor.matmul(pa[:, 0:NT], k.upper[:, :], k.count[:, :], start=True, stop=True)
            nc.tensor.matmul(pb[:, 0:NT], k.ones[:, :], k.count[:, :], start=True, stop=True).then_inc(pe_s, 1)
            pe.wait_ge(v_s, 5)
            nc.tensor.transpose(pc[0:H, 0:P], a8[:, :], k.ident[:, :])
            nc.tensor.transpose(pd[0:H, 0:P], run[:, STRIP - 1, :], k.ident[:, :]).then_inc(pe_s, 1)
            pe.wait_ge(carry_s, 1)
            nc.tensor.transpose(pc[:, 0:H], ci[:, 0:P], k.ident[0:H, 0:H]).then_inc(pe_s, 1)
    st.close()


def scan_weights(k):
    nc, ins = k.nc, k.ins
    st = ExitStack()
    sb = lambda *a: k.sb(st, *a)
    R = H + 2
    fl = sb("node_values", [P, STRIP, 2 * H])
    rec = sb("records", [P, STRIP, R])
    src = sb("src_strips", [P, STRIP], I32)
    pcont, zero = sb("run_from_before", [P, STRIP]), sb("zero_strip", [P, STRIP])
    tail = sb("tail_records", [P, (EROWS - E) // P, R])
    a16, bA, bB, ci, carry = (sb(n, s) for n, s in (("cont16", [P, 2 * H]), ("contT", [2 * H, P]), ("lastT", [2 * H, P]),
                                                    ("carryT", [2 * H, P + 1]), ("carry", [P, 2 * H])))
    pc, pd = (k.ps(st, n, [P, 512]) for n in ("pC", "pD"))
    ld, pad, own, pe_s, v_s, stored, ex = (k.sem("p4_" + n) for n in ("loaded", "padded", "dve", "pe", "dve_done",
                                                                      "stored", "exp"))
    with nc.Block() as block:
        @block.sync
        def _(sp):
            body = (P - 1) * STRIP
            sp.dma_start(fl[:, :, :].rearrange("p c h -> p (c h)"), k.fill_d[0:ES, :].rearrange("(p c) h -> p (c h)", p=P)).then_inc(ld, 16)
            sp.wait_ge(pad, 1)
            sp.dma_start(src[0:P - 1, :], ins["src"][0:body].rearrange("(p c) -> p c", c=STRIP)).then_inc(ld, 16)
            sp.dma_start(src[P - 1:P, 0:EL_LAST], ins["src"][body:E].rearrange("(p c) -> p c", p=1)).then_inc(ld, 16)
            sp.wait_ge(ex, 1)
            sp.wait_ge(v_s, 3)
            sp.dma_start(k.edge_d[0:body, :].rearrange("(p c) r -> p (c r)", c=STRIP), rec[0:P - 1, :, :].rearrange("p c r -> p (c r)")).then_inc(stored, 16)
            sp.dma_start(k.edge_d[body:E, :].rearrange("(p c) r -> p (c r)", p=1), rec[P - 1:P, 0:EL_LAST, :].rearrange("p c r -> p (c r)")).then_inc(stored, 16)
            sp.dma_start(k.edge_d[E:EROWS, :].rearrange("(p c) r -> p (c r)", p=P), tail[:, :, :].rearrange("p c r -> p (c r)")).then_inc(stored, 16)
            sp.wait_ge(stored, 48)

        @block.scalar
        def _(act):
            act.wait_ge(v_s, 4)
            nc.scalar.activation(rec[:, :, 0:H], k.el_e[:, :, :], ACT.Exp).then_inc(ex, 1)

        @block.vector
        def _(dve):
            link = Chain(dve, own)
            link(dve.memset(src[:, :], 0))
            dve.sem_inc(pad, 1)
            link(dve.memset(zero[:, :], 0.0))
            link(dve.memset(tail[:, :, :], 0.0))
            link(dve.memset(tail[:, :, H:H + 1], float(PAD_DST)))
            link(dve.tensor_tensor_scan(pcont[:, :], k.cont[:, :], zero[:, :], 1.0, ALU.mult, ALU.add))
            link(dve.tensor_copy(a16[:, :], pcont[:, STRIP - 1:STRIP].broadcast_to([P, 2 * H])))
            dve.wait_ge(ld, 48)
            link(dve.tensor_copy(rec[:, :, H], k.dst_i[:, :]))
            link(dve.tensor_copy(rec[:, :, H + 1].bitcast(I32), src[:, :]))
            for h in range(2 * H):
                link(dve.tensor_tensor_scan(fl[:, :, h], k.cont[:, :], fl[:, :, h], 0.0, ALU.mult, ALU.add))
            dve.sem_inc(v_s, 1)
            dve.wait_ge(pe_s, 1)
            link(dve.tensor_copy(bA[:, :], pc[0:2 * H, 0:P]))
            link(dve.tensor_copy(bB[:, :], pd[0:2 * H, 0:P]))
            link(dve.memset(ci[:, 0:1], 0.0))
            link(dve.tensor_tensor_scan(ci[:, 1:P + 1], bA[:, :], bB[:, :], 0.0, ALU.mult, ALU.add))
            dve.sem_inc(v_s, 1)
            dve.wait_ge(pe_s, 2)
            link(dve.tensor_copy(carry[:, :], pc[:, 0:2 * H]))
            for h in range(2 * H):
                link(dve.scalar_tensor_tensor(fl[:, :, h], pcont[:, :], carry[:, h:h + 1], fl[:, :, h], ALU.mult, ALU.add))
            dve.sem_inc(v_s, 1)
            link(dve.tensor_tensor(k.el_e[:, :, :], k.el_e[:, :, :], fl[:, :, 0:H], ALU.add))
            link(dve.scalar_tensor_tensor(k.el_e[:, :, :], k.el_e[:, :, :], 0.2, k.el_e[:, :, :], ALU.mult, ALU.max))
            link(dve.tensor_tensor(k.el_e[:, :, :], k.el_e[:, :, :], fl[:, :, H:2 * H], ALU.subtract))
            dve.sem_inc(v_s, 1)

        @block.tensor
        def _(pe):
            pe.wait_ge(v_s, 1)
            nc.tensor.transpose(pc[0:2 * H, 0:P], a16[:, :], k.ident[:, :])
            nc.tensor.transpose(pd[0:2 * H, 0:P], fl[:, STRIP - 1, :], k.ident[:, :]).then_inc(pe_s, 1)
            pe.wait_ge(v_s, 2)
            nc.tensor.transpose(pc[:, 0:2 * H], ci[:, 0:P], k.ident[0:2 * H, 0:2 * H]).then_inc(pe_s, 1)
    st.close()


def message(k):
    nc, ins = k.nc, k.ins
    st = ExitStack()
    sb = lambda *a: k.sb(st, *a)
    U, R = 8, H + 2
    nodes_i, nodes = sb("nodes_int", [P, 1024], I32), sb("node_numbers", [P, NP])
    tabs = sb("table_row", [1, 2 * 512], I32)
    rec = sb("group_records", [P, U, GJ * R])
    feat = sb("group_feat", [P, U, GJ, D])
    oh, wt = sb("group_onehot", [P, U, GJ, P]), sb("group_weighted", [P, U, GJ, GF])
    ps = [k.ps(st, f"pSum{u}", [P, 512]) for u in range(U)]
    rec_in = [k.sem(f"p5_record{u}") for u in range(U)]
    feat_in = [k.sem(f"p5_feat{u}") for u in range(U)]
    zero, tab_in, made, ex_done, mm_done, sum_done, ip = (k.sem("p5_" + n) for n in ("zero", "table", "weighted",
                                                          "weights", "products", "sums", "nodes"))
    with nc.Block() as block:
        @block.sync
        def _(sp):
            sp.dma_start(tabs[:, :], k.table_d.rearrange("a g -> (a g)").rearrange("(o g) -> o g", o=1)).then_inc(tab_in, 16)
            sp.wait_ge(tab_in, 16)
            with sp.Fori(0, NG // U) as i:
                for u in range(U):
                    g = U * i + u
                    base = sp.value_load(tabs[0:1, ds(g, 1)], min_val=0, max_val=E)
                    sp.wait_ge(sum_done, g + 1)
                    sp.dma_start(rec[:, u, :], k.edge_d[ds(base, GE), :].rearrange("(p j) r -> p (j r)", j=GJ)).then_inc(rec_in[u], 16)

        @block.gpsimd
        def _(pool):
            for a in range(0, NP, 1024):
                w = min(1024, NP - a)
                pool.iota(nodes_i[:, 0:w], [[1, w]], base=a, channel_multiplier=0).then_inc(ip, 1)
                pool.wait_ge(ip, 2 * (a // 1024) + 1)
                pool.tensor_copy(nodes[:, a:a + w], nodes_i[:, 0:w]).then_inc(ip, 1)
                pool.wait_ge(ip, 2 * (a // 1024) + 2)
            with pool.Fori(0, NG // U) as i:
                for u in range(U):
                    g = U * i + u
                    pool.wait_ge(rec_in[u], 16 * i + 16)
                    settle(pool, k.passed)
                    pool.wait_ge(made, g + 1)
                    settle(pool, k.passed)
                    for j in range(GJ):
                        at = j * R + H + 1
                        pool.indirect_dma_start(feat[:, u, j, :], None, k.feat_d[:, :],
                                                IndexOn(ap=rec[:, u, at:at + 1].bitcast(I32), axis=0)).then_inc(feat_in[u], 16)

        @block.scalar
        def _(act):
            act.sem_inc(ex_done, U)
            with act.Fori(0, NG // U) as i:
                for u in range(U):
                    act.wait_ge(rec_in[u], 16 * i + 16)
                    act.wait_ge(mm_done, U * i + u + 1)
                    r = rec[:, u, :].rearrange("p (j r) -> p j r", j=GJ)
                    nc.scalar.activation(wt[:, u, :, D:GF], r[:, :, 0:H], ACT.Copy).then_inc(ex_done, 1)

        @block.vector
        def _(dve):
            dve.memset(k.agg[:, :, :], 0.0).then_inc(zero, 1)
            dve.wait_ge(zero, 1)
            dve.wait_ge(ip, 2 * (-(-NP // 1024)))
            dve.wait_ge(tab_in, 16)
            dve.sem_inc(made, U)
            dve.sem_inc(sum_done, U)
            with dve.Fori(0, NG // U) as i:
                tile = {}

                def weigh(u):
                    g = U * i + u
                    tile[u] = dve.value_load(tabs[0:1, ds(512 + g, 1)], min_val=0, max_val=NT - 1)
                    dve.wait_ge(rec_in[u], 16 * i + 16)
                    dve.wait_ge(mm_done, g + 1)
                    for j in range(GJ):
                        dve.tensor_scalar(oh[:, u, j, :], nodes[:, ds(tile[u] * P, P)], rec[:, u, j * R + H:j * R + H + 1],
                                          None, ALU.is_equal)
                    dve.wait_ge(feat_in[u], 16 * GJ * (i + 1))
                    for j in range(GJ):
                        last = dve.tensor_tensor(wt[:, u, j, 0:D].rearrange("p (h c) -> p h c", h=H),
                                                 feat[:, u, j, :].rearrange("p (h c) -> p h c", h=H),
                                                 rec[:, u, j * R:j * R + H].unsqueeze(2).broadcast_to([P, H, HD]), ALU.mult)
                    last.then_inc(made, 1)

                def add(u):
                    g = U * i + u
                    dve.wait_ge(mm_done, g + 1 + U)
                    dve.wait_ge(sum_done, g + U)
                    dve.tensor_tensor(k.agg[:, ds(tile[u], 1), :], k.agg[:, ds(tile[u], 1), :],
                                      ps[u][:, 0:GF].unsqueeze(1), ALU.add).then_inc(sum_done, 1)

                weigh(0)
                for u in range(1, U):
                    weigh(u)
                    add(u - 1)
                add(U - 1)

        @block.tensor
        def _(pe):
            pe.sem_inc(mm_done, U)
            with pe.Fori(0, NG // U) as i:
                for u in range(U):
                    g = U * i + u
                    pe.wait_ge(made, g + 1 + U)
                    pe.wait_ge(ex_done, g + 1 + U)
                    pe.wait_ge(sum_done, g + 1)
                    for j in range(GJ):
                        last = nc.tensor.matmul(ps[u][:, 0:GF], oh[:, u, j, :], wt[:, u, j, :], start=j == 0, stop=j == GJ - 1)
                    last.then_inc(mm_done, 1)
    st.close()


def update(k):
    nc, ins = k.nc, k.ins
    st = ExitStack()
    sb = lambda *a: k.sb(st, *a)
    gb, wr = sb("gat_bias_rows", [P, D]), sb("w_router", [P, DK, X])
    xs, xn = sb("x_in", [P, 2, D]), sb("x2n_stage", [P, 2, D])
    xt, x2t = sb("xT_stage", [P, 2, DK, P]), sb("x2T_stage", [P, 2, DK, P])
    s1, g1, xc = sb("weight_sum", [P, H]), sb("messages", [P, D]), sb("x_plus_bias", [P, 2, D])
    stats, mv, sd, rs = (sb(n, [P, 2, w]) for n, w in (("stats", 6), ("mv", 2), ("sd", 1), ("rs", 1)))
    pu = [k.ps(st, f"pU{b}", [P, 512]) for b in range(2)]
    pt = [k.ps(st, f"pT{b}", [P, 512]) for b in range(2)]
    pl = [k.ps(st, f"pL{b}", [P, 512]) for b in range(2)]
    x_in = [k.sem(f"p6_x_in{b}") for b in range(2)]
    stored = [k.sem(f"p6_stored{b}") for b in range(2)]
    (ld, xt_done, mm_done, u_done, mv_done, sd_done, xn_done, tr_done, x2t_done, lg_mm, lg_done, own, own_r, xc_done, x2_st, z) = (
        k.sem("p6_" + n) for n in ("loaded", "xT", "products", "x2", "mv", "sd", "x2n", "transposed", "x2T",
                                   "logits_mm", "logits", "dve", "dve_rs", "x_plus_bias", "x2_stored", "zero"))
    LINKS = 7
    with nc.Block() as block:
        @block.sync
        def _(sp):
            sp.dma_start(gb[:, :], ins["L0_gnn_gat_bias"].partition_broadcast(P)).then_inc(ld, 16)
            sp.dma_start(wr[:, :, :], ins["L0_ffn_Wr"].rearrange("(k p) n -> p k n", p=P)).then_inc(ld, 16)
            prime(k, sp, stored)

            def load(t, b, rows, i):
                sp.wait_ge(u_done, freed(t))
                sp.dma_start(xs[:rows, b, :], ins["x"][ds(t * P, rows), :]).then_inc(x_in[b], 16)

            def store(t, b, rows, i):
                sp.wait_ge(xn_done, done(t))
                sp.dma_start(k.x2_d[ds(t * P, rows), :].unsqueeze(1), k.agg[:rows, ds(t, 1), 0:D]).then_inc(x2_st, 16)
                sp.dma_start(k.x2n_d[ds(t * P, rows), :], xn[:rows, b, :]).then_inc(stored[b], 16)

            pipeline(sp, (0, load), (2, store))
            for b in range(2):
                sp.wait_ge(stored[b], 16 * (NT // 2 + 2 - b))
            sp.wait_ge(x2_st, 16 * NT)

        @block.gpsimd
        def _(pool):
            def x_bias(t, b, rows, i):
                pool.wait_ge(x_in[b], 16 * i + 16)
                pool.wait_ge(u_done, freed(t))
                pool.tensor_tensor(xc[:rows, b, :], xs[:rows, b, :], k.cb[:rows, :], ALU.add).then_inc(xc_done, 1)

            pipeline(pool, (0, x_bias))

        @block.vector
        def _(dve):
            dve.memset(k.logits[:, :, :], 0.0).then_inc(z, 1)
            dve.sem_inc(u_done, CREDIT)
            dve.sem_inc(xn_done, CREDIT)
            dve.wait_ge(ld, 32)
            h3 = lambda a: a.rearrange("p (h c) -> p h c", h=H)

            def residual(t, b, rows, i):
                link = Chain(dve, own, LINKS * t)
                link(dve.tensor_scalar(s1[:rows, :].unsqueeze(1), k.agg[:rows, ds(t, 1), D:GF], 1.0e-30, None, ALU.max))
                link(dve.reciprocal(s1[:rows, :], s1[:rows, :]))
                link(dve.tensor_tensor(h3(g1[:rows, :]), k.agg[:rows, ds(t, 1), 0:D].rearrange("p a (h c) -> p (a h) c", h=H),
                                       s1[:rows, :].unsqueeze(2).broadcast_to([rows, H, HD]), ALU.mult))
                link(dve.tensor_tensor(g1[:rows, :], g1[:rows, :], gb[:rows, :], ALU.add))
                link(dve.scalar_tensor_tensor(g1[:rows, :], g1[:rows, :], 0.01, g1[:rows, :], ALU.mult, ALU.max))
                dve.wait_ge(x_in[b], 16 * i + 16)
                dve.wait_ge(xc_done, t + 1)
                link(dve.tensor_tensor(g1[:rows, :], g1[:rows, :], xc[:rows, b, :], ALU.add))
                dve.wait_ge(mm_done, done(t))
                x2 = k.agg[:rows, ds(t, 1), 0:D].rearrange("p a d -> p (a d)")
                dve.tensor_tensor(x2, pu[b][:rows, 0:D], g1[:rows, :], ALU.add).then_inc(u_done, 1)
                dve.wait_ge(u_done, done(t))
                settle(dve, k.passed)
                link(dve.bn_stats(stats[:rows, b, :], x2))
                settle(dve, k.passed)
                dve.bn_aggr(mv[:rows, b, :], stats[:rows, b, :]).then_inc(mv_done, 1)
                assert link.n == LINKS

            def normalise(t, b, rows, i):
                dve.wait_ge(sd_done, t + 1)
                Chain(dve, own_r, t)(dve.reciprocal(rs[:rows, b, :], sd[:rows, b, :]))
                dve.wait_ge(tr_done, freed(t))
                dve.wait_ge(stored[b], 16 * i + 16)
                dve.tensor_scalar(xn[:rows, b, :], k.agg[:rows, ds(t, 1), 0:D].rearrange("p a d -> p (a d)"), mv[:rows, b, 0:1], rs[:rows, b, :],
                                  ALU.subtract, ALU.mult).then_inc(xn_done, 1)

            pipeline(dve, (0, residual), (1, normalise))

        @block.scalar
        def _(act):
            act.sem_inc(xt_done, CREDIT)
            act.sem_inc(x2t_done, CREDIT)
            act.sem_inc(lg_done, CREDIT)
            act.wait_ge(z, 1)

            def stage_xT(t, b, rows, i):
                act.wait_ge(mm_done, freed(t))
                nc.scalar.activation(xt[:, b, :, 0:rows], k.xnT[:, :, ds(t * P, rows)], ACT.Copy).then_inc(xt_done, 1)

            def deviation(t, b, rows, i):
                act.wait_ge(mv_done, t + 1)
                nc.scalar.activation(sd[:rows, b, :], mv[:rows, b, 1:2], ACT.Sqrt, bias=k.eps[:rows, :]).then_inc(sd_done, 1)

            def turned(t, b, rows, i):
                act.wait_ge(tr_done, done(t))
                act.wait_ge(lg_mm, freed(t))
                nc.scalar.activation(x2t[:, b, :, 0:rows], pt[b][:, 0:DK * P].rearrange("p (k n) -> p k n", k=DK)[:, :, 0:rows],
                                     ACT.Copy).then_inc(x2t_done, 1)

            def keep_logits(t, b, rows, i):
                act.wait_ge(lg_mm, done(t))
                nc.scalar.activation(k.logits[:rows, ds(t, 1), :], pl[b][:rows, 0:X].unsqueeze(1), ACT.Copy).then_inc(lg_done, 1)

            pipeline(act, (0, stage_xT), (3, turned), (4, keep_logits), (2, deviation))

        @block.tensor
        def _(pe):
            for s in (mm_done, tr_done, lg_mm):
                pe.sem_inc(s, CREDIT)
            pe.wait_ge(ld, 32)

            def product(t, b, rows, i):
                pe.wait_ge(xt_done, done(t))
                pe.wait_ge(u_done, freed(t))
                for c in range(DK):
                    last = nc.tensor.matmul(pu[b][:rows, 0:D], xt[:, b, c, 0:rows], k.w_lin[:, c, :], start=c == 0, stop=c == DK - 1)
                last.then_inc(mm_done, 1)

            def turn(t, b, rows, i):
                pe.wait_ge(xn_done, done(t))
                pe.wait_ge(x2t_done, freed(t))
                for c in range(DK):
                    last = nc.tensor.transpose(pt[b][:, c * P:c * P + rows], xn[:rows, b, c * P:(c + 1) * P], k.ident[:rows, :rows])
                last.then_inc(tr_done, 1)

            def router(t, b, rows, i):
                pe.wait_ge(x2t_done, done(t))
                pe.wait_ge(lg_done, freed(t))
                for c in range(DK):
                    last = nc.tensor.matmul(pl[b][:rows, 0:X], x2t[:, b, c, 0:rows], wr[:, c, :], start=c == 0, stop=c == DK - 1)
                last.then_inc(lg_mm, 1)

            pipeline(pe, (0, product), (2, turn), (3, router))
    st.close()


def load_weights(k, queue):
    shared = ("L0_ffn_W1s", "L0_ffn_b1s", "L0_ffn_W2s", "L0_ffn_b2s")
    routed = ("L0_ffn_W1p", "L0_ffn_b1p", "L0_ffn_W2p", "L0_ffn_b2p")
    for e in (X, *range(X)):
        u, c1, d, c2 = (k.ins[n] if e == X else k.ins[n][e] for n in (shared if e == X else routed))
        landed = k.shared_in if e == X else k.routed_in
        queue.dma_start(k.w_up[:, e, :, :], u.rearrange("(c p) f -> p c f", p=P)).then_inc(landed, 16)
        queue.dma_start(k.w_down[:, e, :, :], d.rearrange("(c p) n -> p c n", p=P)).then_inc(landed, 16)
        with k.nc.allow_non_contiguous_dma("short bias columns"):
            queue.dma_start(k.b_up[:, e, :], c1.rearrange("(c p) -> p c", p=P)).then_inc(landed, 16)
        queue.dma_start(k.b_down[:, e, :], c2.partition_broadcast(P)).then_inc(landed, 16)


def route(k):
    nc = k.nc
    st = ExitStack()
    sb = lambda *a: k.sb(st, *a)
    T1 = NT + 1
    node_i, node, valid, spare = sb("node_int", [P, NT], I32), sb("node_number", [P, NT]), sb("valid", [P, NT]), sb("spare_row", [P, NT])
    own_i, own_f, own_o = sb("shared_int", [P, NT], I32), sb("shared_float", [P, NT]), sb("shared_tokens", [P, NT], I32)
    rev = sb("reversed", [P, 1, X])
    m1, m2, mt, dw = (sb(n, [P, NT, 1]) for n in ("best", "second", "first_index", "difference"))
    l2, t8, oh1, oh2, sel, slot = (sb(n, [P, NT, X]) for n in ("logits2", "tmp8", "choice1", "choice2", "selected", "slot"))
    tb = sb("before_tile", [P, T1, X])
    nbf, be = sb("expert_blocks", [P, X]), sb("block_end", [P, X + 1])
    nbi = sb("expert_blocks_int", [P, X], I32)
    bno_i, bno, cmp_, eb, ebi = (sb("block_int", [P, 2], I32), sb("block_number", [P, 2]), sb("block_compare", [P, 2, X]),
                                 sb("block_expert", [P, 2, 1]), sb("block_expert_int", [P, 2], I32))
    pos = sb("choice_slot", [P, NT])
    sc = [sb(f"scatter_row{j}", [P, NT], I32) for j in range(2)]
    pr, pq = k.ps(st, "pRank", [P, 512]), k.ps(st, "pSum", [P, 512])
    own, cons, pe_s, v_s, ex, scat, stored = (k.sem("p7_" + n) for n in ("dve", "const", "pe", "dve_done", "exp", "scattered", "stored"))
    with nc.Block() as block:
        @block.sync
        def _(sp):
            load_weights(k, sp)
            sp.wait_ge(v_s, 3)
            sp.dma_start(k.token_d[0:NP, :].rearrange("(p c) o -> p (c o)", p=P), own_o[:, :]).then_inc(stored, 16)
            with nc.allow_non_contiguous_dma("a small table, once"):
                sp.dma_start(k.block_d[0, :].rearrange("(c p) -> p c", p=P), ebi[:, :]).then_inc(stored, 16)
            sp.wait_ge(stored, 32)

        @block.gpsimd
        def _(pool):
            pool.iota(node_i[:, :], [[P, NT]], base=0, channel_multiplier=1).then_inc(cons, 1)
            pool.iota(own_i[:, :], [[1, NT]], base=0, channel_multiplier=NT).then_inc(cons, 1)
            pool.iota(bno_i[:, :], [[P, 2]], base=0, channel_multiplier=1).then_inc(cons, 1)
            pool.wait_ge(v_s, 3)
            for t in range(NT):
                for j in range(2):
                    pool.indirect_dma_start(k.token_d[:, :], IndexOn(ap=sc[j][:, t:t + 1], axis=0), node_i[:, t:t + 1], None).then_inc(scat, 16)
            pool.wait_ge(scat, 32 * NT)

        @block.scalar
        def _(act):
            act.wait_ge(v_s, 1)
            nc.scalar.activation(dw[:, :, :], dw[:, :, :], ACT.Exp).then_inc(ex, 1)

        @block.vector
        def _(dve):
            link = Chain(dve, own)
            over_e = lambda a: a.broadcast_to([P, NT, X])
            dve.wait_ge(cons, 3)
            link(dve.tensor_copy(node[:, :], node_i[:, :]))
            link(dve.tensor_copy(own_f[:, :], own_i[:, :]))
            link(dve.tensor_copy(bno[:, :], bno_i[:, :]))
            link(dve.tensor_scalar(own_o[:, :], own_f[:, :], float(N - 1), None, ALU.min))
            link(dve.tensor_scalar(valid[:, :], node[:, :], float(N), None, ALU.is_lt))
            link(dve.tensor_scalar(rev[:, 0, :], k.iota[:, 0:X], -1.0, float(X), ALU.mult, ALU.add))

            def choose(logits, best, out):
                link(dve.tensor_reduce(best[:, :, 0], logits[:, :, :], AX.X, ALU.max))
                link(dve.tensor_tensor(t8[:, :, :], logits[:, :, :], over_e(best[:, :, :]), ALU.is_equal))
                link(dve.tensor_tensor(t8[:, :, :], t8[:, :, :], rev[:, :, :].broadcast_to([P, NT, X]), ALU.mult))
                link(dve.tensor_reduce(mt[:, :, 0], t8[:, :, :], AX.X, ALU.max))
                link(dve.tensor_tensor(out[:, :, :], t8[:, :, :], over_e(mt[:, :, :]), ALU.is_equal))

            choose(k.logits, m1, oh1)
            link(dve.scalar_tensor_tensor(l2[:, :, :], oh1[:, :, :], -BIG, k.logits[:, :, :], ALU.mult, ALU.add))
            choose(l2, m2, oh2)
            link(dve.tensor_tensor(dw[:, :, :], m2[:, :, :], m1[:, :, :], ALU.subtract))
            dve.sem_inc(v_s, 1)
            for oh in (oh1, oh2):
                link(dve.tensor_tensor(oh[:, :, :], oh[:, :, :], over_e(valid[:, :].unsqueeze(2)), ALU.mult))
            link(dve.tensor_tensor(sel[:, :, :], oh1[:, :, :], oh2[:, :, :], ALU.add))
            dve.sem_inc(v_s, 1)
            dve.wait_ge(ex, 1)
            link(dve.tensor_scalar(k.gate[:, 0, :], dw[:, :, 0], 1.0, None, ALU.add))
            link(dve.reciprocal(k.gate[:, 0, :], k.gate[:, 0, :]))
            link(dve.tensor_tensor(k.gate[:, 1, :], k.gate[:, 0, :], dw[:, :, 0], ALU.mult))
            dve.wait_ge(pe_s, 1)
            link(dve.memset(tb[:, 0:1, :], 0.0))
            q3 = pq[:, 0:NT * X].rearrange("p (t e) -> p t e", e=X)
            for e in range(X):
                link(dve.tensor_tensor_scan(tb[:, 1:T1, e], k.ones[:, 0:NT], q3[:, :, e], 0.0, ALU.mult, ALU.add))
            link(dve.tensor_scalar(nbf[:, :], tb[:, NT, :], float(BLK - 1), None, ALU.add))
            link(dve.tensor_copy(nbi[:, :], nbf[:, :]))
            link(dve.tensor_single_scalar(nbi[:, :], nbi[:, :], BLK.bit_length() - 1, ALU.logical_shift_right))
            link(dve.tensor_copy(nbf[:, :], nbi[:, :]))
            link(dve.memset(be[:, 0:1], 0.0))
            link(dve.tensor_tensor_scan(be[:, 1:X + 1], k.ones[:, 0:X], nbf[:, :], 0.0, ALU.mult, ALU.add))
            link(dve.tensor_tensor(slot[:, :, :], pr[:, 0:NT * X].rearrange("p (t e) -> p t e", e=X), tb[:, 0:NT, :], ALU.add))
            link(dve.tensor_scalar(nbf[:, :], be[:, 0:X], float(BLK), float(NT * BLK), ALU.mult, ALU.add))
            link(dve.tensor_tensor(slot[:, :, :], slot[:, :, :], nbf[:, :].unsqueeze(1).broadcast_to([P, NT, X]), ALU.add))
            for j, oh in enumerate((oh1, oh2)):
                link(dve.tensor_tensor(t8[:, :, :], oh[:, :, :], slot[:, :, :], ALU.mult))
                link(dve.tensor_reduce(pos[:, :], t8[:, :, :], AX.X, ALU.add))
                link(dve.tensor_copy(k.slot[:, j, :], pos[:, :]))
                link(dve.tensor_scalar(spare[:, :], valid[:, :], 1.0, -1.0, ALU.subtract, ALU.mult))
                link(dve.tensor_scalar(t8[:, :, 0], node[:, :], float(NB * BLK + j * NP), None, ALU.add))
                link(dve.tensor_tensor(spare[:, :], spare[:, :], t8[:, :, 0], ALU.mult))
                link(dve.tensor_tensor(sc[j][:, :], spare[:, :], pos[:, :], ALU.add))
            link(dve.tensor_scalar(bno[:, :], bno[:, :], float(NT), None, ALU.subtract))
            link(dve.tensor_tensor(cmp_[:, :, :], be[:, 1:X + 1].unsqueeze(1).broadcast_to([P, 2, X]),
                                   bno[:, :].unsqueeze(2).broadcast_to([P, 2, X]), ALU.is_le))
            link(dve.tensor_reduce(eb[:, :, 0], cmp_[:, :, :], AX.X, ALU.add))
            link(dve.tensor_scalar(eb[:, :, 0], eb[:, :, 0], float(X - 1), None, ALU.min))
            link(dve.tensor_scalar(bno[:, :], bno[:, :], 0.0, float(X), ALU.is_lt, ALU.mult))
            link(dve.tensor_tensor(ebi[:, :], eb[:, :, 0], bno[:, :], ALU.add))
            dve.sem_inc(v_s, 1)

        @block.tensor
        def _(pe):
            pe.wait_ge(v_s, 2)
            s2 = sel[:, :, :].rearrange("p t e -> p (t e)")
            nc.tensor.matmul(pr[:, 0:NT * X], k.upper[:, :], s2, start=True, stop=True)
            nc.tensor.matmul(pq[:, 0:NT * X], k.ones[:, :], s2, start=True, stop=True).then_inc(pe_s, 1)
    st.close()


def experts(k):
    nc, ins = k.nc, k.ins
    st = ExitStack()
    sb = lambda *a: k.sb(st, *a)
    XA = X + 1
    w1, w2, b1, b2, sh_in, all_in = k.w_up, k.w_down, k.b_up, k.b_down, k.shared_in, k.routed_in
    tabs = sb("block_row", [1, 2 * P], I32)
    idx, xg = sb("token_index", [P, 2, 1], I32), sb("tokens", [P, 2, D])
    rows_i, rows_f, tokens = sb("token_rows", [P, 2, P], I32), sb("token_rows_f", [P, 2, P]), sb("tokens_of_block", [P, NB], I32)
    xt, hp, ht, y = (sb(n, [P, 2, w]) for n, w in (("tokensT", DK * P), ("hidden", F), ("hiddenT", FK * P), ("result", D)))
    HF = F // 2
    px = k.ps(st, "pX", [P, 512])
    ph = [k.ps(st, f"pH{j}", [P, 512]) for j in range(2)]
    pg = [k.ps(st, f"pG{j}", [P, 512]) for j in range(2)]
    py = [k.ps(st, f"pY{j}", [P, 512]) for j in range(2)]
    x_in, stored = ([k.sem(f"p8_{n}{b}") for b in range(2)] for n in ("tokens", "stored"))
    tok_in, tok_s, tok_pe, x_own = (k.sem("p8_" + n) for n in ("token_rows", "token_columns", "token_turned", "index"))
    tab_in, tx, xt_s, up, hp_s, th, gl, dn, y_s = (k.sem("p8_" + n) for n in (
        "table", "turned", "tokensT", "up", "hidden", "hidden_turned", "gelu", "down", "result"))
    parts = ((0, P), (1, NB - P))
    FIRST = NT // 2
    assert 2 * FIRST <= NT - 1

    def steps(eng, head, body, tail, between=None):
        head()
        for a, z in ((0, FIRST), (FIRST, NB // 2 - 1)):
            with eng.Fori(a, z) as i:
                for b in range(2):
                    body(2 * i + b, b, i)
            if between and a == 0:
                between()
        body(NB - 2, 0, NB // 2 - 1)
        tail()

    with nc.Block() as block:
        @block.sync
        def _(sp):
            sp.dma_start(tabs[:, :], k.block_d).then_inc(tab_in, 16)
            prime(k, sp, stored)
            for c, m in parts:
                sp.dma_start(rows_i[0:m, c, :], k.token_d[c * P * BLK:(c * P + m) * BLK, :].rearrange("(p b) o -> p (b o)", b=BLK)).then_inc(tok_in, 16)

            def store(s, b, i):
                sp.wait_ge(y_s, done(s))
                sp.dma_start(k.y_d[ds(s * BLK, BLK), :], y[:, b, :]).then_inc(stored[b], 16)

            with sp.Fori(0, NB // 2 - 1) as i:
                for b in range(2):
                    store(2 * i + b, b, i)
            for b in range(2):
                store(NB - 2 + b, b, NB // 2 - 1)
            for b in range(2):
                sp.wait_ge(stored[b], 16 * (NB // 2 + 1))

        @block.gpsimd
        def _(pool):
            pool.sem_inc(x_own, CREDIT)
            pool.wait_ge(tok_s, 2)
            with pool.Fori(0, NB // 2) as i:
                for b in range(2):
                    s = 2 * i + b
                    pool.wait_ge(tx, freed(s))
                    pool.tensor_copy(idx[:, b, :], tokens[:, ds(s, 1)]).then_inc(x_own, 1)
                    pool.wait_ge(x_own, done(s))
                    settle(pool, k.passed)
                    pool.indirect_dma_start(xg[:, b, :], None, k.x2n_d[:, :], IndexOn(ap=idx[:, b, :], axis=0)).then_inc(x_in[b], 16)

        @block.vector
        def _(dve):
            def turn(s, b):
                dve.wait_ge(tx, done(s))
                dve.tensor_copy(xt[:, b, :], px[:, 0:DK * P]).then_inc(xt_s, 1)

            def hidden(s, b):
                dve.wait_ge(th, 2 * freed(s))
                for j in range(2):
                    dve.wait_ge(up, 2 * s + j + 1)
                    dve.tensor_copy(hp[:, b, j * HF:(j + 1) * HF], ph[j][:, :]).then_inc(hp_s, 1)

            def result(s, b, i):
                e = dve.value_load(tabs[0:1, ds(s, 1)], min_val=0, max_val=X)
                dve.wait_ge(dn, done(s))
                dve.wait_ge(stored[b], 16 * i + 16)
                dve.tensor_tensor(y[:, b:b + 1, :], py[b][:, 0:D].unsqueeze(1), b2[:, ds(e, 1), :], ALU.add).then_inc(y_s, 1)

            def head():
                dve.wait_ge(tok_in, 32)
                for c, m in parts:
                    last = dve.tensor_copy(rows_f[0:m, c, :], rows_i[0:m, c, :])
                last.then_inc(tok_s, 1)
                dve.wait_ge(tok_pe, 1)
                dve.tensor_copy(tokens[:, :], py[0][:, 0:NB]).then_inc(tok_s, 1)
                dve.sem_inc(y_s, CREDIT)
                dve.wait_ge(sh_in, 64)
                dve.wait_ge(tab_in, 16)
                turn(0, 0)
                turn(1, 1)
                hidden(0, 0)

            def body(s, b, i):
                last = isinstance(s, int)
                if not last:
                    turn(s + 2, b)
                hidden(s + 1, 1 - b)
                result(s, b, i)

            steps(dve, head, body, lambda: result(NB - 1, 1, NB // 2 - 1), lambda: dve.wait_ge(all_in, 64 * X))

        @block.scalar
        def _(act):
            def gelu(s, b):
                e = act.value_load(tabs[0:1, ds(s, 1)], min_val=0, max_val=X)
                act.wait_ge(dn, freed(s))
                for c in range(FK):
                    if c % 4 == 0:
                        act.wait_ge(th, 2 * CREDIT + 2 * s + c // 4 + 1)
                    nc.scalar.activation(ht[:, b, c * P:(c + 1) * P], pg[c // 4][:, c % 4 * P:(c % 4 + 1) * P], ACT.Gelu,
                                         bias=b1[:, ds(e, 1), c]).then_inc(gl, 1)

            act.sem_inc(gl, FK)
            act.wait_ge(sh_in, 64)
            act.wait_ge(tab_in, 16)
            steps(act, lambda: None, lambda s, b, i: gelu(s, b), lambda: gelu(NB - 1, 1), lambda: act.wait_ge(all_in, 64 * X))

        @block.tensor
        def _(pe):
            def turn(s, b, i):
                pe.wait_ge(x_in[b], 16 * i + 16)
                pe.wait_ge(xt_s, s)
                for c in range(DK):
                    last = nc.tensor.transpose(px[:, c * P:(c + 1) * P], xg[:, b, c * P:(c + 1) * P], k.ident[:, :])
                last.then_inc(tx, 1)

            def first_layer(s, b, e, j):
                pe.wait_ge(xt_s, s + 1)
                pe.wait_ge(hp_s, 2 * s)
                for c in range(DK):
                    last = nc.tensor.matmul(ph[j][:, :], xt[:, b, c * P:(c + 1) * P],
                                            w1[:, ds(e, 1), c, j * HF:(j + 1) * HF], start=c == 0, stop=c == DK - 1)
                last.then_inc(up, 1)

            def turn_hidden(s, b):
                pe.wait_ge(hp_s, 2 * s + 2)
                pe.wait_ge(gl, FK * s + FK)
                for c in range(FK):
                    last = nc.tensor.transpose(pg[c // 4][:, c % 4 * P:(c % 4 + 1) * P], hp[:, b, c * P:(c + 1) * P], k.ident[:, :])
                    if c % 4 == 3:
                        last.then_inc(th, 1)

            def second_layer(s, b, e):
                pe.wait_ge(y_s, freed(s))
                for c in range(FK):
                    pe.wait_ge(gl, FK * s + FK + c + 1)
                    last = nc.tensor.matmul(py[b][:, 0:D], ht[:, b, c * P:(c + 1) * P], w2[:, ds(e, 1), c, :],
                                            start=c == 0, stop=c == FK - 1)
                last.then_inc(dn, 1)

            def expert(s):
                return pe.value_load(tabs[0:1, ds(s, 1)], min_val=0, max_val=X)

            def head():
                pe.wait_ge(tok_s, 1)
                for c, m in parts:
                    last = nc.tensor.transpose(py[0][:, c * P:c * P + m], rows_f[0:m, c, :], k.ident[0:m, 0:m])
                last.then_inc(tok_pe, 1)
                pe.sem_inc(tx, CREDIT)
                pe.sem_inc(dn, CREDIT)
                pe.sem_inc(th, 2 * CREDIT)
                pe.wait_ge(sh_in, 64)
                pe.wait_ge(tab_in, 16)
                turn(0, 0, 0)
                turn(1, 1, 0)
                e = expert(0)
                first_layer(0, 0, e, 0)
                first_layer(0, 0, e, 1)

            def body(s, b, i):
                e0, e1 = expert(s), expert(s + 1)
                if not isinstance(s, int):
                    turn(s + 2, b, i + 1)
                first_layer(s + 1, 1 - b, e1, 0)
                turn_hidden(s, b)
                first_layer(s + 1, 1 - b, e1, 1)
                second_layer(s, b, e0)

            def tail():
                turn_hidden(NB - 1, 1)
                second_layer(NB - 1, 1, expert(NB - 1))

            steps(pe, head, body, tail, lambda: pe.wait_ge(all_in, 64 * X))
    st.close()


def combine(k):
    nc = k.nc
    st = ExitStack()
    sb = lambda *a: k.sb(st, *a)
    idx = sb("slots", [P, 2, 2, 1], I32)
    base, shared, one, two, o = (sb(n, [P, 2, D]) for n in ("x2_in", "shared_rows", "first_rows", "second_rows", "out_rows"))
    r_in, y_in, stored = ([k.sem(f"p9_{n}{b}") for b in range(2)] for n in ("rows", "routed", "stored"))
    picked, o_done, own = k.sem("p9_picked"), k.sem("p9_out"), k.sem("p9_dve")
    with nc.Block() as block:
        @block.sync
        def _(sp):
            for t, b, rows, i in each_tile(sp):
                sp.wait_ge(o_done, freed(t))
                sp.dma_start(base[:rows, b, :], k.x2_d[ds(t * P, rows), :]).then_inc(r_in[b], 16)
                sp.dma_start(shared[:rows, b, :], k.y_d[ds(t * P, rows), :]).then_inc(r_in[b], 16)

        @block.gpsimd
        def _(pool):
            for t, b, rows, i in each_tile(pool):
                pool.wait_ge(o_done, freed(t))
                pool.tensor_copy(idx[:, b, :, :], k.slot[:, :, ds(t, 1)]).then_inc(picked, 1)
                pool.wait_ge(picked, t + 1)
                settle(pool, k.passed)
                for j, into in enumerate((one, two)):
                    pool.indirect_dma_start(into[:, b, :], None, k.y_d[:, :], IndexOn(ap=idx[:, b, j, :], axis=0)).then_inc(y_in[b], 16)

        @block.scalar
        def _(act):
            prime(k, act, stored)
            for t, b, rows, i in each_tile(act):
                act.wait_ge(o_done, done(t))
                act.dma_start(k.out[ds(t * P, rows), :], o[:rows, b, :]).then_inc(stored[b], 16)
            for b in range(2):
                act.wait_ge(stored[b], 16 * (NT // 2 + 2 - b))

        @block.vector
        def _(dve):
            dve.sem_inc(o_done, CREDIT)
            for t, b, rows, i in each_tile(dve):
                link = Chain(dve, own, 2 * t)
                dve.wait_ge(r_in[b], 32 * i + 32)
                dve.wait_ge(stored[b], 16 * i + 16)
                link(dve.tensor_tensor(o[:rows, b, :], base[:rows, b, :], shared[:rows, b, :], ALU.add))
                dve.wait_ge(y_in[b], 32 * i + 32)
                link(dve.scalar_tensor_tensor(o[:rows, b, :], one[:rows, b, :], k.gate[:rows, 0, ds(t, 1)], o[:rows, b, :], ALU.mult, ALU.add))
                dve.scalar_tensor_tensor(o[:rows, b, :], two[:rows, b, :], k.gate[:rows, 1, ds(t, 1)], o[:rows, b, :],
                                         ALU.mult, ALU.add).then_inc(o_done, 1)
    st.close()


def build(nc, ins, out):
    k = Kernel(nc, ins, out)
    k.outer = outer = ExitStack()
    sb = lambda *a: k.sb(outer, *a)
    k.ident, k.upper, k.ones, k.iota = (sb(n, [P, P]) for n in ("ident", "upper", "ones", "iota_row"))
    k.eps = sb("eps", [P, 1])
    k.er = sb("er", [P, NT, H])
    k.cb = sb("update_bias", [P, D])
    k.w_lin = sb("w_lin", [P, DK, D])
    k.logits, k.gate = sb("router_logits", [P, NT, X]), sb("gates", [P, 2, NT])
    k.slot = sb("slots_of_token", [P, 2, NT], I32)
    wide, edges, nodes = ExitStack(), ExitStack(), ExitStack()
    k.w_feat, k.b_feat = k.sb(wide, "w_feat", [P, DK, D + 2 * H]), k.sb(wide, "b_feat", [P, D + 2 * H])
    k.xnT = k.sb(wide, "xnT", [P, DK, NP])
    k.count = k.sb(edges, "edges_of_node", [P, NT])
    k.el_e = k.sb(edges, "el_of_edge", [P, STRIP, H])
    k.dst_i = k.sb(edges, "dst_strips", [P, STRIP], I32)
    k.cont = k.sb(edges, "run_continues", [P, STRIP])
    k.xn = k.sb(nodes, "xn", [P, NT, D])
    prepare(k)
    project(k)
    collect(k)
    nodes.close()
    scan_max(k)
    scan_weights(k)
    edges.close()
    k.agg = k.sb(wide, "node_sums", [P, NT, GF])
    message(k)
    update(k)
    wide.close()
    k.w_up, k.w_down = sb("w_up", [P, X + 1, DK, F]), sb("w_down", [P, X + 1, FK, D])
    k.b_up, k.b_down = sb("b_up", [P, X + 1, FK]), sb("b_down_rows", [P, X + 1, D])
    k.shared_in, k.routed_in = k.sem("shared_weights_in"), k.sem("routed_weights_in")
    route(k)
    experts(k)
    combine(k)
    outer.close()
    k.stack.close()


_INS = ['x', 'src', 'dst', 'L0_gnn_W_lin', 'L0_gnn_b_lin', 'L0_gnn_W_gat', 'L0_gnn_attn_l', 'L0_gnn_attn_r',
        'L0_gnn_gat_bias', 'L0_mix_W_qk', 'L0_mix_b_qk', 'L0_mix_W_v', 'L0_mix_b_v', 'L0_mix_gamma',
        'L0_mix_beta', 'L0_ffn_Wr', 'L0_ffn_W1s', 'L0_ffn_b1s', 'L0_ffn_W2s', 'L0_ffn_b2s', 'L0_ffn_W1p',
        'L0_ffn_b1p', 'L0_ffn_W2p', 'L0_ffn_b2p']


def kernel(**inputs):
    import numpy as _np
    import concourse.bacc as _bacc
    from concourse import mybir as _mybir
    from concourse.bass_utils import run_bass_kernel_spmd as _run

    nc = _bacc.Bacc("TRN2", target_bir_lowering=False, num_devices=1)
    arrays, ins = {}, {}
    for name in _INS:
        a = _np.ascontiguousarray(inputs[name])
        arrays[f"in_{name}"] = a
        ins[name] = nc.dram_tensor(f"in_{name}", a.shape, _mybir.dt.from_np(a.dtype), kind="ExternalInput").ap()
    out = nc.dram_tensor("out_0", (N, D), _mybir.dt.float32, kind="ExternalOutput").ap()
    build(nc, ins, out)
    r = _run(nc, [arrays], core_ids=[0])
    return r.results[0]["out_0"]
```

```python
from contextlib import ExitStack

import numpy as np

import concourse.bass as bass
from concourse import mybir

F32 = mybir.dt.float32
BF16 = mybir.dt.bfloat16
I32 = mybir.dt.int32
ALU = mybir.AluOpType
ACT = mybir.ActivationFunctionType
AX = mybir.AxisListType
ds = bass.ds
IndexOn = bass.IndirectOffsetOnAxis

P = 128
N, D = 6250, 256
E = 100000
H, HD = 8, 32
X, F = 8, 1024
DK = D // P
FK = F // P
NT = -(-N // P)
LAST = N - (NT - 1) * P
NP = NT * P
STRIP = -(-E // P)
ES = STRIP * P
EL_LAST = E - (P - 1) * STRIP
COLS = 17
STEPS = STRIP // COLS
assert STEPS * COLS == STRIP and STEPS % 2 == 0
GATHERED = 28
GJ = 2
GE = GJ * P
NG = E // GE + NT
NG += -NG % 8
TABLE = NG + -NG % P
EROWS = E + GE + P * 2
GF = D + H
CH = 512
BLK = P
NRB = (2 * N) // BLK + X
NB = NT + NRB
NB += NB % 2
SLOTS = (NB - NT) * BLK
OUT_ROWS = N // 5
BIG = 1.0e30
EPS = 1.0e-5
PAD_DST = 8191
CREDIT = 2


def done(t):
    return t + 1 + CREDIT


def freed(t):
    return t + 1


def each_tile(eng):
    with eng.Fori(0, NT // 2) as i:
        for b in range(2):
            yield 2 * i + b, b, P, i
    yield NT - 1, 0, LAST, NT // 2


def pipeline(eng, *stages):
    most = max(lag for lag, _ in stages)

    def step(s, b, i):
        for lag, stage in stages:
            at = (b - lag) % 2
            if isinstance(s, int) and not 0 <= s - lag < NT:
                continue
            rows = LAST if isinstance(s, int) and s - lag == NT - 1 else P
            stage(s - lag, at, rows, i + (b - lag - at) // 2)

    head = most + most % 2
    for s in range(head):
        step(s, s % 2, s // 2)
    with eng.Fori(head // 2, NT // 2) as i:
        for b in range(2):
            step(2 * i + b, b, i)
    for s in range(NT - 1, NT + most):
        step(s, s % 2, s // 2)


def settle(eng, sem):
    eng.sem_inc(sem, 1)


def prime(k, queue, sems, n=1):
    for s in sems:
        for _ in range(n):
            queue.dma_start(k.scrap_d[k.scraps:k.scraps + 1, :], k.ones[0:1, 0:32]).then_inc(s, 16)
            k.scraps += 1


class Chain:

    def __init__(self, eng, sem, start=0):
        self.eng, self.sem, self.start, self.n = eng, sem, start, 0

    def __call__(self, ins):
        ins.then_inc(self.sem, 1)
        self.n += 1
        self.eng.wait_ge(self.sem, self.start + self.n)


class Kernel:
    def __init__(self, nc, ins, out):
        self.nc, self.ins, self.out = nc, ins, out
        self.stack = ExitStack()
        self.names = {}
        self.passed = self.stack.enter_context(nc.semaphore("waits_passed"))
        nc_ = nc
        d = lambda name, shape, dt=F32: nc_.dram_tensor(name, shape, dt).ap()
        self.feat_d = d("feat_rows", (N, D))
        self.el_d = d("el_rows", (N, H))
        self.scan_d = d("scan_rows", (ES, H))
        self.fill_d = d("fill_rows", (ES + NP, 2 * H))
        self.edge_d = d("edge_rows", (EROWS, H + 2))
        self.table_d = d("group_table", (2, TABLE), I32)
        self.scrap_d, self.scraps = d("scrap_rows", (32, 32)), 0
        self.x2_d = d("x2_rows", (NP, D))
        self.x2n_d, self.acc_d = d("x2n_rows", (N + BLK, D)), d("sum_rows", (N + BLK, D))
        self.token_d = d("slot_tokens", (SLOTS + 2 * NP, 2))
        self.block_d = d("block_table", (1, 2 * P), I32)

    def sem(self, name):
        return self.stack.enter_context(self.nc.semaphore(name))

    def sb(self, stack, name, shape, dt=F32):
        return stack.enter_context(self.nc.sbuf_tensor(self.unique(name), shape, dt))

    def ps(self, stack, name, shape, dt=F32):
        return stack.enter_context(self.nc.psum_tensor(self.unique(name), shape, dt))

    def unique(self, name):
        self.names[name] = self.names.get(name, 0) + 1
        return name if self.names[name] == 1 else f"{name}_{self.names[name]}"


def prepare(k):
    nc, ins = k.nc, k.ins
    st = ExitStack()
    sb = lambda *a: k.sb(st, *a)
    w_gat = sb("w_gat", [P, DK, D])
    ext = sb("w_ext", [P, DK, D + 2 * H])
    attn = sb("attn_rows", [P, 2, D])
    prod = sb("attn_prod", [P, D])
    w_linT = sb("w_linT", [P, DK, D])
    blin_rep = sb("blin_rep", [P, DK, P])
    blin_col = sb("blin_col", [P, DK])
    idx = sb("idx", [P, P], I32)
    zeros, spare = sb("zeros", [P, 2048]), sb("spare_slots", [P, BLK, 2])
    ip = k.ps(st, "pT", [P, 2, 2, P])
    pw = k.ps(st, "pW", [P, 2, 512])
    pb = k.ps(st, "pB", [P, 512])
    s_ld, s_c, s_pe, s_cp, s_ch, s_z, s_g, s_ex, s_sp = (k.sem("p0_" + x) for x in (
        "load", "const", "pe", "copied", "dve", "zeros", "pool", "ext", "spare"))
    with nc.Block() as block:
        @block.sync
        def _(sp):
            w3 = lambda a: a.rearrange("(k p) n -> p k n", p=P)
            sp.dma_start(k.w_lin[:, :, :], w3(ins["L0_gnn_W_lin"])).then_inc(s_ld, 16)
            sp.dma_start(w_gat[:, :, :], w3(ins["L0_gnn_W_gat"])).then_inc(s_ld, 16)
            sp.dma_start(ext[:, :, 0:D], w3(ins["L0_gnn_W_gat"])).then_inc(s_ld, 16)
            for j, a in enumerate(("L0_gnn_attn_l", "L0_gnn_attn_r")):
                sp.dma_start(attn[:, j, :], ins[a].rearrange("h c -> (h c)").partition_broadcast(P)).then_inc(s_ld, 16)
            with nc.allow_non_contiguous_dma("a short bias column"):
                sp.dma_start(blin_col[:, :], ins["L0_gnn_b_lin"].rearrange("(k p) -> p k", p=P)).then_inc(s_ld, 16)
            sp.wait_ge(s_ld, 96)
            sp.wait_ge(s_z, 1)
            fr = k.fill_d[0:ES, :].rearrange("(p c) h -> p (c h)", p=P)
            w = STRIP * 2 * H
            n = 0
            for a in range(0, w, 2048):
                m = min(2048, w - a)
                sp.dma_start(fr[:, a:a + m], zeros[:, 0:m]).then_inc(s_z, 16)
                n += 1
            sp.dma_start(k.x2n_d[N:N + BLK, :], zeros[:, 0:D]).then_inc(s_z, 16)
            sp.dma_start(k.acc_d[N:N + BLK, :], zeros[:, 0:D]).then_inc(s_z, 16)
            sp.wait_ge(s_sp, 1)
            sp.dma_start(k.token_d[0:SLOTS, :].rearrange("(b s) o -> b (s o)", s=BLK),
                         spare[0:SLOTS // BLK, :, :].rearrange("p s o -> p (s o)")).then_inc(s_z, 16)
            sp.wait_ge(s_z, 1 + 16 * (n + 3))

        @block.gpsimd
        def _(pool):
            link = Chain(pool, s_g)
            link(pool.memset(zeros[:, :], 0.0))
            pool.sem_inc(s_z, 1)
            link(pool.memset(k.ident[:, :], 0.0))
            link(pool.affine_select(out=k.ident[:, :], in_=k.ident[:, :], compare_op=ALU.not_equal, fill=1.0,
                                    base=0, pattern=[[-1, P]], channel_multiplier=1))
            link(pool.memset(k.upper[:, :], 1.0))
            link(pool.affine_select(out=k.upper[:, :], in_=k.upper[:, :], compare_op=ALU.is_gt, fill=0.0,
                                    base=0, pattern=[[1, P]], channel_multiplier=-1))
            link(pool.memset(k.ones[:, :], 1.0))
            link(pool.memset(k.eps[:, :], EPS))
            link(pool.iota(idx[:, :], [[1, P]], base=0, channel_multiplier=0))
            pool.tensor_copy(k.iota[:, :], idx[:, :]).then_inc(s_c, 1)
            link(pool.memset(spare[:, :, :], 0.0))
            pool.wait_ge(s_c, 1)
            link(pool.iota(idx[:, :], [[1, P]], base=N, channel_multiplier=0))
            pool.tensor_copy(spare[:, :, 0:1].bitcast(I32), idx[:, :].unsqueeze(2)).then_inc(s_sp, 1)

        @block.vector
        def _(dve):
            link = Chain(dve, s_ch)
            dve.wait_ge(s_ld, 96)
            for j in range(2):
                for c in range(DK):
                    link(dve.tensor_tensor(prod[:, :], w_gat[:, c, :], attn[:, j, :], ALU.mult))
                    link(dve.tensor_reduce(ext[:, c, D + j * H:D + (j + 1) * H],
                                           prod[:, :].rearrange("p (h c) -> p h c", h=H), AX.X, ALU.add))
            for c in range(DK):
                last = dve.tensor_copy(blin_rep[:, c, :], blin_col[:, c:c + 1].broadcast_to([P, P]))
            last.then_inc(s_ex, 1)
            dve.wait_ge(s_pe, 1)
            for c in range(DK):
                last = dve.tensor_copy(w_linT[:, c, :].rearrange("p (a b) -> p a b", a=2), ip[:, c, :, :])
            last.then_inc(s_cp, 1)
            dve.wait_ge(s_pe, 2)
            for m in range(2):
                link(dve.tensor_copy(k.w_feat[:, m, :], pw[:, m, 0:D + 2 * H]))
            link(dve.tensor_copy(k.b_feat[:, :], pb[:, 0:D + 2 * H]))

        @block.tensor
        def _(pe):
            pe.wait_ge(s_ld, 96)
            pe.wait_ge(s_c, 1)
            for m in range(2):
                for c in range(DK):
                    last = nc.tensor.transpose(ip[:, c, m, :], k.w_lin[:, m, c * P:(c + 1) * P], k.ident[:, :])
            last.then_inc(s_pe, 1)
            pe.wait_ge(s_cp, 1)
            pe.wait_ge(s_ex, 1)
            for m in range(2):
                for c in range(DK):
                    nc.tensor.matmul(pw[:, m, 0:D + 2 * H], w_linT[:, c, m * P:(m + 1) * P], ext[:, c, :],
                                     start=c == 0, stop=c == DK - 1)
            for c in range(DK):
                last = nc.tensor.matmul(pb[:, 0:D + 2 * H], blin_rep[:, c, :], ext[:, c, :],
                                        start=c == 0, stop=c == DK - 1)
            last.then_inc(s_pe, 1)
    st.close()


def project(k):
    nc, ins = k.nc, k.ins
    st = ExitStack()
    sb = lambda *a: k.sb(st, *a)
    xs, xn, fs = sb("x_in", [P, 2, D]), sb("xn_stage", [P, 2, D]), sb("feat_stage", [P, 2, D + 2 * H])
    stats, mv, sd, rs = (sb(n, [P, 2, w]) for n, w in (("stats", 6), ("mv", 2), ("sd", 1), ("rs", 1)))
    xt = sb("xT_stage", [P, 2, DK, P])
    pt = [k.ps(st, f"pT{b}", [P, 512]) for b in range(2)]
    pf = [k.ps(st, f"pF{b}", [P, 512]) for b in range(2)]
    x_in = [k.sem(f"p1_x_in{b}") for b in range(2)]
    stored = [k.sem(f"p1_stored{b}") for b in range(2)]
    (mv_done, sd_done, xn_done, keep_done, tr_done, xt_done, xtk_done, feat_done, fs_done, er_done, own, own_r, z) = (
        k.sem("p1_" + n) for n in ("mv", "sd", "xn", "xn_kept", "transposed", "xT", "xT_kept", "feat", "fs",
                                   "er", "dve", "dve_rs", "zero"))
    with nc.Block() as block:
        @block.sync
        def _(sp):
            prime(k, sp, stored, 2)

            def load(t, b, rows, i):
                sp.wait_ge(xn_done, freed(t))
                sp.dma_start(xs[:rows, b, :], ins["x"][ds(t * P, rows), :]).then_inc(x_in[b], 16)

            def store(t, b, rows, i):
                sp.wait_ge(fs_done, done(t))
                sp.dma_start(k.feat_d[ds(t * P, rows), :], fs[:rows, b, 0:D]).then_inc(stored[b], 16)
                sp.dma_start(k.el_d[ds(t * P, rows), :], fs[:rows, b, D:D + H]).then_inc(stored[b], 16)

            pipeline(sp, (0, load), (4, store))
            for b in range(2):
                sp.wait_ge(stored[b], 32 * (NT // 2 + 2 - b))

        @block.gpsimd
        def _(pool):
            pool.sem_inc(keep_done, CREDIT)
            pool.memset(k.elr[:, :, :], 0.0).then_inc(z, 1)

            def keep(t, b, rows, i):
                pool.wait_ge(xn_done, done(t))
                pool.tensor_copy(k.xn[:rows, ds(t, 1), :], xn[:rows, b:b + 1, :]).then_inc(keep_done, 1)

            pipeline(pool, (0, keep))

        @block.vector
        def _(dve):
            dve.sem_inc(xn_done, CREDIT)
            dve.sem_inc(fs_done, CREDIT)

            def moments(t, b, rows, i):
                dve.wait_ge(x_in[b], 16 * i + 16)
                Chain(dve, own, t)(dve.bn_stats(stats[:rows, b, :], xs[:rows, b, :]))
                settle(dve, k.passed)
                dve.bn_aggr(mv[:rows, b, :], stats[:rows, b, :]).then_inc(mv_done, 1)

            def normalise(t, b, rows, i):
                dve.wait_ge(sd_done, t + 1)
                Chain(dve, own_r, t)(dve.reciprocal(rs[:rows, b, :], sd[:rows, b, :]))
                dve.wait_ge(keep_done, freed(t))
                dve.wait_ge(tr_done, freed(t))
                dve.tensor_scalar(xn[:rows, b, :], xs[:rows, b, :], mv[:rows, b, 0:1], rs[:rows, b, :],
                                  ALU.subtract, ALU.mult).then_inc(xn_done, 1)

            def features(t, b, rows, i):
                dve.wait_ge(feat_done, done(t))
                dve.wait_ge(stored[b], 32 * i + 32)
                dve.wait_ge(er_done, freed(t))
                dve.tensor_tensor(fs[:rows, b, :], pf[b][:rows, 0:D + 2 * H], k.b_feat[:rows, :],
                                  ALU.add).then_inc(fs_done, 1)

            pipeline(dve, (0, moments), (3, features), (1, normalise))

        @block.scalar
        def _(act):
            act.sem_inc(xt_done, CREDIT)
            act.sem_inc(xtk_done, CREDIT)
            act.sem_inc(er_done, CREDIT)
            act.wait_ge(z, 1)

            def deviation(t, b, rows, i):
                act.wait_ge(mv_done, t + 1)
                nc.scalar.activation(sd[:rows, b, :], mv[:rows, b, 1:2], ACT.Sqrt,
                                     bias=k.eps[:rows, :]).then_inc(sd_done, 1)

            def turned(t, b, rows, i):
                act.wait_ge(tr_done, done(t))
                act.wait_ge(feat_done, freed(t))
                src = pt[b][:, 0:DK * P].rearrange("p (k n) -> p k n", k=DK)[:, :, 0:rows]
                nc.scalar.activation(xt[:, b, :, 0:rows], src, ACT.Copy).then_inc(xt_done, 1)
                nc.scalar.activation(k.xnT[:, :, ds(t * P, rows)], src, ACT.Copy).then_inc(xtk_done, 1)

            def keep_er(t, b, rows, i):
                act.wait_ge(fs_done, done(t))
                nc.scalar.activation(k.elr[:rows, ds(t, 1), :], fs[:rows, b:b + 1, D:D + 2 * H],
                                     ACT.Copy).then_inc(er_done, 1)

            pipeline(act, (0, deviation), (2, turned), (4, keep_er))

        @block.tensor
        def _(pe):
            pe.sem_inc(tr_done, CREDIT)
            pe.sem_inc(feat_done, CREDIT)

            def turn(t, b, rows, i):
                pe.wait_ge(xn_done, done(t))
                pe.wait_ge(xtk_done, freed(t))
                for c in range(DK):
                    last = nc.tensor.transpose(pt[b][:, c * P:c * P + rows], xn[:rows, b, c * P:(c + 1) * P],
                                               k.ident[:rows, :rows])
                last.then_inc(tr_done, 1)

            def product(t, b, rows, i):
                pe.wait_ge(xt_done, done(t))
                pe.wait_ge(fs_done, freed(t))
                for c in range(DK):
                    last = nc.tensor.matmul(pf[b][:rows, 0:D + 2 * H], xt[:, b, c, 0:rows], k.w_feat[:, c, :],
                                            start=c == 0, stop=c == DK - 1)
                last.then_inc(feat_done, 1)

            pipeline(pe, (0, turn), (1, product))
    st.close()


def collect(k):
    nc, ins = k.nc, k.ins
    st = ExitStack()
    sb = lambda *a: k.sb(st, *a)
    src = sb("src_strips", [P, STRIP], I32)
    idx, got = sb("gather_index", [P, 2, COLS], I32), sb("gathered_el", [P, 2, COLS, H])
    dst_i, lo_i = sb("dst_int", [P, STRIP], I32), sb("dst_part", [P, STRIP], I32)
    lo, hi, iotab = sb("dst_lo", [P, NT * COLS], BF16), sb("dst_hi", [P, NT * COLS], BF16), sb("iota_bf16", [P, P], BF16)
    oh_lo, oh_hi = sb("onehot_lo", [P, 2, COLS, P], BF16), sb("onehot_hi", [P, 2, COLS, NT], BF16)
    wk, wq, wv = (sb(n, [P, DK, D]) for n in ("w_k", "w_q", "w_v"))
    cols = sb("mix_columns", [P, 4, DK])
    bv, blin = sb("b_v_rows", [P, D]), sb("b_lin_rows", [P, D])
    NC = -(-N // CH)
    kmax = sb("key_max_chunks", [P, DK, NC])
    nb = sb("exp_bias", [P, 3, DK])
    es = sb("expT_stage", [P, 2, DK, P])
    e2 = sb("exp_stage", [P, 2, D])
    pn, pnT, lam, bn, wqT = (sb(n, [P, DK, D]) for n in ("pool_mean", "pool_meanT", "lam", "bn", "w_qT"))
    rden, stats, mv, rg = (sb(n, [P, DK, w]) for n, w in (("rden", 1), ("lam_stats", 6), ("lam_mv", 2), ("lam_rg", 2)))
    bq_rep = sb("b_q_rep", [P, DK, P])
    zf, zb = sb("zero_f32", [P, 512]), sb("zero_bf16", [P, P], BF16)
    pk = [k.ps(st, f"pK{b}", [P, 512]) for b in range(2)]
    pe_ = [k.ps(st, f"pE{b}", [P, 512]) for b in range(2)]
    pp = [k.ps(st, f"pP{b}", [P, 512]) for b in range(2)]
    ph = k.ps(st, "pHist", [P, 512])
    px = k.ps(st, "pX", [P, 512])
    g_land = [k.sem(f"p2_gathered{b}") for b in range(2)]
    (ld, pad, z, kt_mm, key_done, kt_mx, nb_s, exp_done, et_done, e2_done, acc_done, oh_done, hist_mm, kept, own, own_p,
     own_a, tail_pe, tail_v, idx_done, sd_s) = (
        k.sem("p2_" + n) for n in ("loaded", "padded", "zeros", "keys", "keys_again", "keys_max", "bias", "exp",
                                   "exp_transposed", "exp_staged", "accumulated", "onehots", "histogram", "el_kept",
                                   "dve", "pool", "act", "tail_pe", "tail_dve", "index", "lam_sd"))

    OS, W = STEPS - GATHERED, ((0, 6), (6, 6), (12, 5))
    assert sum(w for _, w in W) == COLS and OS % 2 == 0 and GATHERED % 2 == 0
    OC, HT = OS * COLS, H * NT
    slo_i, slo, shi = lo_i[:, 0:OC], lo[:, 0:OC + COLS], hi[:, 0:OC + COLS]
    tab, rest, part = sb("el_parts", [P, 3, H, NT], BF16), sb("el_rest", [P, H, NT]), zf[:, 0:HT].rearrange("p (h t) -> p h t", h=H)
    m49, mask, identb = sb("tile_mask", [NT, NT]), sb("mask", [NT, H, NT], BF16), sb("ident_bf16", [P, P], BF16)
    loT, hiT = sb("lo_turned", [P, 2, 6, P], BF16), sb("hi_turned", [NT, 2, 6, P], BF16)
    picked = e2[:, :, 0:COLS * H].rearrange("p b (c h) -> p b c h", c=COLS)
    o_start, o_hot, o_tr, o_ev, o_mm, o_red, o_kept, m_s = (k.sem("p2o_" + n) for n in (
        "start", "onehots", "turned", "staged", "products", "picked", "kept", "mask"))

    def turned(bank, rows, w):
        return bank[0:rows, :].bitcast(BF16)[:, 0:w * P].rearrange("p (j n) -> p j n", j=w)

    def bank(b, c):
        order = [(c2 + b2) % 4 for b2 in (b, 1 - b, b) for c2 in range(COLS)]
        at = 2 * COLS + c
        return (*pp, ph, px)[order[at]], next(d for d in range(1, at) if order[at - d] == order[at])

    def batches(eng, body):
        with eng.Fori(0, OS // 2) as i:
            for b in range(2):
                for q in range(3):
                    g = 2 * i + b
                    body(g, b, q, 3 * g + q, (3 * b + q) % 2)

    def chunks(eng):
        with eng.Fori(0, NC - 1) as c:
            yield c, CH
        yield NC - 1, N - (NC - 1) * CH

    with nc.Block() as block:
        @block.sync
        def _(sp):
            w3 = lambda a: a.rearrange("(k p) n -> p k n", p=P)
            sp.dma_start(wk[:, :, :], w3(ins["L0_mix_W_qk"][1])).then_inc(ld, 16)
            sp.dma_start(wq[:, :, :], w3(ins["L0_mix_W_qk"][0])).then_inc(ld, 16)
            sp.dma_start(wv[:, :, :], w3(ins["L0_mix_W_v"])).then_inc(ld, 16)
            with nc.allow_non_contiguous_dma("short bias columns"):
                for j, a in enumerate((ins["L0_mix_b_qk"][0], ins["L0_mix_b_qk"][1], ins["L0_mix_gamma"],
                                       ins["L0_mix_beta"])):
                    sp.dma_start(cols[:, j, :], a.rearrange("(k p) -> p k", p=P)).then_inc(ld, 16)
            sp.dma_start(bv[:, :], ins["L0_mix_b_v"].partition_broadcast(P)).then_inc(ld, 16)
            sp.dma_start(blin[:, :], ins["L0_gnn_b_lin"].partition_broadcast(P)).then_inc(ld, 16)
            sp.wait_ge(pad, 2)
            sp.dma_start(dst_i[0:P - 1, :], ins["dst"][0:(P - 1) * STRIP].rearrange("(p c) -> p c", c=STRIP)).then_inc(ld, 16)
            sp.dma_start(dst_i[P - 1:P, 0:EL_LAST], ins["dst"][(P - 1) * STRIP:E].rearrange("(p c) -> p c", p=1)).then_inc(ld, 16)

        @block.gpsimd
        def _(pool):
            link = Chain(pool, own_p)
            link(pool.memset(src[:, :], 0))
            pool.sem_inc(pad, 1)
            pool.memset(m49[:, :], -BIG).then_inc(m_s, 1)
            pool.wait_ge(m_s, 1)
            pool.affine_select(out=m49[:, :], in_=m49[:, :], compare_op=ALU.not_equal, fill=0.0,
                               base=0, pattern=[[-1, NT]], channel_multiplier=1).then_inc(m_s, 1)
            pool.dma_start(src[0:P - 1, :], ins["src"][0:(P - 1) * STRIP].rearrange("(p c) -> p c", c=STRIP)).then_inc(idx_done, 16)
            pool.dma_start(src[P - 1:P, 0:EL_LAST], ins["src"][(P - 1) * STRIP:E].rearrange("(p c) -> p c", p=1)).then_inc(idx_done, 16)
            pool.wait_ge(idx_done, 32)

            def gathers(s, b):
                pool.tensor_copy(idx[:, b, :], src[:, ds(s * COLS, COLS)]).then_inc(own_p, 1)
                pool.wait_ge(own_p, s + 2)
                settle(pool, k.passed)
                for c in range(COLS):
                    pool.indirect_dma_start(got[:, b, c, :], None, k.el_d[:, :],
                                            IndexOn(ap=idx[:, b, c:c + 1], axis=0)).then_inc(g_land[b], 16)

            def keep(s, b, n):
                pool.wait_ge(g_land[b], 16 * COLS * n)
                pool.tensor_copy(k.el_e[:, ds(s * COLS, COLS), :], got[:, b, :, :]).then_inc(kept, 1)
                pool.wait_ge(kept, s + 1)

            for b in range(2):
                gathers(b, b)
            with pool.Fori(1, GATHERED // 2) as i:
                for b in range(2):
                    keep(2 * i + b - 2, b, i)
                    gathers(2 * i + b, b)
            for b in range(2):
                keep(GATHERED - 2 + b, b, GATHERED // 2)

        @block.vector
        def _(dve):
            link = Chain(dve, own)
            link(dve.memset(dst_i[:, :], PAD_DST))
            dve.sem_inc(pad, 1)
            link(dve.memset(zf[:, :], 0.0))
            link(dve.memset(zb[:, :], 0.0))
            dve.sem_inc(z, 1)
            dve.wait_ge(ld, 16 * 11)
            link(dve.tensor_copy(iotab[:, :], k.iota[:, :]))
            link(dve.tensor_single_scalar(lo_i[:, :], dst_i[:, :], P - 1, ALU.bitwise_and))
            link(dve.memset(lo[:, STRIP:NT * COLS], 0.0))
            link(dve.memset(hi[:, STRIP:NT * COLS], float(PAD_DST >> 7)))
            link(dve.tensor_copy(lo[:, 0:STRIP], lo_i[:, :]))
            link(dve.tensor_single_scalar(lo_i[:, :], dst_i[:, :], 7, ALU.logical_shift_right))
            link(dve.tensor_copy(hi[:, 0:STRIP], lo_i[:, :]))
            for c in range(DK):
                link(dve.tensor_copy(bq_rep[:, c, :], cols[:, 0, c:c + 1].broadcast_to([P, P])))
            dve.sem_inc(kt_mx, 1)
            for c, w in chunks(dve):
                dve.wait_ge(kt_mm, c + 1)
                for m in range(DK):
                    last = dve.reduce_max(kmax[:, m, ds(c, 1)], pk[m][:, 0:w], AX.X)
                last.then_inc(kt_mx, 1)
            dve.wait_ge(kt_mx, NC + 1)
            for m in range(DK):
                link(dve.reduce_max(nb[:, 0, m:m + 1], kmax[:, m, :], AX.X))
            link(dve.tensor_tensor(nb[:, 1, :], nb[:, 0, :], cols[:, 1, :], ALU.add))
            dve.tensor_tensor(nb[:, 2, :], cols[:, 1, :], nb[:, 1, :], ALU.subtract).then_inc(nb_s, 1)
            dve.sem_inc(e2_done, CREDIT)
            dve.sem_inc(oh_done, CREDIT)

            def stage_exp(t, b, rows, i):
                dve.wait_ge(et_done, done(t))
                dve.wait_ge(acc_done, freed(t))
                dve.tensor_copy(e2[:rows, b, :], pe_[b][:rows, 0:D]).then_inc(e2_done, 1)

            def dst_onehots(s, b, rows, i):
                dve.wait_ge(hist_mm, freed(s))
                dve.tensor_tensor(oh_lo[:, b, :, :], iotab[:, :].unsqueeze(1).broadcast_to([P, COLS, P]),
                                  lo[:, ds(s * COLS, COLS)].unsqueeze(2).broadcast_to([P, COLS, P]), ALU.is_equal)
                dve.tensor_tensor(oh_hi[:, b, :, :], iotab[:, 0:NT].unsqueeze(1).broadcast_to([P, COLS, NT]),
                                  hi[:, ds(s * COLS, COLS)].unsqueeze(2).broadcast_to([P, COLS, NT]),
                                  ALU.is_equal).then_inc(oh_done, 1)

            pipeline(dve, (0, dst_onehots), (0, stage_exp))
            dve.wait_ge(hist_mm, done(NT))
            link(dve.tensor_copy(k.count[:, :], ph[:, 0:NT]))
            dve.wait_ge(tail_pe, 1)
            for m in range(DK):
                link(dve.reciprocal(rden[:, m, :], pp[m][:, D:D + 1]))
                link(dve.tensor_scalar(pn[:, m, :], pp[m][:, 0:D], rden[:, m, :], None, ALU.mult))
            dve.sem_inc(tail_v, 1)
            dve.wait_ge(tail_pe, 2)
            for m in range(DK):
                link(dve.tensor_copy(pnT[:, :, m * P:(m + 1) * P], pk[m][:, 0:D].rearrange("p (c n) -> p c n", c=DK)))
                link(dve.tensor_copy(wqT[:, :, m * P:(m + 1) * P], pe_[m][:, 0:D].rearrange("p (c n) -> p c n", c=DK)))
            dve.sem_inc(tail_v, 1)
            dve.wait_ge(tail_pe, 3)
            for m in range(DK):
                link(dve.tensor_tensor(lam[:, m, :], pp[m][:, 0:D], bv[:, :], ALU.add))
                link(dve.bn_stats(stats[:, m, :], lam[:, m, :]))
                link(dve.bn_aggr(mv[:, m, :], stats[:, m, :]))
            dve.sem_inc(tail_v, 1)
            dve.wait_ge(sd_s, 1)
            for m in range(DK):
                link(dve.reciprocal(rg[:, m, 1:2], rg[:, m, 0:1]))
                link(dve.tensor_scalar(bn[:, m, :], lam[:, m, :], mv[:, m, 0:1], rg[:, m, 1:2], ALU.subtract, ALU.mult))
                link(dve.tensor_scalar(bn[:, m, :], bn[:, m, :], cols[:, 2, m:m + 1], cols[:, 3, m:m + 1],
                                       ALU.mult, ALU.add))
            dve.sem_inc(tail_v, 1)
            dve.wait_ge(tail_pe, 4)
            for m in range(DK):
                link(dve.tensor_tensor(k.w_lin[:, m, :], pk[m][:, 0:D], k.w_lin[:, m, :], ALU.add))
            link(dve.tensor_tensor(k.cb[:, :], px[:, 0:D], blin[:, :], ALU.add))
            dve.wait_ge(idx_done, 32)
            dve.wait_ge(m_s, 2)
            src_o = src[:, GATHERED * COLS:STRIP]
            link(dve.tensor_single_scalar(slo_i[:, :], src_o, P - 1, ALU.bitwise_and))
            link(dve.memset(slo[:, OC:OC + COLS], 0.0))
            link(dve.memset(shi[:, OC:OC + COLS], 0.0))
            link(dve.tensor_copy(slo[:, 0:OC], slo_i[:, :]))
            link(dve.tensor_single_scalar(slo_i[:, :], src_o, 7, ALU.logical_shift_right))
            link(dve.tensor_copy(shi[:, 0:OC], slo_i[:, :]))
            link(dve.tensor_copy(identb[:, :], k.ident[:, :]))
            link(dve.tensor_copy(mask[:, :, :], m49[:, :].unsqueeze(1).broadcast_to([NT, H, NT])))
            link(dve.tensor_copy(rest[:, :, :], k.elr[:, :, 0:H].rearrange("p t h -> p h t")))
            for j in range(3):
                link(dve.tensor_copy(tab[:, j, :, :], rest[:, :, :]))
                if j < 2:
                    link(dve.tensor_copy(part[:, :, :], tab[:, j, :, :]))
                    link(dve.tensor_tensor(rest[:, :, :], rest[:, :, :], part[:, :, :], ALU.subtract))
            dve.sem_inc(o_start, 1)
            dve.sem_inc(o_red, 5)
            dve.sem_inc(o_kept, 2)

            def onehots(g, b, q, n):
                a, w = W[q]
                dve.wait_ge(o_tr, n + 1)
                dve.tensor_tensor(oh_lo[:, b, a:a + w, :], iotab[:, :].unsqueeze(1).broadcast_to([P, w, P]),
                                  slo[:, ds(g * COLS + a, w)].unsqueeze(2).broadcast_to([P, w, P]), ALU.is_equal)
                dve.tensor_tensor(oh_hi[:, b, a:a + w, :], iotab[:, 0:NT].unsqueeze(1).broadcast_to([P, w, NT]),
                                  shi[:, ds(g * COLS + a, w)].unsqueeze(2).broadcast_to([P, w, NT]),
                                  ALU.is_equal).then_inc(o_hot, 1)

            def pick(g, b, q):
                a, w = W[q]
                if q == 0:
                    dve.wait_ge(o_kept, g + 1)
                for c in range(a, a + w):
                    m = COLS * g + c
                    dve.wait_ge(o_mm, m + 1 + COLS)
                    dve.reduce_max(picked[:, b, c, :], bank(b, c)[0][:, 0:HT].rearrange("p (h t) -> p h t", h=H),
                                   AX.X).then_inc(o_red, 1)
                if q == 2:
                    dve.wait_ge(o_red, COLS * g + COLS + 5)
                    dve.tensor_copy(k.el_e[:, ds((g + GATHERED) * COLS, COLS), :], picked[:, b, :, :]).then_inc(o_kept, 1)

            def dve_batch(g, b, q, n, _):
                onehots(g + 1, 1 - b, q, n + 3)
                pick(g, b, q)

            for q in range(3):
                onehots(0, 0, q, q)
            batches(dve, dve_batch)
            dve.wait_ge(o_kept, OS + 2)

        @block.scalar
        def _(act):
            act.sem_inc(exp_done, CREDIT)
            act.wait_ge(nb_s, 1)
            for t, b, rows, i in each_tile(act):
                act.wait_ge(key_done, done(t))
                act.wait_ge(et_done, freed(t))
                for m in range(DK):
                    last = nc.scalar.activation(es[:, b, m, 0:rows], pk[b][:, m * P:m * P + rows], ACT.Exp,
                                                bias=nb[:, 2, m:m + 1])
                last.then_inc(exp_done, 1)
            act.wait_ge(tail_v, 3)
            for m in range(DK):
                last = nc.scalar.activation(rg[:, m, 0:1], mv[:, m, 1:2], ACT.Sqrt, bias=k.eps[:, :])
            last.then_inc(sd_s, 1)
            act.sem_inc(o_ev, 2)

            def stage(g, b, q, n, x):
                a, w = W[q]
                act.wait_ge(o_tr, n + 7)
                act.wait_ge(o_mm, COLS * g + (12, COLS, COLS + 6)[q])
                nc.scalar.activation(loT[:, x, 0:w, :], turned(pk[x], P, w), ACT.Copy)
                nc.scalar.activation(hiT[:, x, 0:w, :], turned(pe_[x], NT, w), ACT.Copy).then_inc(o_ev, 1)

            batches(act, stage)

        @block.tensor
        def _(pe):
            pe.wait_ge(ld, 16 * 11)
            pe.wait_ge(z, 1)
            for c, w in chunks(pe):
                pe.wait_ge(kt_mx, c + 1)
                for m in range(DK):
                    for q in range(DK):
                        last = nc.tensor.matmul(pk[m][:, 0:w], wk[:, q, m * P:(m + 1) * P],
                                                k.xnT[:, q, ds(c * CH, w)], start=q == 0, stop=q == DK - 1)
                last.then_inc(kt_mm, 1)
            pe.wait_ge(kt_mx, NC + 1)
            pe.sem_inc(key_done, CREDIT)
            pe.sem_inc(et_done, CREDIT)
            pe.sem_inc(acc_done, CREDIT)
            for m in range(DK):
                nc.tensor.matmul(pp[m][:, 0:D + 1], zf[:, 0:P], zf[:, 0:D + 1], start=True, stop=False)
            nc.tensor.matmul(ph[:, 0:NT], zb[:, :], zb[:, 0:NT], start=True, stop=False)

            def key(t, b, rows, i):
                pe.wait_ge(exp_done, freed(t))
                for m in range(DK):
                    for q in range(DK):
                        last = nc.tensor.matmul(pk[b][:, m * P:m * P + rows], wk[:, q, m * P:(m + 1) * P],
                                                k.xnT[:, q, ds(t * P, rows)], start=q == 0, stop=q == DK - 1)
                last.then_inc(key_done, 1)

            def turn(t, b, rows, i):
                pe.wait_ge(exp_done, done(t))
                pe.wait_ge(e2_done, freed(t))
                for m in range(DK):
                    last = nc.tensor.transpose(pe_[b][:rows, m * P:(m + 1) * P], es[:, b, m, 0:rows], k.ident[:, :])
                last.then_inc(et_done, 1)

            def accumulate(t, b, rows, i):
                pe.wait_ge(e2_done, done(t))
                for m in range(DK):
                    nc.tensor.matmul(pp[m][:, 0:D], e2[:rows, b, m * P:(m + 1) * P], k.xn[:rows, ds(t, 1), :],
                                     start=False, stop=False)
                    last = nc.tensor.matmul(pp[m][:, D:D + 1], e2[:rows, b, m * P:(m + 1) * P], k.ones[:rows, 0:1],
                                            start=False, stop=False)
                last.then_inc(acc_done, 1)

            def count_dst(s, b, rows, i):
                pe.wait_ge(oh_done, done(s))
                for c in range(COLS):
                    last = nc.tensor.matmul(ph[:, 0:NT], oh_lo[:, b, c, :], oh_hi[:, b, c, :], start=False, stop=False)
                last.then_inc(hist_mm, 1)

            pe.sem_inc(hist_mm, CREDIT)
            pipeline(pe, (0, key), (1, turn), (2, accumulate), (2, count_dst))
            for m in range(DK):
                last = nc.tensor.matmul(pp[m][:, 0:D + 1], zf[:, 0:P], zf[:, 0:D + 1], start=False, stop=True)
            last.then_inc(tail_pe, 1)
            nc.tensor.matmul(ph[:, 0:NT], zb[:, :], zb[:, 0:NT], start=False, stop=True).then_inc(hist_mm, 1)
            pe.wait_ge(tail_v, 1)
            for m in range(DK):
                for c in range(DK):
                    nc.tensor.transpose(pk[m][:, c * P:(c + 1) * P], pn[:, m, c * P:(c + 1) * P], k.ident[:, :])
                    last = nc.tensor.transpose(pe_[m][:, c * P:(c + 1) * P], wq[:, m, c * P:(c + 1) * P], k.ident[:, :])
            last.then_inc(tail_pe, 1)
            pe.wait_ge(tail_v, 2)
            for m in range(DK):
                for c in range(DK):
                    last = nc.tensor.matmul(pp[m][:, 0:D], pnT[:, c, m * P:(m + 1) * P], wv[:, c, :],
                                            start=c == 0, stop=c == DK - 1)
            last.then_inc(tail_pe, 1)
            pe.wait_ge(tail_v, 4)
            for m in range(DK):
                for c in range(DK):
                    nc.tensor.matmul(pk[m][:, 0:D], wqT[:, c, m * P:(m + 1) * P], bn[:, c, :],
                                     start=c == 0, stop=c == DK - 1)
            for c in range(DK):
                last = nc.tensor.matmul(px[:, 0:D], bq_rep[:, c, :], bn[:, c, :], start=c == 0, stop=c == DK - 1)
            last.then_inc(tail_pe, 1)
            pe.sem_inc(o_tr, 6)
            pe.sem_inc(o_mm, COLS)
            pe.wait_ge(o_start, 1)

            def turn_hots(b, q, n, x):
                a, w = W[q]
                pe.wait_ge(o_hot, n + 1)
                pe.wait_ge(o_ev, n + 1)
                for j in range(w):
                    nc.tensor.transpose(turned(pk[x], P, w)[:, j, :], oh_lo[:, b, a + j, :], identb[:, :])
                    last = nc.tensor.transpose(turned(pe_[x], NT, w)[:, j, :], oh_hi[:, b, a + j, :], identb[:, :])
                last.then_inc(o_tr, 1)

            def products(g, b, q, n, x):
                a, w = W[q]
                if q < 2:
                    turn_hots(b, q + 1, n + 1, 1 - x)
                else:
                    turn_hots(1 - b, 0, n + 1, 1 - x)
                pe.wait_ge(o_ev, n + 3)
                for c in range(a, a + w):
                    m = COLS * g + c
                    out, ago = bank(b, c)
                    out = out[:, 0:HT]
                    pe.wait_ge(o_red, m + 6 - ago)
                    for j in range(3):
                        nc.tensor.matmul(out, loT[:, x, c - a, :], tab[:, j, :, :].rearrange("p h t -> p (h t)"),
                                         start=j == 0, stop=False)
                    nc.tensor.matmul(out, hiT[:, x, c - a, :], mask[:, :, :].rearrange("p h t -> p (h t)"),
                                     start=False, stop=True).then_inc(o_mm, 1)

            turn_hots(0, 0, 0, 0)
            batches(pe, products)
    st.close()


def scan_max(k):
    nc, ins = k.nc, k.ins
    st = ExitStack()
    sb = lambda *a: k.sb(st, *a)
    prev = sb("dst_before", [P, STRIP], I32)
    neg = sb("run_starts", [P, STRIP])
    run = sb("running_max", [P, STRIP, H])
    a8, bA, bB, ci, carry = (sb(n, s) for n, s in (("starts8", [P, H]), ("startsT", [H, P]), ("lastT", [H, P]),
                                                    ("carryT", [H, P + 1]), ("carry", [P, H])))
    T1 = NT + 1
    total, base, gk, gkf, val = (sb(n, [P, T1]) for n in ("tile_edges", "tile_start", "group_start", "groups", "offset"))
    gi = sb("groups_int", [P, T1], I32)
    start, has, node, t1, t2 = (sb(n, [P, NT]) for n in ("node_start", "has_edges", "node_number", "tmp1", "tmp2"))
    node_i = sb("node_int", [P, NT], I32)
    sidx, eidx = sb("first_edge", [P, NT], I32), sb("last_edge", [P, NT], I32)
    G4 = TABLE // P
    gno_i, gno = sb("group_int", [P, G4], I32), sb("group_number", [P, G4])
    cmp_ = sb("group_compare", [P, G4, T1])
    tg, bs = sb("group_tile", [P, G4, 1]), sb("group_base", [P, G4, 1])
    tab = sb("table", [P, 2, G4], I32)
    mx, v16, zz = sb("node_max", [P, NT, H]), sb("node_er_m", [P, NT, 2 * H]), sb("node_sum", [P, NT, H])
    pa, pb, pc, pd = (k.ps(st, n, [P, 512]) for n in ("pA", "pB", "pC", "pD"))
    (ld, pad, own, carry_s, pe_s, v_s, stored, cons, g_in, m_s, sc) = (
        k.sem("p3_" + n) for n in ("loaded", "padded", "dve", "carry", "pe", "dve_to_pe", "stored", "const", "max_in",
                                   "node_max", "scattered"))
    with nc.Block() as block:
        @block.sync
        def _(sp):
            dst = ins["dst"]
            sp.wait_ge(pad, 1)
            body = (P - 1) * STRIP
            sp.dma_start(k.dst_i[0:P - 1, :], dst[0:body].rearrange("(p c) -> p c", c=STRIP)).then_inc(ld, 16)
            sp.dma_start(k.dst_i[P - 1:P, 0:EL_LAST], dst[body:E].rearrange("(p c) -> p c", p=1)).then_inc(ld, 16)
            sp.dma_start(prev[0:1, 1:STRIP], dst[0:STRIP - 1].rearrange("(p c) -> p c", p=1)).then_inc(ld, 16)
            sp.dma_start(prev[1:P - 1, :], dst[STRIP - 1:body - 1].rearrange("(p c) -> p c", c=STRIP)).then_inc(ld, 16)
            sp.dma_start(prev[P - 1:P, 0:EL_LAST + 1], dst[body - 1:E].rearrange("(p c) -> p c", p=1)).then_inc(ld, 16)
            sp.wait_ge(v_s, 4)
            with nc.allow_non_contiguous_dma("a small table, once"):
                for j in range(2):
                    sp.dma_start(k.table_d[j, :].rearrange("(c p) -> p c", p=P), tab[:, j, :]).then_inc(stored, 16)
            sp.wait_ge(v_s, 6)
            sp.dma_start(k.scan_d.rearrange("(p c) h -> p (c h)", p=P), run[:, :, :].rearrange("p c h -> p (c h)")).then_inc(stored, 16)
            sp.wait_ge(stored, 48)

        @block.gpsimd
        def _(pool):
            pool.iota(node_i[:, :], [[P, NT]], base=0, channel_multiplier=1).then_inc(cons, 1)
            pool.iota(gno_i[:, :], [[P, G4]], base=0, channel_multiplier=1).then_inc(cons, 1)
            pool.wait_ge(stored, 48)
            pool.wait_ge(v_s, 4)
            for t in range(NT):
                pool.indirect_dma_start(mx[:, t, :], None, k.scan_d[:, :], IndexOn(ap=eidx[:, t:t + 1], axis=0)).then_inc(g_in, 16)
            pool.wait_ge(m_s, 1)
            for t in range(NT):
                pool.indirect_dma_start(k.fill_d[:, :], IndexOn(ap=sidx[:, t:t + 1], axis=0), v16[:, t, :], None).then_inc(sc, 16)
            pool.wait_ge(sc, 16 * NT)

        @block.vector
        def _(dve):
            link = Chain(dve, own)
            link(dve.memset(k.dst_i[:, :], PAD_DST))
            link(dve.memset(prev[:, :], -1))
            dve.sem_inc(pad, 1)
            dve.wait_ge(pe_s, 1)
            link(dve.memset(total[:, :], 0.0))
            link(dve.tensor_copy(total[:, 0:NT], pb[:, 0:NT]))
            link(dve.memset(base[:, :], 0.0))
            link(dve.memset(gk[:, :], 0.0))
            link(dve.tensor_tensor_scan(base[:, 1:T1], k.ones[:, 0:NT], total[:, 0:NT], 0.0, ALU.mult, ALU.add))
            link(dve.tensor_tensor(start[:, :], pa[:, 0:NT], base[:, 0:NT], ALU.add))
            dve.wait_ge(cons, 2)
            link(dve.tensor_copy(node[:, :], node_i[:, :]))
            link(dve.tensor_copy(gno[:, :], gno_i[:, :]))
            link(dve.tensor_scalar(has[:, :], k.count[:, :], 0.0, None, ALU.is_gt))
            link(dve.tensor_tensor(t1[:, :], start[:, :], has[:, :], ALU.mult))
            link(dve.tensor_scalar(node[:, :], node[:, :], float(ES), None, ALU.add))
            link(dve.tensor_tensor(t2[:, :], node[:, :], has[:, :], ALU.mult))
            link(dve.tensor_tensor(t2[:, :], node[:, :], t2[:, :], ALU.subtract))
            link(dve.tensor_tensor(sidx[:, :], t1[:, :], t2[:, :], ALU.add))
            link(dve.tensor_tensor(t1[:, :], start[:, :], k.count[:, :], ALU.add))
            link(dve.tensor_scalar(eidx[:, :], t1[:, :], -1.0, 0.0, ALU.add, ALU.max))
            link(dve.tensor_scalar(t1[:, :], total[:, 0:NT], float(GE - 1), None, ALU.add))
            link(dve.tensor_copy(gi[:, 0:NT], t1[:, :]))
            link(dve.tensor_single_scalar(gi[:, 0:NT], gi[:, 0:NT], GE.bit_length() - 1, ALU.logical_shift_right))
            link(dve.tensor_copy(gkf[:, 0:NT], gi[:, 0:NT]))
            link(dve.tensor_tensor_scan(gk[:, 1:T1], k.ones[:, 0:NT], gkf[:, 0:NT], 0.0, ALU.mult, ALU.add))
            link(dve.scalar_tensor_tensor(val[:, :], gk[:, :], -float(GE), base[:, :], ALU.mult, ALU.add))
            b3 = lambda a, n: a.unsqueeze(1).broadcast_to([P, G4, n])
            link(dve.tensor_tensor(cmp_[:, :, 0:NT], b3(gk[:, 1:T1], NT), gno[:, :].unsqueeze(2).broadcast_to([P, G4, NT]), ALU.is_le))
            link(dve.tensor_reduce(tg[:, :, 0], cmp_[:, :, 0:NT], AX.X, ALU.add))
            link(dve.tensor_tensor(cmp_[:, :, :], b3(k.iota[:, 0:T1], T1), tg[:, :, :].broadcast_to([P, G4, T1]), ALU.is_equal))
            link(dve.tensor_tensor(cmp_[:, :, :], cmp_[:, :, :], b3(val[:, :], T1), ALU.mult))
            link(dve.tensor_reduce(bs[:, :, 0], cmp_[:, :, :], AX.X, ALU.add))
            link(dve.scalar_tensor_tensor(bs[:, :, 0], gno[:, :], float(GE), bs[:, :, 0], ALU.mult, ALU.add))
            link(dve.tensor_scalar(tab[:, 0, :], bs[:, :, 0], float(E), None, ALU.min))
            link(dve.tensor_scalar(tab[:, 1, :], tg[:, :, 0], float(NT - 1), None, ALU.min))
            dve.sem_inc(v_s, 4)
            dve.wait_ge(ld, 80)
            link(dve.tensor_tensor(k.cont[:, :], k.dst_i[:, :], prev[:, :], ALU.is_equal))
            link(dve.tensor_scalar(neg[:, :], k.cont[:, :], 1.0, BIG, ALU.subtract, ALU.mult))
            for h in range(H):
                link(dve.tensor_tensor_scan(run[:, :, h], neg[:, :], k.el_e[:, :, h], -BIG, ALU.add, ALU.max))
            link(dve.tensor_reduce(a8[:, 0:1], neg[:, :], AX.X, ALU.min))
            link(dve.tensor_copy(a8[:, 1:H], a8[:, 0:1].broadcast_to([P, H - 1])))
            dve.sem_inc(v_s, 1)
            dve.wait_ge(pe_s, 2)
            link(dve.tensor_copy(bA[:, :], pc[0:H, 0:P]))
            link(dve.tensor_copy(bB[:, :], pd[0:H, 0:P]))
            link(dve.memset(ci[:, :], -BIG))
            link(dve.tensor_tensor_scan(ci[:, 1:P + 1], bA[:, :], bB[:, :], -BIG, ALU.add, ALU.max))
            dve.sem_inc(carry_s, 1)
            dve.wait_ge(pe_s, 3)
            link(dve.tensor_copy(carry[:, :], pc[:, 0:H]))
            for h in range(H):
                link(dve.tensor_tensor_scan(run[:, :, h], neg[:, :], k.el_e[:, :, h], carry[:, h:h + 1], ALU.add, ALU.max))
            dve.sem_inc(v_s, 1)
            link(dve.tensor_copy(v16[:, :, 0:H], k.elr[:, :, H:2 * H]))
            dve.wait_ge(g_in, 16 * NT)
            link(dve.tensor_tensor(zz[:, :, :], mx[:, :, :], k.elr[:, :, H:2 * H], ALU.add))
            link(dve.scalar_tensor_tensor(v16[:, :, H:2 * H], zz[:, :, :], 0.2, zz[:, :, :], ALU.mult, ALU.max))
            dve.sem_inc(m_s, 1)

        @block.tensor
        def _(pe):
            nc.tensor.matmul(pa[:, 0:NT], k.upper[:, :], k.count[:, :], start=True, stop=True)
            nc.tensor.matmul(pb[:, 0:NT], k.ones[:, :], k.count[:, :], start=True, stop=True).then_inc(pe_s, 1)
            pe.wait_ge(v_s, 5)
            nc.tensor.transpose(pc[0:H, 0:P], a8[:, :], k.ident[:, :])
            nc.tensor.transpose(pd[0:H, 0:P], run[:, STRIP - 1, :], k.ident[:, :]).then_inc(pe_s, 1)
            pe.wait_ge(carry_s, 1)
            nc.tensor.transpose(pc[:, 0:H], ci[:, 0:P], k.ident[0:H, 0:H]).then_inc(pe_s, 1)
    st.close()


def scan_weights(k):
    nc, ins = k.nc, k.ins
    st = ExitStack()
    sb = lambda *a: k.sb(st, *a)
    R = H + 2
    fl = sb("node_values", [P, STRIP, 2 * H])
    rec = sb("records", [P, STRIP, R])
    src = sb("src_strips", [P, STRIP], I32)
    pcont, zero = sb("run_from_before", [P, STRIP]), sb("zero_strip", [P, STRIP])
    tail = sb("tail_records", [P, (EROWS - E) // P, R])
    a16, bA, bB, ci, carry = (sb(n, s) for n, s in (("cont16", [P, 2 * H]), ("contT", [2 * H, P]), ("lastT", [2 * H, P]),
                                                    ("carryT", [2 * H, P + 1]), ("carry", [P, 2 * H])))
    pc, pd = (k.ps(st, n, [P, 512]) for n in ("pC", "pD"))
    ld, pad, own, pe_s, v_s, stored, ex = (k.sem("p4_" + n) for n in ("loaded", "padded", "dve", "pe", "dve_done",
                                                                      "stored", "exp"))
    with nc.Block() as block:
        @block.sync
        def _(sp):
            body = (P - 1) * STRIP
            sp.dma_start(fl[:, :, :].rearrange("p c h -> p (c h)"), k.fill_d[0:ES, :].rearrange("(p c) h -> p (c h)", p=P)).then_inc(ld, 16)
            sp.wait_ge(pad, 1)
            sp.dma_start(src[0:P - 1, :], ins["src"][0:body].rearrange("(p c) -> p c", c=STRIP)).then_inc(ld, 16)
            sp.dma_start(src[P - 1:P, 0:EL_LAST], ins["src"][body:E].rearrange("(p c) -> p c", p=1)).then_inc(ld, 16)
            sp.wait_ge(ex, 1)
            sp.wait_ge(v_s, 3)
            sp.dma_start(k.edge_d[0:body, :].rearrange("(p c) r -> p (c r)", c=STRIP), rec[0:P - 1, :, :].rearrange("p c r -> p (c r)")).then_inc(stored, 16)
            sp.dma_start(k.edge_d[body:E, :].rearrange("(p c) r -> p (c r)", p=1), rec[P - 1:P, 0:EL_LAST, :].rearrange("p c r -> p (c r)")).then_inc(stored, 16)
            sp.dma_start(k.edge_d[E:EROWS, :].rearrange("(p c) r -> p (c r)", p=P), tail[:, :, :].rearrange("p c r -> p (c r)")).then_inc(stored, 16)
            sp.wait_ge(stored, 48)

        @block.scalar
        def _(act):
            act.wait_ge(v_s, 4)
            nc.scalar.activation(rec[:, :, 0:H], k.el_e[:, :, :], ACT.Exp).then_inc(ex, 1)

        @block.vector
        def _(dve):
            link = Chain(dve, own)
            link(dve.memset(src[:, :], 0))
            dve.sem_inc(pad, 1)
            link(dve.memset(zero[:, :], 0.0))
            link(dve.memset(tail[:, :, :], 0.0))
            link(dve.memset(tail[:, :, H:H + 1], float(PAD_DST)))
            link(dve.tensor_tensor_scan(pcont[:, :], k.cont[:, :], zero[:, :], 1.0, ALU.mult, ALU.add))
            link(dve.tensor_copy(a16[:, :], pcont[:, STRIP - 1:STRIP].broadcast_to([P, 2 * H])))
            dve.wait_ge(ld, 48)
            link(dve.tensor_copy(rec[:, :, H], k.dst_i[:, :]))
            link(dve.tensor_copy(rec[:, :, H + 1].bitcast(I32), src[:, :]))
            for h in range(2 * H):
                link(dve.tensor_tensor_scan(fl[:, :, h], k.cont[:, :], fl[:, :, h], 0.0, ALU.mult, ALU.add))
            dve.sem_inc(v_s, 1)
            dve.wait_ge(pe_s, 1)
            link(dve.tensor_copy(bA[:, :], pc[0:2 * H, 0:P]))
            link(dve.tensor_copy(bB[:, :], pd[0:2 * H, 0:P]))
            link(dve.memset(ci[:, 0:1], 0.0))
            link(dve.tensor_tensor_scan(ci[:, 1:P + 1], bA[:, :], bB[:, :], 0.0, ALU.mult, ALU.add))
            dve.sem_inc(v_s, 1)
            dve.wait_ge(pe_s, 2)
            link(dve.tensor_copy(carry[:, :], pc[:, 0:2 * H]))
            for h in range(2 * H):
                link(dve.scalar_tensor_tensor(fl[:, :, h], pcont[:, :], carry[:, h:h + 1], fl[:, :, h], ALU.mult, ALU.add))
            dve.sem_inc(v_s, 1)
            link(dve.tensor_tensor(k.el_e[:, :, :], k.el_e[:, :, :], fl[:, :, 0:H], ALU.add))
            link(dve.scalar_tensor_tensor(k.el_e[:, :, :], k.el_e[:, :, :], 0.2, k.el_e[:, :, :], ALU.mult, ALU.max))
            link(dve.tensor_tensor(k.el_e[:, :, :], k.el_e[:, :, :], fl[:, :, H:2 * H], ALU.subtract))
            dve.sem_inc(v_s, 1)

        @block.tensor
        def _(pe):
            pe.wait_ge(v_s, 1)
            nc.tensor.transpose(pc[0:2 * H, 0:P], a16[:, :], k.ident[:, :])
            nc.tensor.transpose(pd[0:2 * H, 0:P], fl[:, STRIP - 1, :], k.ident[:, :]).then_inc(pe_s, 1)
            pe.wait_ge(v_s, 2)
            nc.tensor.transpose(pc[:, 0:2 * H], ci[:, 0:P], k.ident[0:2 * H, 0:2 * H]).then_inc(pe_s, 1)
    st.close()


def message(k):
    nc, ins = k.nc, k.ins
    st = ExitStack()
    sb = lambda *a: k.sb(st, *a)
    U, R = 8, H + 2
    nodes_i, nodes = sb("nodes_int", [P, 1024], I32), sb("node_numbers", [P, NP])
    tabs = sb("table_row", [1, 2 * TABLE], I32)
    rec = sb("group_records", [P, U, GJ * R])
    feat = sb("group_feat", [P, U, GJ, D])
    oh, wt = sb("group_onehot", [P, U, GJ, P]), sb("group_weighted", [P, U, GJ, GF])
    ps = [k.ps(st, f"pSum{u}", [P, 512]) for u in range(U)]
    rec_in = [k.sem(f"p5_record{u}") for u in range(U)]
    feat_in = [k.sem(f"p5_feat{u}") for u in range(U)]
    zero, tab_in, made, ex_done, mm_done, sum_done, ip = (k.sem("p5_" + n) for n in ("zero", "table", "weighted",
                                                          "weights", "products", "sums", "nodes"))
    with nc.Block() as block:
        @block.sync
        def _(sp):
            sp.dma_start(tabs[:, :], k.table_d.rearrange("a g -> (a g)").rearrange("(o g) -> o g", o=1)).then_inc(tab_in, 16)
            sp.wait_ge(tab_in, 16)
            with sp.Fori(0, NG // U) as i:
                for u in range(U):
                    g = U * i + u
                    base = sp.value_load(tabs[0:1, ds(g, 1)], min_val=0, max_val=E)
                    sp.wait_ge(sum_done, g + 1)
                    sp.dma_start(rec[:, u, :], k.edge_d[ds(base, GE), :].rearrange("(p j) r -> p (j r)", j=GJ)).then_inc(rec_in[u], 16)

        @block.gpsimd
        def _(pool):
            for a in range(0, NP, 1024):
                w = min(1024, NP - a)
                pool.iota(nodes_i[:, 0:w], [[1, w]], base=a, channel_multiplier=0).then_inc(ip, 1)
                pool.wait_ge(ip, 2 * (a // 1024) + 1)
                pool.tensor_copy(nodes[:, a:a + w], nodes_i[:, 0:w]).then_inc(ip, 1)
                pool.wait_ge(ip, 2 * (a // 1024) + 2)
            with pool.Fori(0, NG // U) as i:
                for u in range(U):
                    pool.wait_ge(rec_in[u], 16 * i + 16)
                    settle(pool, k.passed)
                    for j in range(GJ):
                        at = j * R + H + 1
                        pool.indirect_dma_start(feat[:, u, j, :], None, k.feat_d[:, :],
                                                IndexOn(ap=rec[:, u, at:at + 1].bitcast(I32), axis=0)).then_inc(feat_in[u], 16)

        @block.scalar
        def _(act):
            act.sem_inc(ex_done, U)
            with act.Fori(0, NG // U) as i:
                for u in range(U):
                    act.wait_ge(rec_in[u], 16 * i + 16)
                    act.wait_ge(mm_done, U * i + u + 1)
                    r = rec[:, u, :].rearrange("p (j r) -> p j r", j=GJ)
                    nc.scalar.activation(wt[:, u, :, D:GF], r[:, :, 0:H], ACT.Copy).then_inc(ex_done, 1)

        @block.vector
        def _(dve):
            dve.memset(k.agg[:, :, :], 0.0).then_inc(zero, 1)
            dve.wait_ge(zero, 1)
            dve.wait_ge(ip, 2 * (-(-NP // 1024)))
            dve.wait_ge(tab_in, 16)
            dve.sem_inc(made, U)
            dve.sem_inc(sum_done, U)
            with dve.Fori(0, NG // U) as i:
                tile = {}

                def weigh(u):
                    g = U * i + u
                    tile[u] = dve.value_load(tabs[0:1, ds(TABLE + g, 1)], min_val=0, max_val=NT - 1)
                    dve.wait_ge(rec_in[u], 16 * i + 16)
                    dve.wait_ge(mm_done, g + 1)
                    for j in range(GJ):
                        dve.tensor_scalar(oh[:, u, j, :], nodes[:, ds(tile[u] * P, P)], rec[:, u, j * R + H:j * R + H + 1],
                                          None, ALU.is_equal)
                    dve.wait_ge(feat_in[u], 16 * GJ * (i + 1))
                    for j in range(GJ):
                        last = dve.tensor_tensor(wt[:, u, j, 0:D].rearrange("p (h c) -> p h c", h=H),
                                                 feat[:, u, j, :].rearrange("p (h c) -> p h c", h=H),
                                                 rec[:, u, j * R:j * R + H].unsqueeze(2).broadcast_to([P, H, HD]), ALU.mult)
                    last.then_inc(made, 1)

                def add(u):
                    g = U * i + u
                    dve.wait_ge(mm_done, g + 1 + U)
                    dve.wait_ge(sum_done, g + U)
                    dve.tensor_tensor(k.agg[:, ds(tile[u], 1), :], k.agg[:, ds(tile[u], 1), :],
                                      ps[u][:, 0:GF].unsqueeze(1), ALU.add).then_inc(sum_done, 1)

                weigh(0)
                for u in range(1, U):
                    weigh(u)
                    add(u - 1)
                add(U - 1)

        @block.tensor
        def _(pe):
            pe.sem_inc(mm_done, U)
            with pe.Fori(0, NG // U) as i:
                for u in range(U):
                    g = U * i + u
                    pe.wait_ge(made, g + 1 + U)
                    pe.wait_ge(ex_done, g + 1 + U)
                    pe.wait_ge(sum_done, g + 1)
                    for j in range(GJ):
                        last = nc.tensor.matmul(ps[u][:, 0:GF], oh[:, u, j, :], wt[:, u, j, :], start=j == 0, stop=j == GJ - 1)
                    last.then_inc(mm_done, 1)
    st.close()


def update(k):
    nc, ins = k.nc, k.ins
    st = ExitStack()
    sb = lambda *a: k.sb(st, *a)
    gb, wr = sb("gat_bias_rows", [P, D]), sb("w_router", [P, DK, X])
    xs, xn = sb("x_in", [P, 2, D]), sb("x2n_stage", [P, 2, D])
    xt, x2t = sb("xT_stage", [P, 2, DK, P]), sb("x2T_stage", [P, 2, DK, P])
    s1, g1, xc = sb("weight_sum", [P, H]), sb("messages", [P, D]), sb("x_plus_bias", [P, 2, D])
    stats, mv, sd, rs = (sb(n, [P, 2, w]) for n, w in (("stats", 6), ("mv", 2), ("sd", 1), ("rs", 1)))
    pu = [k.ps(st, f"pU{b}", [P, 512]) for b in range(2)]
    pt = [k.ps(st, f"pT{b}", [P, 512]) for b in range(2)]
    pl = [k.ps(st, f"pL{b}", [P, 512]) for b in range(2)]
    x_in = [k.sem(f"p6_x_in{b}") for b in range(2)]
    stored = [k.sem(f"p6_stored{b}") for b in range(2)]
    (ld, xt_done, mm_done, u_done, mv_done, sd_done, xn_done, tr_done, x2t_done, lg_mm, lg_done, own, own_r, xc_done, x2_st, z) = (
        k.sem("p6_" + n) for n in ("loaded", "xT", "products", "x2", "mv", "sd", "x2n", "transposed", "x2T",
                                   "logits_mm", "logits", "dve", "dve_rs", "x_plus_bias", "x2_stored", "zero"))
    LINKS = 7
    with nc.Block() as block:
        @block.sync
        def _(sp):
            sp.dma_start(gb[:, :], ins["L0_gnn_gat_bias"].partition_broadcast(P)).then_inc(ld, 16)
            sp.dma_start(wr[:, :, :], ins["L0_ffn_Wr"].rearrange("(k p) n -> p k n", p=P)).then_inc(ld, 16)
            prime(k, sp, stored)

            def load(t, b, rows, i):
                sp.wait_ge(u_done, freed(t))
                sp.dma_start(xs[:rows, b, :], ins["x"][ds(t * P, rows), :]).then_inc(x_in[b], 16)

            def store(t, b, rows, i):
                sp.wait_ge(xn_done, done(t))
                sp.dma_start(k.x2_d[ds(t * P, rows), :].unsqueeze(1), k.agg[:rows, ds(t, 1), 0:D]).then_inc(x2_st, 16)
                sp.dma_start(k.x2n_d[ds(t * P, rows), :], xn[:rows, b, :]).then_inc(stored[b], 16)

            pipeline(sp, (0, load), (2, store))
            for b in range(2):
                sp.wait_ge(stored[b], 16 * (NT // 2 + 2 - b))
            sp.wait_ge(x2_st, 16 * NT)

        @block.gpsimd
        def _(pool):
            def x_bias(t, b, rows, i):
                pool.wait_ge(x_in[b], 16 * i + 16)
                pool.wait_ge(u_done, freed(t))
                pool.tensor_tensor(xc[:rows, b, :], xs[:rows, b, :], k.cb[:rows, :], ALU.add).then_inc(xc_done, 1)

            pipeline(pool, (0, x_bias))

        @block.vector
        def _(dve):
            dve.memset(k.logits[:, :, :], 0.0).then_inc(z, 1)
            dve.sem_inc(u_done, CREDIT)
            dve.sem_inc(xn_done, CREDIT)
            dve.wait_ge(ld, 32)
            h3 = lambda a: a.rearrange("p (h c) -> p h c", h=H)

            def residual(t, b, rows, i):
                link = Chain(dve, own, LINKS * t)
                link(dve.tensor_scalar(s1[:rows, :].unsqueeze(1), k.agg[:rows, ds(t, 1), D:GF], 1.0e-30, None, ALU.max))
                link(dve.reciprocal(s1[:rows, :], s1[:rows, :]))
                link(dve.tensor_tensor(h3(g1[:rows, :]), k.agg[:rows, ds(t, 1), 0:D].rearrange("p a (h c) -> p (a h) c", h=H),
                                       s1[:rows, :].unsqueeze(2).broadcast_to([rows, H, HD]), ALU.mult))
                link(dve.tensor_tensor(g1[:rows, :], g1[:rows, :], gb[:rows, :], ALU.add))
                link(dve.scalar_tensor_tensor(g1[:rows, :], g1[:rows, :], 0.01, g1[:rows, :], ALU.mult, ALU.max))
                dve.wait_ge(x_in[b], 16 * i + 16)
                dve.wait_ge(xc_done, t + 1)
                link(dve.tensor_tensor(g1[:rows, :], g1[:rows, :], xc[:rows, b, :], ALU.add))
                dve.wait_ge(mm_done, done(t))
                x2 = k.agg[:rows, ds(t, 1), 0:D].rearrange("p a d -> p (a d)")
                dve.tensor_tensor(x2, pu[b][:rows, 0:D], g1[:rows, :], ALU.add).then_inc(u_done, 1)
                dve.wait_ge(u_done, done(t))
                settle(dve, k.passed)
                link(dve.bn_stats(stats[:rows, b, :], x2))
                settle(dve, k.passed)
                dve.bn_aggr(mv[:rows, b, :], stats[:rows, b, :]).then_inc(mv_done, 1)
                assert link.n == LINKS

            def normalise(t, b, rows, i):
                dve.wait_ge(sd_done, t + 1)
                Chain(dve, own_r, t)(dve.reciprocal(rs[:rows, b, :], sd[:rows, b, :]))
                dve.wait_ge(tr_done, freed(t))
                dve.wait_ge(stored[b], 16 * i + 16)
                dve.tensor_scalar(xn[:rows, b, :], k.agg[:rows, ds(t, 1), 0:D].rearrange("p a d -> p (a d)"), mv[:rows, b, 0:1], rs[:rows, b, :],
                                  ALU.subtract, ALU.mult).then_inc(xn_done, 1)

            pipeline(dve, (0, residual), (1, normalise))

        @block.scalar
        def _(act):
            act.sem_inc(xt_done, CREDIT)
            act.sem_inc(x2t_done, CREDIT)
            act.sem_inc(lg_done, CREDIT)
            act.wait_ge(z, 1)

            def stage_xT(t, b, rows, i):
                act.wait_ge(mm_done, freed(t))
                nc.scalar.activation(xt[:, b, :, 0:rows], k.xnT[:, :, ds(t * P, rows)], ACT.Copy).then_inc(xt_done, 1)

            def deviation(t, b, rows, i):
                act.wait_ge(mv_done, t + 1)
                nc.scalar.activation(sd[:rows, b, :], mv[:rows, b, 1:2], ACT.Sqrt, bias=k.eps[:rows, :]).then_inc(sd_done, 1)

            def turned(t, b, rows, i):
                act.wait_ge(tr_done, done(t))
                act.wait_ge(lg_mm, freed(t))
                nc.scalar.activation(x2t[:, b, :, 0:rows], pt[b][:, 0:DK * P].rearrange("p (k n) -> p k n", k=DK)[:, :, 0:rows],
                                     ACT.Copy).then_inc(x2t_done, 1)

            def keep_logits(t, b, rows, i):
                act.wait_ge(lg_mm, done(t))
                nc.scalar.activation(k.logits[:rows, ds(t, 1), :], pl[b][:rows, 0:X].unsqueeze(1), ACT.Copy).then_inc(lg_done, 1)

            pipeline(act, (0, stage_xT), (3, turned), (4, keep_logits), (2, deviation))

        @block.tensor
        def _(pe):
            for s in (mm_done, tr_done, lg_mm):
                pe.sem_inc(s, CREDIT)
            pe.wait_ge(ld, 32)

            def product(t, b, rows, i):
                pe.wait_ge(xt_done, done(t))
                pe.wait_ge(u_done, freed(t))
                for c in range(DK):
                    last = nc.tensor.matmul(pu[b][:rows, 0:D], xt[:, b, c, 0:rows], k.w_lin[:, c, :], start=c == 0, stop=c == DK - 1)
                last.then_inc(mm_done, 1)

            def turn(t, b, rows, i):
                pe.wait_ge(xn_done, done(t))
                pe.wait_ge(x2t_done, freed(t))
                for c in range(DK):
                    last = nc.tensor.transpose(pt[b][:, c * P:c * P + rows], xn[:rows, b, c * P:(c + 1) * P], k.ident[:rows, :rows])
                last.then_inc(tr_done, 1)

            def router(t, b, rows, i):
                pe.wait_ge(x2t_done, done(t))
                pe.wait_ge(lg_done, freed(t))
                for c in range(DK):
                    last = nc.tensor.matmul(pl[b][:rows, 0:X], x2t[:, b, c, 0:rows], wr[:, c, :], start=c == 0, stop=c == DK - 1)
                last.then_inc(lg_mm, 1)

            pipeline(pe, (0, product), (2, turn), (3, router))
    st.close()


def load_weights(k, queue, experts):
    shared = ("L0_ffn_W1s", "L0_ffn_b1s", "L0_ffn_W2s", "L0_ffn_b2s")
    routed = ("L0_ffn_W1p", "L0_ffn_b1p", "L0_ffn_W2p", "L0_ffn_b2p")
    for e in experts:
        u, c1, d, c2 = (k.ins[n] if e == X else k.ins[n][e] for n in (shared if e == X else routed))
        landed = k.shared_in if e == X else k.routed_in
        queue.dma_start(k.w_up[:, e, :, :], u.rearrange("(c p) f -> p c f", p=P)).then_inc(landed, 16)
        queue.dma_start(k.w_down[:, e, :, :], d.rearrange("(c p) n -> p c n", p=P)).then_inc(landed, 16)
        with k.nc.allow_non_contiguous_dma("short bias columns"):
            queue.dma_start(k.b_up[:, e, :], c1.rearrange("(c p) -> p c", p=P)).then_inc(landed, 16)
        queue.dma_start(k.b_down[:, e, :], c2.partition_broadcast(P)).then_inc(landed, 16)


def route(k):
    nc = k.nc
    st = ExitStack()
    sb = lambda *a: k.sb(st, *a)
    T1 = NT + 1
    node_i, node, valid, spare = sb("node_int", [P, NT], I32), sb("node_number", [P, NT]), sb("valid", [P, NT]), sb("spare_row", [P, NT])
    rev = sb("reversed", [P, 1, X])
    m1, m2, mt, dw = (sb(n, [P, NT, 1]) for n in ("best", "second", "first_index", "difference"))
    l2, t8, oh1, oh2, sel, slot = (sb(n, [P, NT, X]) for n in ("logits2", "tmp8", "choice1", "choice2", "selected", "slot"))
    tb = sb("before_tile", [P, T1, X])
    nbf, be = sb("expert_blocks", [P, X]), sb("block_end", [P, X + 1])
    nbi = sb("expert_blocks_int", [P, X], I32)
    bno_i, bno, cmp_, eb, ebi = (sb("block_int", [P, 2], I32), sb("block_number", [P, 2]), sb("block_compare", [P, 2, X]),
                                 sb("block_expert", [P, 2, 1]), sb("block_expert_int", [P, 2], I32))
    pos = sb("choice_slot", [P, NT])
    gate = sb("gates", [P, 2, NT])
    pr, pq = k.ps(st, "pRank", [P, 512]), k.ps(st, "pSum", [P, 512])
    own, cons, pe_s, v_s, ex, stored = (k.sem("p7_" + n) for n in ("dve", "const", "pe", "dve_done", "exp", "stored"))
    with nc.Block() as block:
        @block.sync
        def _(sp):
            load_weights(k, sp, (X,))
            sp.wait_ge(v_s, 3)
            with nc.allow_non_contiguous_dma("a small table, once"):
                sp.dma_start(k.block_d[0, :].rearrange("(c p) -> p c", p=P), ebi[:, :]).then_inc(stored, 16)
            sp.wait_ge(stored, 16)

        @block.gpsimd
        def _(pool):
            pool.iota(node_i[:, :], [[P, NT]], base=0, channel_multiplier=1).then_inc(cons, 1)
            pool.iota(bno_i[:, :], [[P, 2]], base=0, channel_multiplier=1).then_inc(cons, 1)

        @block.scalar
        def _(act):
            act.wait_ge(v_s, 1)
            nc.scalar.activation(dw[:, :, :], dw[:, :, :], ACT.Exp).then_inc(ex, 1)

        @block.vector
        def _(dve):
            link = Chain(dve, own)
            over_e = lambda a: a.broadcast_to([P, NT, X])
            dve.wait_ge(cons, 2)
            link(dve.tensor_copy(node[:, :], node_i[:, :]))
            link(dve.tensor_copy(bno[:, :], bno_i[:, :]))
            link(dve.tensor_scalar(valid[:, :], node[:, :], float(N), None, ALU.is_lt))
            link(dve.tensor_scalar(rev[:, 0, :], k.iota[:, 0:X], -1.0, float(X), ALU.mult, ALU.add))

            def choose(logits, best, out):
                link(dve.tensor_reduce(best[:, :, 0], logits[:, :, :], AX.X, ALU.max))
                link(dve.tensor_tensor(t8[:, :, :], logits[:, :, :], over_e(best[:, :, :]), ALU.is_equal))
                link(dve.tensor_tensor(t8[:, :, :], t8[:, :, :], rev[:, :, :].broadcast_to([P, NT, X]), ALU.mult))
                link(dve.tensor_reduce(mt[:, :, 0], t8[:, :, :], AX.X, ALU.max))
                link(dve.tensor_tensor(out[:, :, :], t8[:, :, :], over_e(mt[:, :, :]), ALU.is_equal))

            choose(k.logits, m1, oh1)
            link(dve.scalar_tensor_tensor(l2[:, :, :], oh1[:, :, :], -BIG, k.logits[:, :, :], ALU.mult, ALU.add))
            choose(l2, m2, oh2)
            link(dve.tensor_tensor(dw[:, :, :], m2[:, :, :], m1[:, :, :], ALU.subtract))
            dve.sem_inc(v_s, 1)
            for oh in (oh1, oh2):
                link(dve.tensor_tensor(oh[:, :, :], oh[:, :, :], over_e(valid[:, :].unsqueeze(2)), ALU.mult))
            link(dve.tensor_tensor(sel[:, :, :], oh1[:, :, :], oh2[:, :, :], ALU.add))
            dve.sem_inc(v_s, 1)
            dve.wait_ge(ex, 1)
            link(dve.tensor_scalar(gate[:, 0, :], dw[:, :, 0], 1.0, None, ALU.add))
            link(dve.reciprocal(gate[:, 0, :], gate[:, 0, :]))
            link(dve.tensor_tensor(gate[:, 1, :], gate[:, 0, :], dw[:, :, 0], ALU.mult))
            link(dve.tensor_copy(k.choice[:, :, :, 1], gate[:, :, :]))
            for j in range(2):
                link(dve.tensor_copy(k.choice[:, j, :, 0].bitcast(I32), node_i[:, :]))
            dve.wait_ge(pe_s, 1)
            link(dve.memset(tb[:, 0:1, :], 0.0))
            q3 = pq[:, 0:NT * X].rearrange("p (t e) -> p t e", e=X)
            for e in range(X):
                link(dve.tensor_tensor_scan(tb[:, 1:T1, e], k.ones[:, 0:NT], q3[:, :, e], 0.0, ALU.mult, ALU.add))
            link(dve.tensor_scalar(nbf[:, :], tb[:, NT, :], float(BLK - 1), None, ALU.add))
            link(dve.tensor_copy(nbi[:, :], nbf[:, :]))
            link(dve.tensor_single_scalar(nbi[:, :], nbi[:, :], BLK.bit_length() - 1, ALU.logical_shift_right))
            link(dve.tensor_copy(nbf[:, :], nbi[:, :]))
            link(dve.memset(be[:, 0:1], 0.0))
            link(dve.tensor_tensor_scan(be[:, 1:X + 1], k.ones[:, 0:X], nbf[:, :], 0.0, ALU.mult, ALU.add))
            link(dve.tensor_tensor(slot[:, :, :], pr[:, 0:NT * X].rearrange("p (t e) -> p t e", e=X), tb[:, 0:NT, :], ALU.add))
            link(dve.tensor_scalar(nbf[:, :], be[:, 0:X], float(BLK), None, ALU.mult))
            link(dve.tensor_tensor(slot[:, :, :], slot[:, :, :], nbf[:, :].unsqueeze(1).broadcast_to([P, NT, X]), ALU.add))
            for j, oh in enumerate((oh1, oh2)):
                link(dve.tensor_tensor(t8[:, :, :], oh[:, :, :], slot[:, :, :], ALU.mult))
                link(dve.tensor_reduce(pos[:, :], t8[:, :, :], AX.X, ALU.add))
                link(dve.tensor_scalar(spare[:, :], valid[:, :], 1.0, -1.0, ALU.subtract, ALU.mult))
                link(dve.tensor_scalar(t8[:, :, 0], node[:, :], float(SLOTS + j * NP), None, ALU.add))
                link(dve.tensor_tensor(spare[:, :], spare[:, :], t8[:, :, 0], ALU.mult))
                link(dve.tensor_tensor(k.slot[:, j, :], spare[:, :], pos[:, :], ALU.add))
            link(dve.tensor_scalar(bno[:, :], bno[:, :], float(NT), None, ALU.subtract))
            link(dve.tensor_tensor(cmp_[:, :, :], be[:, 1:X + 1].unsqueeze(1).broadcast_to([P, 2, X]),
                                   bno[:, :].unsqueeze(2).broadcast_to([P, 2, X]), ALU.is_le))
            link(dve.tensor_reduce(eb[:, :, 0], cmp_[:, :, :], AX.X, ALU.add))
            link(dve.tensor_scalar(eb[:, :, 0], eb[:, :, 0], float(X - 1), None, ALU.min))
            link(dve.tensor_scalar(bno[:, :], bno[:, :], 0.0, float(X), ALU.is_lt, ALU.mult))
            link(dve.tensor_tensor(ebi[:, :], eb[:, :, 0], bno[:, :], ALU.add))
            dve.sem_inc(v_s, 1)

        @block.tensor
        def _(pe):
            pe.wait_ge(v_s, 2)
            s2 = sel[:, :, :].rearrange("p t e -> p (t e)")
            nc.tensor.matmul(pr[:, 0:NT * X], k.upper[:, :], s2, start=True, stop=True)
            nc.tensor.matmul(pq[:, 0:NT * X], k.ones[:, :], s2, start=True, stop=True).then_inc(pe_s, 1)
    st.close()


def experts(k):
    nc, ins = k.nc, k.ins
    st = ExitStack()
    sb = lambda *a: k.sb(st, *a)
    XA = X + 1
    w1, w2, b1, b2, sh_in, all_in = k.w_up, k.w_down, k.b_up, k.b_down, k.shared_in, k.routed_in
    tabs = sb("block_row", [1, 2 * P], I32)
    idx, sidx, xg = sb("token_index", [P, 2, 1], I32), sb("sum_index", [P, 2, 1], I32), sb("tokens", [P, 2, D])
    RB = NB - NT
    rows_i, rows_f = sb("slot_rows", [P, BLK, 2]), sb("slot_rows_f", [P, 2, BLK])
    tokens, gates = sb("tokens_of_block", [P, RB], I32), sb("gates_of_block", [P, RB, 1])
    x2, yb = sb("x2_in", [P, 2, D]), sb("result_plus_bias", [P, 2, D])
    xt, hp, ht, y = (sb(n, [P, 2, w]) for n, w in (("tokensT", DK * P), ("hidden", F), ("hiddenT", FK * P), ("result", D)))
    HF = F // 2
    px, pw = k.ps(st, "pX", [P, 512]), k.ps(st, "pSlots", [P, 512])
    ph = [k.ps(st, f"pH{j}", [P, 512]) for j in range(2)]
    pg = [k.ps(st, f"pG{j}", [P, 512]) for j in range(2)]
    py = [k.ps(st, f"pY{j}", [P, 512]) for j in range(2)]
    x_in, x2_in, x_got, stored, added = ([k.sem(f"p8_{n}{b}") for b in range(2)] for n in (
        "tokens", "x2", "tokens_gathered", "stored", "added"))
    filled, tok_in, tok_s, tok_pe, x_own, own = (k.sem("p8_" + n) for n in (
        "slots_filled", "slot_rows", "slot_columns", "slots_turned", "index", "dve"))
    tab_in, tx, xt_s, up, hp_s, th, gl, dn, y_s = (k.sem("p8_" + n) for n in (
        "table", "turned", "tokensT", "up", "hidden", "hidden_turned", "gelu", "down", "result"))
    SLOTS_AT, FIRST = NT // 2 - 6, NT // 2 - 1
    assert NT % 2 == 1 and NB % 2 == 0

    def steps(eng, head, body, tail, slots=None, routed=None):
        head()

        def pairs(a, z):
            with eng.Fori(a, z) as i:
                for b in range(2):
                    body(2 * i + b, b, i)

        pairs(0, SLOTS_AT)
        if slots:
            slots()
        pairs(SLOTS_AT, FIRST)
        if routed:
            routed()
        for i in (FIRST, FIRST + 1):
            for b in range(2):
                body(2 * i + b, b, i)
        pairs(FIRST + 2, NB // 2 - 1)
        body(NB - 2, 0, NB // 2 - 1)
        tail()

    with nc.Block() as block:
        @block.sync
        def _(sp):
            sp.dma_start(tabs[:, :], k.block_d).then_inc(tab_in, 16)
            prime(k, sp, stored)

            def load(t, b, rows, i):
                sp.wait_ge(tx, freed(t))
                sp.dma_start(xg[:, b, :], k.x2n_d[ds(t * P, P), :]).then_inc(x_in[b], 16)

            def load_x2(t, b, rows, i):
                sp.wait_ge(y_s, freed(t))
                sp.dma_start(x2[:rows, b, :], k.x2_d[ds(t * P, rows), :]).then_inc(x2_in[b], 16)

            def store(t, b, rows, i):
                sp.wait_ge(y_s, done(t))
                sp.dma_start(k.acc_d[ds(t * P, rows), :], y[:rows, b, :]).then_inc(stored[b], 16)

            pipeline(sp, (0, load), (4, store), (2, load_x2))

        @block.gpsimd
        def _(pool):
            pool.sem_inc(x_own, CREDIT)
            prime(k, pool, added)
            for t in range(NT):
                for j in range(2):
                    pool.indirect_dma_start(k.token_d[:, :], IndexOn(ap=k.slot[:, j, t:t + 1], axis=0), k.choice[:, j, t, :], None).then_inc(filled, 16)
            pool.wait_ge(filled, 32 * NT)
            pool.dma_start(rows_i[0:RB, :, :].rearrange("p s o -> p (s o)"), k.token_d[0:SLOTS, :].rearrange("(b s) o -> b (s o)", s=BLK)).then_inc(tok_in, 16)
            pool.wait_ge(tok_s, 2)

            def gather(s, b):
                pool.wait_ge(tx, freed(s))
                pool.tensor_copy(idx[:, b, :], tokens[:, ds(s - NT, 1)]).then_inc(x_own, 1)
                pool.wait_ge(x_own, seen(s, 0))
                settle(pool, k.passed)
                pool.indirect_dma_start(xg[:, b, :], None, k.x2n_d[:, :], IndexOn(ap=idx[:, b, :], axis=0)).then_inc(x_got[b], 16)

            def add(s, b, i):
                pool.tensor_copy(sidx[:, b, :], tokens[:, ds(s - NT, 1)]).then_inc(x_own, 1)
                pool.wait_ge(x_own, seen(s + 4, 1))
                settle(pool, k.passed)
                pool.wait_ge(added[1 - b], 16 * (i - NT // 2 + 1))
                settle(pool, k.passed)
                pool.wait_ge(y_s, done(s))
                settle(pool, k.passed)
                pool.indirect_dma_start(k.acc_d[:, :], IndexOn(ap=sidx[:, b, :], axis=0), y[:, b, :], None,
                                        compute_op=ALU.add).then_inc(added[b], 16)

            def seen(s, adds):
                if isinstance(s, int):
                    return CREDIT + min(s - NT + 1, RB) + max(s - NT - 4 + adds, 0)
                return CREDIT + 2 * s - 2 * NT - 3 + adds

            for s in range(NT, NT + 5):
                gather(s, s % 2)
            for b in range(2):
                pool.wait_ge(stored[b], 16 * (NT // 2 + 2 - b))
            add(NT, 1, NT // 2)
            with pool.Fori((NT + 5) // 2, NB // 2) as i:
                for b in range(2):
                    gather(2 * i + b, b)
                    add(2 * i + b - 4, b, i - 2)
            for s in range(NB - 4, NB):
                add(s, s % 2, s // 2)
            for b in range(2):
                pool.wait_ge(added[b], 16 * (NB // 2 - NT // 2 + b))
            for a in range(0, N, OUT_ROWS):
                pool.dma_start(k.out[a:a + OUT_ROWS, :], k.acc_d[a:a + OUT_ROWS, :]).then_inc(tok_in, 16)
            pool.wait_ge(tok_in, 16 * (1 + N // OUT_ROWS))

        @block.vector
        def _(dve):
            def turn(s, b):
                dve.wait_ge(tx, done(s))
                dve.tensor_copy(xt[:, b, :], px[:, 0:DK * P]).then_inc(xt_s, 1)

            def hidden(s, b):
                dve.wait_ge(th, 2 * freed(s))
                for j in range(2):
                    dve.wait_ge(up, 2 * s + j + 1)
                    dve.tensor_copy(hp[:, b, j * HF:(j + 1) * HF], ph[j][:, :]).then_inc(hp_s, 1)

            def result(s, b, i, shared):
                e = dve.value_load(tabs[0:1, ds(s, 1)], min_val=0, max_val=X)
                dve.wait_ge(dn, done(s))
                Chain(dve, own, s)(dve.tensor_tensor(yb[:, b:b + 1, :], py[b][:, 0:D].unsqueeze(1), b2[:, ds(e, 1), :], ALU.add))
                if shared:
                    dve.wait_ge(stored[b], 16 * i + 16)
                    dve.wait_ge(x2_in[b], 16 * i + 16)
                    dve.tensor_tensor(y[:, b, :], yb[:, b, :], x2[:, b, :], ALU.add).then_inc(y_s, 1)
                else:
                    if isinstance(s, int) and s == NT:
                        for c in range(2):
                            dve.wait_ge(stored[c], 16 * (NT // 2 + 2 - c))
                    dve.wait_ge(added[b], 16 * (i - NT // 2 + b))
                    dve.tensor_tensor(y[:, b:b + 1, :], yb[:, b:b + 1, :], gates[:, ds(s - NT, 1), :].broadcast_to([P, 1, D]),
                                      ALU.mult).then_inc(y_s, 1)

            def head():
                dve.sem_inc(y_s, CREDIT)
                dve.wait_ge(sh_in, 64)
                dve.wait_ge(tab_in, 16)
                turn(0, 0)
                turn(1, 1)
                hidden(0, 0)

            def body(s, b, i):
                shared = s < NT if isinstance(s, int) else not phase
                if not (isinstance(s, int) and s == NB - 2):
                    turn(s + 2, b)
                hidden(s + 1, 1 - b)
                result(s, b, i, shared)

            phase = []

            def slots():
                dve.wait_ge(tok_in, 16)
                dve.tensor_copy(rows_f[0:RB, 0, :], rows_i[0:RB, :, 0].bitcast(I32))
                dve.tensor_copy(rows_f[0:RB, 1, :], rows_i[0:RB, :, 1]).then_inc(tok_s, 1)
                dve.wait_ge(tok_pe, 1)
                dve.tensor_copy(gates[:, :, 0], pw[:, P:P + RB])
                dve.tensor_copy(tokens[:, :], pw[:, 0:RB]).then_inc(tok_s, 1)

            def routed():
                phase.append("routed")
                dve.wait_ge(all_in, 64 * X)

            steps(dve, head, body, lambda: result(NB - 1, 1, NB // 2 - 1, False), slots, routed)

        @block.scalar
        def _(act):
            def gelu(s, b):
                e = act.value_load(tabs[0:1, ds(s, 1)], min_val=0, max_val=X)
                act.wait_ge(dn, freed(s))
                for c in range(FK):
                    if c % 4 == 0:
                        act.wait_ge(th, 2 * CREDIT + 2 * s + c // 4 + 1)
                    nc.scalar.activation(ht[:, b, c * P:(c + 1) * P], pg[c // 4][:, c % 4 * P:(c % 4 + 1) * P], ACT.Gelu,
                                         bias=b1[:, ds(e, 1), c]).then_inc(gl, 1)

            act.sem_inc(gl, FK)
            act.wait_ge(sh_in, 64)
            load_weights(k, act, range(X))
            act.wait_ge(tab_in, 16)
            steps(act, lambda: None, lambda s, b, i: gelu(s, b), lambda: gelu(NB - 1, 1),
                  routed=lambda: act.wait_ge(all_in, 64 * X))

        @block.tensor
        def _(pe):
            def turn(s, b, i, shared):
                if shared:
                    pe.wait_ge(x_in[b], 16 * i + 16)
                else:
                    pe.wait_ge(x_got[b], 16 * (i - NT // 2 + b))
                pe.wait_ge(xt_s, s)
                for c in range(DK):
                    last = nc.tensor.transpose(px[:, c * P:(c + 1) * P], xg[:, b, c * P:(c + 1) * P], k.ident[:, :])
                last.then_inc(tx, 1)

            def first_layer(s, b, e, j):
                pe.wait_ge(xt_s, s + 1)
                pe.wait_ge(hp_s, 2 * s)
                for c in range(DK):
                    last = nc.tensor.matmul(ph[j][:, :], xt[:, b, c * P:(c + 1) * P],
                                            w1[:, ds(e, 1), c, j * HF:(j + 1) * HF], start=c == 0, stop=c == DK - 1)
                last.then_inc(up, 1)

            def turn_hidden(s, b):
                pe.wait_ge(hp_s, 2 * s + 2)
                pe.wait_ge(gl, FK * s + FK)
                for c in range(FK):
                    last = nc.tensor.transpose(pg[c // 4][:, c % 4 * P:(c % 4 + 1) * P], hp[:, b, c * P:(c + 1) * P], k.ident[:, :])
                    if c % 4 == 3:
                        last.then_inc(th, 1)

            def second_layer(s, b, e):
                pe.wait_ge(y_s, freed(s))
                for c in range(FK):
                    pe.wait_ge(gl, FK * s + FK + c + 1)
                    last = nc.tensor.matmul(py[b][:, 0:D], ht[:, b, c * P:(c + 1) * P], w2[:, ds(e, 1), c, :],
                                            start=c == 0, stop=c == FK - 1)
                last.then_inc(dn, 1)

            def expert(s):
                return pe.value_load(tabs[0:1, ds(s, 1)], min_val=0, max_val=X)

            def head():
                pe.sem_inc(tx, CREDIT)
                pe.sem_inc(dn, CREDIT)
                pe.sem_inc(th, 2 * CREDIT)
                pe.wait_ge(sh_in, 64)
                pe.wait_ge(tab_in, 16)
                turn(0, 0, 0, True)
                turn(1, 1, 0, True)
                e = expert(0)
                first_layer(0, 0, e, 0)
                first_layer(0, 0, e, 1)

            def body(s, b, i):
                e0, e1 = expert(s), expert(s + 1)
                if not (isinstance(s, int) and s == NB - 2):
                    turn(s + 2, b, i + 1, s + 2 < NT if isinstance(s, int) else not phase)
                first_layer(s + 1, 1 - b, e1, 0)
                turn_hidden(s, b)
                first_layer(s + 1, 1 - b, e1, 1)
                second_layer(s, b, e0)

            def slots():
                pe.wait_ge(tok_s, 1)
                for c in range(2):
                    last = nc.tensor.transpose(pw[:, c * P:c * P + RB], rows_f[0:RB, c, :], k.ident[0:RB, 0:RB])
                last.then_inc(tok_pe, 1)

            phase = []

            def routed():
                phase.append("routed")
                pe.wait_ge(all_in, 64 * X)

            def tail():
                turn_hidden(NB - 1, 1)
                second_layer(NB - 1, 1, expert(NB - 1))

            steps(pe, head, body, tail, slots, routed)
    st.close()




def build(nc, ins, out):
    k = Kernel(nc, ins, out)
    k.outer = outer = ExitStack()
    sb = lambda *a: k.sb(outer, *a)
    k.ident, k.upper, k.ones, k.iota = (sb(n, [P, P]) for n in ("ident", "upper", "ones", "iota_row"))
    k.eps = sb("eps", [P, 1])
    k.elr = sb("el_er", [P, NT, 2 * H])
    k.cb = sb("update_bias", [P, D])
    k.w_lin = sb("w_lin", [P, DK, D])
    k.logits = sb("router_logits", [P, NT, X])
    k.choice, k.slot = sb("choices", [P, 2, NT, 2]), sb("slots_of_choices", [P, 2, NT], I32)
    wide, edges, nodes = ExitStack(), ExitStack(), ExitStack()
    k.w_feat, k.b_feat = k.sb(wide, "w_feat", [P, DK, D + 2 * H]), k.sb(wide, "b_feat", [P, D + 2 * H])
    k.xnT = k.sb(wide, "xnT", [P, DK, NP])
    k.count = k.sb(edges, "edges_of_node", [P, NT])
    k.el_e = k.sb(edges, "el_of_edge", [P, STRIP, H])
    k.dst_i = k.sb(edges, "dst_strips", [P, STRIP], I32)
    k.cont = k.sb(edges, "run_continues", [P, STRIP])
    k.xn = k.sb(nodes, "xn", [P, NT, D])
    prepare(k)
    project(k)
    collect(k)
    nodes.close()
    scan_max(k)
    scan_weights(k)
    edges.close()
    k.agg = k.sb(wide, "node_sums", [P, NT, GF])
    message(k)
    update(k)
    wide.close()
    k.w_up, k.w_down = sb("w_up", [P, X + 1, DK, F]), sb("w_down", [P, X + 1, FK, D])
    k.b_up, k.b_down = sb("b_up", [P, X + 1, FK]), sb("b_down_rows", [P, X + 1, D])
    k.shared_in, k.routed_in = k.sem("shared_weights_in"), k.sem("routed_weights_in")
    route(k)
    experts(k)
    outer.close()
    k.stack.close()


_INS = ['x', 'src', 'dst', 'L0_gnn_W_lin', 'L0_gnn_b_lin', 'L0_gnn_W_gat', 'L0_gnn_attn_l', 'L0_gnn_attn_r',
        'L0_gnn_gat_bias', 'L0_mix_W_qk', 'L0_mix_b_qk', 'L0_mix_W_v', 'L0_mix_b_v', 'L0_mix_gamma',
        'L0_mix_beta', 'L0_ffn_Wr', 'L0_ffn_W1s', 'L0_ffn_b1s', 'L0_ffn_W2s', 'L0_ffn_b2s', 'L0_ffn_W1p',
        'L0_ffn_b1p', 'L0_ffn_W2p', 'L0_ffn_b2p']


def kernel(**inputs):
    import numpy as _np
    import concourse.bacc as _bacc
    from concourse import mybir as _mybir
    from concourse.bass_utils import run_bass_kernel_spmd as _run

    nc = _bacc.Bacc("TRN2", target_bir_lowering=False, num_devices=1)
    arrays, ins = {}, {}
    for name in _INS:
        a = _np.ascontiguousarray(inputs[name])
        arrays[f"in_{name}"] = a
        ins[name] = nc.dram_tensor(f"in_{name}", a.shape, _mybir.dt.from_np(a.dtype), kind="ExternalInput").ap()
    out = nc.dram_tensor("out_0", (N, D), _mybir.dt.float32, kind="ExternalOutput").ap()
    build(nc, ins, out)
    r = _run(nc, [arrays], core_ids=[0])
    return r.results[0]["out_0"]
```

```python
from contextlib import ExitStack

import numpy as np

import concourse.bass as bass
from concourse import mybir

F32 = mybir.dt.float32
BF16 = mybir.dt.bfloat16
I32 = mybir.dt.int32
ALU = mybir.AluOpType
ACT = mybir.ActivationFunctionType
AX = mybir.AxisListType
ds = bass.ds
IndexOn = bass.IndirectOffsetOnAxis

P = 128
N, D = 6250, 256
E = 100000
H, HD = 8, 32
X, F = 8, 1024
DK = D // P
FK = F // P
NT = -(-N // P)
LAST = N - (NT - 1) * P
NP = NT * P
STRIP = -(-E // P)
ES = STRIP * P
EL_LAST = E - (P - 1) * STRIP
COLS = 17
STEPS = STRIP // COLS
assert STEPS * COLS == STRIP and STEPS % 2 == 0
GATHERED = 28
GJ = 2
GE = GJ * P
NG = E // GE + NT
NG += -NG % 8
TABLE = NG + -NG % P
EROWS = E + GE + P * 2
GF = D + H
CH = 512
BLK = P
NRB = (2 * N) // BLK + X
NB = NT + NRB
NB += NB % 2
SLOTS = (NB - NT) * BLK
CT = 12
X_LOADS = (NT - 1) // CT + 1
assert (NT - 1) % CT == 0
OUT_ROWS = N // 5
BIG = 1.0e30
EPS = 1.0e-5
PAD_DST = 8191
CREDIT = 2


def done(t):
    return t + 1 + CREDIT


def freed(t):
    return t + 1


def each_tile(eng):
    with eng.Fori(0, NT // 2) as i:
        for b in range(2):
            yield 2 * i + b, b, P, i
    yield NT - 1, 0, LAST, NT // 2


def pipeline(eng, *stages):
    most = max(lag for lag, _ in stages)

    def step(s, b, i):
        for lag, stage in stages:
            at = (b - lag) % 2
            if isinstance(s, int) and not 0 <= s - lag < NT:
                continue
            rows = LAST if isinstance(s, int) and s - lag == NT - 1 else P
            stage(s - lag, at, rows, i + (b - lag - at) // 2)

    head = most + most % 2
    for s in range(head):
        step(s, s % 2, s // 2)
    with eng.Fori(head // 2, NT // 2) as i:
        for b in range(2):
            step(2 * i + b, b, i)
    for s in range(NT - 1, NT + most):
        step(s, s % 2, s // 2)


def settle(eng, sem):
    eng.sem_inc(sem, 1)


def prime(k, queue, sems, n=1):
    for s in sems:
        for _ in range(n):
            queue.dma_start(k.scrap_d[k.scraps:k.scraps + 1, :], k.ones[0:1, 0:32]).then_inc(s, 16)
            k.scraps += 1


class Chain:

    def __init__(self, eng, sem, start=0):
        self.eng, self.sem, self.start, self.n = eng, sem, start, 0

    def __call__(self, ins):
        ins.then_inc(self.sem, 1)
        self.n += 1
        self.eng.wait_ge(self.sem, self.start + self.n)


class Kernel:
    def __init__(self, nc, ins, out):
        self.nc, self.ins, self.out = nc, ins, out
        self.stack = ExitStack()
        self.names = {}
        self.passed = self.stack.enter_context(nc.semaphore("waits_passed"))
        nc_ = nc
        d = lambda name, shape, dt=F32: nc_.dram_tensor(name, shape, dt).ap()
        self.feat_d = d("feat_rows", (N, D))
        self.el_d = d("el_rows", (N, H))
        self.fill_d = d("fill_rows", (ES + NP, H))
        self.edge_d = d("edge_rows", (EROWS, H + 2))
        self.table_d = d("group_table", (2, TABLE), I32)
        self.scrap_d, self.scraps = d("scrap_rows", (32, 32)), 0
        self.x2_d = d("x2_rows", (NP, D))
        self.x2n_d, self.acc_d = d("x2n_rows", (N + BLK, D)), d("sum_rows", (N + BLK, D))
        self.token_d = d("slot_tokens", (SLOTS + 2 * NP, 2))
        self.block_d = d("block_table", (1, 2 * P), I32)

    def sem(self, name):
        return self.stack.enter_context(self.nc.semaphore(name))

    def sb(self, stack, name, shape, dt=F32):
        return stack.enter_context(self.nc.sbuf_tensor(self.unique(name), shape, dt))

    def ps(self, stack, name, shape, dt=F32):
        return stack.enter_context(self.nc.psum_tensor(self.unique(name), shape, dt))

    def unique(self, name):
        self.names[name] = self.names.get(name, 0) + 1
        return name if self.names[name] == 1 else f"{name}_{self.names[name]}"


def prepare(k):
    nc, ins = k.nc, k.ins
    st = ExitStack()
    sb = lambda *a: k.sb(st, *a)
    w_gat = sb("w_gat", [P, DK, D])
    ext = sb("w_ext", [P, DK, D + 2 * H])
    attn = sb("attn_rows", [P, 2, D])
    prod = sb("attn_prod", [P, D])
    w_linT = sb("w_linT", [P, DK, D])
    blin_rep = sb("blin_rep", [P, DK, P])
    blin_col = sb("blin_col", [P, DK])
    idx = sb("idx", [P, P], I32)
    zeros, spare = sb("zeros", [P, 2048]), sb("spare_slots", [P, BLK, 2])
    ip = k.ps(st, "pT", [P, 2, 2, P])
    pw = k.ps(st, "pW", [P, 2, 512])
    pb = k.ps(st, "pB", [P, 512])
    s_ld, s_c, s_pe, s_cp, s_ch, s_z, s_g, s_ex, s_sp = (k.sem("p0_" + x) for x in (
        "load", "const", "pe", "copied", "dve", "zeros", "pool", "ext", "spare"))
    with nc.Block() as block:
        @block.sync
        def _(sp):
            w3 = lambda a: a.rearrange("(k p) n -> p k n", p=P)
            sp.dma_start(k.w_lin[:, :, :], w3(ins["L0_gnn_W_lin"])).then_inc(s_ld, 16)
            sp.dma_start(w_gat[:, :, :], w3(ins["L0_gnn_W_gat"])).then_inc(s_ld, 16)
            sp.dma_start(ext[:, :, 0:D], w3(ins["L0_gnn_W_gat"])).then_inc(s_ld, 16)
            for j, a in enumerate(("L0_gnn_attn_l", "L0_gnn_attn_r")):
                sp.dma_start(attn[:, j, :], ins[a].rearrange("h c -> (h c)").partition_broadcast(P)).then_inc(s_ld, 16)
            with nc.allow_non_contiguous_dma("a short bias column"):
                sp.dma_start(blin_col[:, :], ins["L0_gnn_b_lin"].rearrange("(k p) -> p k", p=P)).then_inc(s_ld, 16)
            load_x(k, sp)
            sp.wait_ge(s_ld, 96)
            sp.wait_ge(s_z, 1)
            fr = k.fill_d[0:ES, :].rearrange("(p c) h -> p (c h)", p=P)
            w = STRIP * H
            n = 0
            for a in range(0, w, 2048):
                m = min(2048, w - a)
                sp.dma_start(fr[:, a:a + m], zeros[:, 0:m]).then_inc(s_z, 16)
                n += 1
            sp.dma_start(k.x2n_d[N:N + BLK, :], zeros[:, 0:D]).then_inc(s_z, 16)
            sp.dma_start(k.acc_d[N:N + BLK, :], zeros[:, 0:D]).then_inc(s_z, 16)
            sp.wait_ge(s_sp, 1)
            sp.dma_start(k.token_d[0:SLOTS, :].rearrange("(b s) o -> b (s o)", s=BLK),
                         spare[0:SLOTS // BLK, :, :].rearrange("p s o -> p (s o)")).then_inc(s_z, 16)
            sp.wait_ge(s_z, 1 + 16 * (n + 3))

        @block.gpsimd
        def _(pool):
            link = Chain(pool, s_g)
            link(pool.memset(zeros[:, :], 0.0))
            pool.sem_inc(s_z, 1)
            link(pool.memset(k.ident[:, :], 0.0))
            link(pool.affine_select(out=k.ident[:, :], in_=k.ident[:, :], compare_op=ALU.not_equal, fill=1.0,
                                    base=0, pattern=[[-1, P]], channel_multiplier=1))
            link(pool.memset(k.upper[:, :], 1.0))
            link(pool.affine_select(out=k.upper[:, :], in_=k.upper[:, :], compare_op=ALU.is_gt, fill=0.0,
                                    base=0, pattern=[[1, P]], channel_multiplier=-1))
            link(pool.memset(k.ones[:, :], 1.0))
            link(pool.memset(k.eps[:, :], EPS))
            link(pool.iota(idx[:, :], [[1, P]], base=0, channel_multiplier=0))
            pool.tensor_copy(k.iota[:, :], idx[:, :]).then_inc(s_c, 1)
            link(pool.memset(spare[:, :, :], 0.0))
            pool.wait_ge(s_c, 1)
            link(pool.iota(idx[:, :], [[1, P]], base=N, channel_multiplier=0))
            pool.tensor_copy(spare[:, :, 0:1].bitcast(I32), idx[:, :].unsqueeze(2)).then_inc(s_sp, 1)

        @block.vector
        def _(dve):
            link = Chain(dve, s_ch)
            dve.wait_ge(s_ld, 96)
            for j in range(2):
                for c in range(DK):
                    link(dve.tensor_tensor(prod[:, :], w_gat[:, c, :], attn[:, j, :], ALU.mult))
                    link(dve.tensor_reduce(ext[:, c, D + j * H:D + (j + 1) * H],
                                           prod[:, :].rearrange("p (h c) -> p h c", h=H), AX.X, ALU.add))
            for c in range(DK):
                last = dve.tensor_copy(blin_rep[:, c, :], blin_col[:, c:c + 1].broadcast_to([P, P]))
            last.then_inc(s_ex, 1)
            dve.wait_ge(s_pe, 1)
            for c in range(DK):
                last = dve.tensor_copy(w_linT[:, c, :].rearrange("p (a b) -> p a b", a=2), ip[:, c, :, :])
            last.then_inc(s_cp, 1)
            dve.wait_ge(s_pe, 2)
            for m in range(2):
                link(dve.tensor_copy(k.w_feat[:, m, :], pw[:, m, 0:D + 2 * H]))
            link(dve.tensor_copy(k.b_feat[:, :], pb[:, 0:D + 2 * H]))

        @block.tensor
        def _(pe):
            pe.wait_ge(s_ld, 96)
            pe.wait_ge(s_c, 1)
            for m in range(2):
                for c in range(DK):
                    last = nc.tensor.transpose(ip[:, c, m, :], k.w_lin[:, m, c * P:(c + 1) * P], k.ident[:, :])
            last.then_inc(s_pe, 1)
            pe.wait_ge(s_cp, 1)
            pe.wait_ge(s_ex, 1)
            for m in range(2):
                for c in range(DK):
                    nc.tensor.matmul(pw[:, m, 0:D + 2 * H], w_linT[:, c, m * P:(m + 1) * P], ext[:, c, :],
                                     start=c == 0, stop=c == DK - 1)
            for c in range(DK):
                last = nc.tensor.matmul(pb[:, 0:D + 2 * H], blin_rep[:, c, :], ext[:, c, :],
                                        start=c == 0, stop=c == DK - 1)
            last.then_inc(s_pe, 1)
    st.close()


def load_x(k, queue):
    x = k.ins["x"]
    for j in range(X_LOADS):
        if j * CT < NT - 1:
            a = j * CT * P
            queue.dma_start(k.xn[:, j * CT:(j + 1) * CT, :],
                            x[a:a + CT * P, :].rearrange("(t p) d -> p t d", p=P)).then_inc(k.x_in, 16)
        else:
            queue.dma_start(k.xn[0:LAST, NT - 1, :], x[(NT - 1) * P:N, :]).then_inc(k.x_in, 16)


def project(k):
    nc, ins = k.nc, k.ins
    st = ExitStack()
    sb = lambda *a: k.sb(st, *a)
    xn, fs = sb("xn_stage", [P, 2, D]), sb("feat_stage", [P, 2, D + 2 * H])
    stats, mv, sd, rs = (sb(n, [P, 2, w]) for n, w in (("stats", 6), ("mv", 2), ("sd", 1), ("rs", 1)))
    xt = sb("xT_stage", [P, 2, DK, P])
    pt = [k.ps(st, f"pT{b}", [P, 512]) for b in range(2)]
    pf = [k.ps(st, f"pF{b}", [P, 512]) for b in range(2)]
    stored = [k.sem(f"p1_stored{b}") for b in range(2)]
    (mv_done, sd_done, xn_done, keep_done, tr_done, xt_done, xtk_done, feat_done, fs_done, er_done, own, own_r, z) = (
        k.sem("p1_" + n) for n in ("mv", "sd", "xn", "xn_kept", "transposed", "xT", "xT_kept", "feat", "fs",
                                   "er", "dve", "dve_rs", "zero"))
    with nc.Block() as block:
        @block.sync
        def _(sp):
            prime(k, sp, stored, 2)

            def store(t, b, rows, i):
                sp.wait_ge(fs_done, done(t))
                sp.dma_start(k.feat_d[ds(t * P, rows), :], fs[:rows, b, 0:D]).then_inc(stored[b], 16)
                sp.dma_start(k.el_d[ds(t * P, rows), :], fs[:rows, b, D:D + H]).then_inc(stored[b], 16)

            pipeline(sp, (0, store))
            for b in range(2):
                sp.wait_ge(stored[b], 32 * (NT // 2 + 2 - b))

        @block.gpsimd
        def _(pool):
            pool.sem_inc(keep_done, CREDIT)
            pool.memset(k.elr[:, :, :], 0.0).then_inc(z, 1)

            def keep(t, b, rows, i):
                pool.wait_ge(xn_done, done(t))
                pool.tensor_copy(k.xn[:rows, ds(t, 1), :], xn[:rows, b:b + 1, :]).then_inc(keep_done, 1)

            pipeline(pool, (0, keep))

        @block.vector
        def _(dve):
            dve.sem_inc(xn_done, CREDIT)
            dve.sem_inc(fs_done, CREDIT)

            def moments(t, b, rows, i):
                Chain(dve, own, t)(dve.bn_stats(stats[:rows, b, :], k.xn[:rows, ds(t, 1), :].rearrange("p a d -> p (a d)")))
                settle(dve, k.passed)
                dve.bn_aggr(mv[:rows, b, :], stats[:rows, b, :]).then_inc(mv_done, 1)

            def normalise(t, b, rows, i):
                dve.wait_ge(sd_done, t + 1)
                Chain(dve, own_r, t)(dve.reciprocal(rs[:rows, b, :], sd[:rows, b, :]))
                dve.wait_ge(keep_done, freed(t))
                dve.wait_ge(tr_done, freed(t))
                dve.tensor_scalar(xn[:rows, b:b + 1, :], k.xn[:rows, ds(t, 1), :], mv[:rows, b, 0:1], rs[:rows, b, :],
                                  ALU.subtract, ALU.mult).then_inc(xn_done, 1)

            def features(t, b, rows, i):
                dve.wait_ge(feat_done, done(t))
                dve.wait_ge(stored[b], 32 * i + 32)
                dve.wait_ge(er_done, freed(t))
                dve.tensor_tensor(fs[:rows, b, :], pf[b][:rows, 0:D + 2 * H], k.b_feat[:rows, :],
                                  ALU.add).then_inc(fs_done, 1)

            dve.wait_ge(k.x_in, 16 * X_LOADS)
            pipeline(dve, (0, moments), (3, features), (1, normalise))

        @block.scalar
        def _(act):
            act.sem_inc(xt_done, CREDIT)
            act.sem_inc(xtk_done, CREDIT)
            act.sem_inc(er_done, CREDIT)
            act.wait_ge(z, 1)

            def deviation(t, b, rows, i):
                act.wait_ge(mv_done, t + 1)
                nc.scalar.activation(sd[:rows, b, :], mv[:rows, b, 1:2], ACT.Sqrt,
                                     bias=k.eps[:rows, :]).then_inc(sd_done, 1)

            def turned(t, b, rows, i):
                act.wait_ge(tr_done, done(t))
                act.wait_ge(feat_done, freed(t))
                src = pt[b][:, 0:DK * P].rearrange("p (k n) -> p k n", k=DK)[:, :, 0:rows]
                nc.scalar.activation(xt[:, b, :, 0:rows], src, ACT.Copy).then_inc(xt_done, 1)
                nc.scalar.activation(k.xnT[:, :, ds(t * P, rows)], src, ACT.Copy).then_inc(xtk_done, 1)

            def keep_er(t, b, rows, i):
                act.wait_ge(fs_done, done(t))
                nc.scalar.activation(k.elr[:rows, ds(t, 1), :], fs[:rows, b:b + 1, D:D + 2 * H],
                                     ACT.Copy).then_inc(er_done, 1)

            pipeline(act, (0, deviation), (2, turned), (4, keep_er))

        @block.tensor
        def _(pe):
            pe.sem_inc(tr_done, CREDIT)
            pe.sem_inc(feat_done, CREDIT)

            def turn(t, b, rows, i):
                pe.wait_ge(xn_done, done(t))
                pe.wait_ge(xtk_done, freed(t))
                for c in range(DK):
                    last = nc.tensor.transpose(pt[b][:, c * P:c * P + rows], xn[:rows, b, c * P:(c + 1) * P],
                                               k.ident[:rows, :rows])
                last.then_inc(tr_done, 1)

            def product(t, b, rows, i):
                pe.wait_ge(xt_done, done(t))
                pe.wait_ge(fs_done, freed(t))
                for c in range(DK):
                    last = nc.tensor.matmul(pf[b][:rows, 0:D + 2 * H], xt[:, b, c, 0:rows], k.w_feat[:, c, :],
                                            start=c == 0, stop=c == DK - 1)
                last.then_inc(feat_done, 1)

            pipeline(pe, (1, product), (0, turn))
    st.close()


def collect(k):
    nc, ins = k.nc, k.ins
    st = ExitStack()
    sb = lambda *a: k.sb(st, *a)
    src = sb("src_strips", [P, STRIP], I32)
    idx, got = sb("gather_index", [P, 2, COLS], I32), sb("gathered_el", [P, 2, COLS, H])
    dst_i, lo_i = sb("dst_int", [P, STRIP], I32), sb("dst_part", [P, STRIP], I32)
    lo, hi, iotab = sb("dst_lo", [P, NT * COLS], BF16), sb("dst_hi", [P, NT * COLS], BF16), sb("iota_bf16", [P, P], BF16)
    oh_lo, oh_hi = sb("onehot_lo", [P, 2, COLS, P], BF16), sb("onehot_hi", [P, 2, COLS, NT], BF16)
    wk, wq, wv = (sb(n, [P, DK, D]) for n in ("w_k", "w_q", "w_v"))
    cols = sb("mix_columns", [P, 4, DK])
    bv, blin = sb("b_v_rows", [P, D]), sb("b_lin_rows", [P, D])
    NC = -(-N // CH)
    kmax = sb("key_max_chunks", [P, DK, NC])
    nb = sb("exp_bias", [P, 3, DK])
    es = sb("expT_stage", [P, 2, DK, P])
    e2 = sb("exp_stage", [P, 2, D])
    pn, pnT, lam, bn, wqT = (sb(n, [P, DK, D]) for n in ("pool_mean", "pool_meanT", "lam", "bn", "w_qT"))
    rden, stats, mv, rg = (sb(n, [P, DK, w]) for n, w in (("rden", 1), ("lam_stats", 6), ("lam_mv", 2), ("lam_rg", 2)))
    bq_rep = sb("b_q_rep", [P, DK, P])
    zf, zb = sb("zero_f32", [P, 512]), sb("zero_bf16", [P, P], BF16)
    pk = [k.ps(st, f"pK{b}", [P, 512]) for b in range(2)]
    pe_ = [k.ps(st, f"pE{b}", [P, 512]) for b in range(2)]
    pp = [k.ps(st, f"pP{b}", [P, 512]) for b in range(2)]
    ph = k.ps(st, "pHist", [P, 512])
    px = k.ps(st, "pX", [P, 512])
    g_land = [k.sem(f"p2_gathered{b}") for b in range(2)]
    (ld, pad, z, kt_mm, key_done, kt_mx, nb_s, exp_done, et_done, e2_done, acc_done, oh_done, hist_mm, kept, own, own_p,
     own_a, tail_pe, tail_v, idx_done, sd_s) = (
        k.sem("p2_" + n) for n in ("loaded", "padded", "zeros", "keys", "keys_again", "keys_max", "bias", "exp",
                                   "exp_transposed", "exp_staged", "accumulated", "onehots", "histogram", "el_kept",
                                   "dve", "pool", "act", "tail_pe", "tail_dve", "index", "lam_sd"))

    OS, W = STEPS - GATHERED, ((0, 6), (6, 6), (12, 5))
    assert sum(w for _, w in W) == COLS and OS % 2 == 0 and GATHERED % 2 == 0
    OC, HT = OS * COLS, H * NT
    slo_i, slo, shi = lo_i[:, 0:OC], lo[:, 0:OC + COLS], hi[:, 0:OC + COLS]
    tab, rest, part = sb("el_parts", [P, 3, H, NT], BF16), sb("el_rest", [P, H, NT]), zf[:, 0:HT].rearrange("p (h t) -> p h t", h=H)
    m49, mask, identb = sb("tile_mask", [NT, NT]), sb("mask", [NT, H, NT], BF16), sb("ident_bf16", [P, P], BF16)
    loT, hiT = sb("lo_turned", [P, 2, 6, P], BF16), sb("hi_turned", [NT, 2, 6, P], BF16)
    picked = e2[:, :, 0:COLS * H].rearrange("p b (c h) -> p b c h", c=COLS)
    o_start, o_hot, o_tr, o_ev, o_mm, o_red, o_kept, m_s = (k.sem("p2o_" + n) for n in (
        "start", "onehots", "turned", "staged", "products", "picked", "kept", "mask"))

    def turned(bank, rows, w):
        return bank[0:rows, :].bitcast(BF16)[:, 0:w * P].rearrange("p (j n) -> p j n", j=w)

    def bank(b, c):
        order = [(c2 + b2) % 4 for b2 in (b, 1 - b, b) for c2 in range(COLS)]
        at = 2 * COLS + c
        return (*pp, ph, px)[order[at]], next(d for d in range(1, at) if order[at - d] == order[at])

    def batches(eng, body):
        with eng.Fori(0, OS // 2) as i:
            for b in range(2):
                for q in range(3):
                    g = 2 * i + b
                    body(g, b, q, 3 * g + q, (3 * b + q) % 2)

    def chunks(eng):
        with eng.Fori(0, NC - 1) as c:
            yield c, CH
        yield NC - 1, N - (NC - 1) * CH

    with nc.Block() as block:
        @block.sync
        def _(sp):
            w3 = lambda a: a.rearrange("(k p) n -> p k n", p=P)
            sp.dma_start(wk[:, :, :], w3(ins["L0_mix_W_qk"][1])).then_inc(ld, 16)
            sp.dma_start(wq[:, :, :], w3(ins["L0_mix_W_qk"][0])).then_inc(ld, 16)
            sp.dma_start(wv[:, :, :], w3(ins["L0_mix_W_v"])).then_inc(ld, 16)
            with nc.allow_non_contiguous_dma("short bias columns"):
                for j, a in enumerate((ins["L0_mix_b_qk"][0], ins["L0_mix_b_qk"][1], ins["L0_mix_gamma"],
                                       ins["L0_mix_beta"])):
                    sp.dma_start(cols[:, j, :], a.rearrange("(k p) -> p k", p=P)).then_inc(ld, 16)
            sp.dma_start(bv[:, :], ins["L0_mix_b_v"].partition_broadcast(P)).then_inc(ld, 16)
            sp.dma_start(blin[:, :], ins["L0_gnn_b_lin"].partition_broadcast(P)).then_inc(ld, 16)
            sp.wait_ge(pad, 2)
            sp.dma_start(dst_i[0:P - 1, :], ins["dst"][0:(P - 1) * STRIP].rearrange("(p c) -> p c", c=STRIP)).then_inc(ld, 16)
            sp.dma_start(dst_i[P - 1:P, 0:EL_LAST], ins["dst"][(P - 1) * STRIP:E].rearrange("(p c) -> p c", p=1)).then_inc(ld, 16)

        @block.gpsimd
        def _(pool):
            link = Chain(pool, own_p)
            link(pool.memset(src[:, :], 0))
            pool.sem_inc(pad, 1)
            pool.memset(m49[:, :], -BIG).then_inc(m_s, 1)
            pool.wait_ge(m_s, 1)
            pool.affine_select(out=m49[:, :], in_=m49[:, :], compare_op=ALU.not_equal, fill=0.0,
                               base=0, pattern=[[-1, NT]], channel_multiplier=1).then_inc(m_s, 1)
            pool.dma_start(src[0:P - 1, :], ins["src"][0:(P - 1) * STRIP].rearrange("(p c) -> p c", c=STRIP)).then_inc(idx_done, 16)
            pool.dma_start(src[P - 1:P, 0:EL_LAST], ins["src"][(P - 1) * STRIP:E].rearrange("(p c) -> p c", p=1)).then_inc(idx_done, 16)
            pool.wait_ge(idx_done, 32)

            def gathers(s, b):
                pool.tensor_copy(idx[:, b, :], src[:, ds(s * COLS, COLS)]).then_inc(own_p, 1)
                pool.wait_ge(own_p, s + 2)
                settle(pool, k.passed)
                for c in range(COLS):
                    pool.indirect_dma_start(got[:, b, c, :], None, k.el_d[:, :],
                                            IndexOn(ap=idx[:, b, c:c + 1], axis=0)).then_inc(g_land[b], 16)

            def keep(s, b, n):
                pool.wait_ge(g_land[b], 16 * COLS * n)
                pool.tensor_copy(k.el_e[:, ds(s * COLS, COLS), :], got[:, b, :, :]).then_inc(kept, 1)
                pool.wait_ge(kept, s + 1)

            for b in range(2):
                gathers(b, b)
            with pool.Fori(1, GATHERED // 2) as i:
                for b in range(2):
                    keep(2 * i + b - 2, b, i)
                    gathers(2 * i + b, b)
            for b in range(2):
                keep(GATHERED - 2 + b, b, GATHERED // 2)

        @block.vector
        def _(dve):
            link = Chain(dve, own)
            link(dve.memset(dst_i[:, :], PAD_DST))
            dve.sem_inc(pad, 1)
            link(dve.memset(zf[:, :], 0.0))
            link(dve.memset(zb[:, :], 0.0))
            dve.sem_inc(z, 1)
            dve.wait_ge(ld, 16 * 11)
            link(dve.tensor_copy(iotab[:, :], k.iota[:, :]))
            link(dve.tensor_single_scalar(lo_i[:, :], dst_i[:, :], P - 1, ALU.bitwise_and))
            link(dve.memset(lo[:, STRIP:NT * COLS], 0.0))
            link(dve.memset(hi[:, STRIP:NT * COLS], float(PAD_DST >> 7)))
            link(dve.tensor_copy(lo[:, 0:STRIP], lo_i[:, :]))
            link(dve.tensor_single_scalar(lo_i[:, :], dst_i[:, :], 7, ALU.logical_shift_right))
            link(dve.tensor_copy(hi[:, 0:STRIP], lo_i[:, :]))
            for c in range(DK):
                link(dve.tensor_copy(bq_rep[:, c, :], cols[:, 0, c:c + 1].broadcast_to([P, P])))
            dve.sem_inc(kt_mx, 1)
            for c, w in chunks(dve):
                dve.wait_ge(kt_mm, c + 1)
                for m in range(DK):
                    last = dve.reduce_max(kmax[:, m, ds(c, 1)], pk[m][:, 0:w], AX.X)
                last.then_inc(kt_mx, 1)
            dve.wait_ge(kt_mx, NC + 1)
            for m in range(DK):
                link(dve.reduce_max(nb[:, 0, m:m + 1], kmax[:, m, :], AX.X))
            link(dve.tensor_tensor(nb[:, 1, :], nb[:, 0, :], cols[:, 1, :], ALU.add))
            dve.tensor_tensor(nb[:, 2, :], cols[:, 1, :], nb[:, 1, :], ALU.subtract).then_inc(nb_s, 1)
            dve.sem_inc(e2_done, CREDIT)
            dve.sem_inc(oh_done, CREDIT)

            def stage_exp(t, b, rows, i):
                dve.wait_ge(et_done, done(t))
                dve.wait_ge(acc_done, freed(t))
                dve.tensor_copy(e2[:rows, b, :], pe_[b][:rows, 0:D]).then_inc(e2_done, 1)

            def dst_onehots(s, b, rows, i):
                dve.wait_ge(hist_mm, freed(s))
                dve.tensor_tensor(oh_lo[:, b, :, :], iotab[:, :].unsqueeze(1).broadcast_to([P, COLS, P]),
                                  lo[:, ds(s * COLS, COLS)].unsqueeze(2).broadcast_to([P, COLS, P]), ALU.is_equal)
                dve.tensor_tensor(oh_hi[:, b, :, :], iotab[:, 0:NT].unsqueeze(1).broadcast_to([P, COLS, NT]),
                                  hi[:, ds(s * COLS, COLS)].unsqueeze(2).broadcast_to([P, COLS, NT]),
                                  ALU.is_equal).then_inc(oh_done, 1)

            pipeline(dve, (0, dst_onehots), (0, stage_exp))
            dve.wait_ge(hist_mm, done(NT))
            link(dve.tensor_copy(k.count[:, :], ph[:, 0:NT]))
            dve.wait_ge(tail_pe, 1)
            for m in range(DK):
                link(dve.reciprocal(rden[:, m, :], pp[m][:, D:D + 1]))
                link(dve.tensor_scalar(pn[:, m, :], pp[m][:, 0:D], rden[:, m, :], None, ALU.mult))
            dve.sem_inc(tail_v, 1)
            dve.wait_ge(tail_pe, 2)
            for m in range(DK):
                link(dve.tensor_copy(pnT[:, :, m * P:(m + 1) * P], pk[m][:, 0:D].rearrange("p (c n) -> p c n", c=DK)))
                link(dve.tensor_copy(wqT[:, :, m * P:(m + 1) * P], pe_[m][:, 0:D].rearrange("p (c n) -> p c n", c=DK)))
            dve.sem_inc(tail_v, 1)
            dve.wait_ge(tail_pe, 3)
            for m in range(DK):
                link(dve.tensor_tensor(lam[:, m, :], pp[m][:, 0:D], bv[:, :], ALU.add))
                link(dve.bn_stats(stats[:, m, :], lam[:, m, :]))
                link(dve.bn_aggr(mv[:, m, :], stats[:, m, :]))
            dve.sem_inc(tail_v, 1)
            dve.wait_ge(sd_s, 1)
            for m in range(DK):
                link(dve.reciprocal(rg[:, m, 1:2], rg[:, m, 0:1]))
                link(dve.tensor_scalar(bn[:, m, :], lam[:, m, :], mv[:, m, 0:1], rg[:, m, 1:2], ALU.subtract, ALU.mult))
                link(dve.tensor_scalar(bn[:, m, :], bn[:, m, :], cols[:, 2, m:m + 1], cols[:, 3, m:m + 1],
                                       ALU.mult, ALU.add))
            dve.sem_inc(tail_v, 1)
            dve.wait_ge(tail_pe, 4)
            for m in range(DK):
                link(dve.tensor_tensor(k.w_lin[:, m, :], pk[m][:, 0:D], k.w_lin[:, m, :], ALU.add))
            link(dve.tensor_tensor(k.cb[:, :], px[:, 0:D], blin[:, :], ALU.add))
            dve.wait_ge(idx_done, 32)
            dve.wait_ge(m_s, 2)
            src_o = src[:, GATHERED * COLS:STRIP]
            link(dve.tensor_single_scalar(slo_i[:, :], src_o, P - 1, ALU.bitwise_and))
            link(dve.memset(slo[:, OC:OC + COLS], 0.0))
            link(dve.memset(shi[:, OC:OC + COLS], 0.0))
            link(dve.tensor_copy(slo[:, 0:OC], slo_i[:, :]))
            link(dve.tensor_single_scalar(slo_i[:, :], src_o, 7, ALU.logical_shift_right))
            link(dve.tensor_copy(shi[:, 0:OC], slo_i[:, :]))
            link(dve.tensor_copy(identb[:, :], k.ident[:, :]))
            link(dve.tensor_copy(mask[:, :, :], m49[:, :].unsqueeze(1).broadcast_to([NT, H, NT])))
            link(dve.tensor_copy(rest[:, :, :], k.elr[:, :, 0:H].rearrange("p t h -> p h t")))
            for j in range(3):
                link(dve.tensor_copy(tab[:, j, :, :], rest[:, :, :]))
                if j < 2:
                    link(dve.tensor_copy(part[:, :, :], tab[:, j, :, :]))
                    link(dve.tensor_tensor(rest[:, :, :], rest[:, :, :], part[:, :, :], ALU.subtract))
            dve.sem_inc(o_start, 1)
            dve.sem_inc(o_red, 5)
            dve.sem_inc(o_kept, 2)

            def onehots(g, b, q, n):
                a, w = W[q]
                dve.wait_ge(o_tr, n + 1)
                dve.tensor_tensor(oh_lo[:, b, a:a + w, :], iotab[:, :].unsqueeze(1).broadcast_to([P, w, P]),
                                  slo[:, ds(g * COLS + a, w)].unsqueeze(2).broadcast_to([P, w, P]), ALU.is_equal)
                dve.tensor_tensor(oh_hi[:, b, a:a + w, :], iotab[:, 0:NT].unsqueeze(1).broadcast_to([P, w, NT]),
                                  shi[:, ds(g * COLS + a, w)].unsqueeze(2).broadcast_to([P, w, NT]),
                                  ALU.is_equal).then_inc(o_hot, 1)

            def pick(g, b, q):
                a, w = W[q]
                if q == 0:
                    dve.wait_ge(o_kept, g + 1)
                for c in range(a, a + w):
                    m = COLS * g + c
                    dve.wait_ge(o_mm, m + 1 + COLS)
                    dve.reduce_max(picked[:, b, c, :], bank(b, c)[0][:, 0:HT].rearrange("p (h t) -> p h t", h=H),
                                   AX.X).then_inc(o_red, 1)
                if q == 2:
                    dve.wait_ge(o_red, COLS * g + COLS + 5)
                    dve.tensor_copy(k.el_e[:, ds((g + GATHERED) * COLS, COLS), :], picked[:, b, :, :]).then_inc(o_kept, 1)

            def dve_batch(g, b, q, n, _):
                onehots(g + 1, 1 - b, q, n + 3)
                pick(g, b, q)

            for q in range(3):
                onehots(0, 0, q, q)
            batches(dve, dve_batch)
            dve.wait_ge(o_kept, OS + 2)

        @block.scalar
        def _(act):
            act.sem_inc(exp_done, CREDIT)
            act.wait_ge(nb_s, 1)
            for t, b, rows, i in each_tile(act):
                act.wait_ge(key_done, done(t))
                act.wait_ge(et_done, freed(t))
                for m in range(DK):
                    last = nc.scalar.activation(es[:, b, m, 0:rows], pk[b][:, m * P:m * P + rows], ACT.Exp,
                                                bias=nb[:, 2, m:m + 1])
                last.then_inc(exp_done, 1)
            act.wait_ge(tail_v, 3)
            for m in range(DK):
                last = nc.scalar.activation(rg[:, m, 0:1], mv[:, m, 1:2], ACT.Sqrt, bias=k.eps[:, :])
            last.then_inc(sd_s, 1)
            act.sem_inc(o_ev, 2)

            def stage(g, b, q, n, x):
                a, w = W[q]
                act.wait_ge(o_tr, n + 7)
                act.wait_ge(o_mm, COLS * g + (12, COLS, COLS + 6)[q])
                nc.scalar.activation(loT[:, x, 0:w, :], turned(pk[x], P, w), ACT.Copy)
                nc.scalar.activation(hiT[:, x, 0:w, :], turned(pe_[x], NT, w), ACT.Copy).then_inc(o_ev, 1)

            batches(act, stage)

        @block.tensor
        def _(pe):
            pe.wait_ge(ld, 16 * 11)
            pe.wait_ge(z, 1)
            for c, w in chunks(pe):
                pe.wait_ge(kt_mx, c + 1)
                for m in range(DK):
                    for q in range(DK):
                        last = nc.tensor.matmul(pk[m][:, 0:w], wk[:, q, m * P:(m + 1) * P],
                                                k.xnT[:, q, ds(c * CH, w)], start=q == 0, stop=q == DK - 1)
                last.then_inc(kt_mm, 1)
            pe.wait_ge(kt_mx, NC + 1)
            pe.sem_inc(key_done, CREDIT)
            pe.sem_inc(et_done, CREDIT)
            pe.sem_inc(acc_done, CREDIT)
            for m in range(DK):
                nc.tensor.matmul(pp[m][:, 0:D + 1], zf[:, 0:P], zf[:, 0:D + 1], start=True, stop=False)
            nc.tensor.matmul(ph[:, 0:NT], zb[:, :], zb[:, 0:NT], start=True, stop=False)

            def key(t, b, rows, i):
                pe.wait_ge(exp_done, freed(t))
                for m in range(DK):
                    for q in range(DK):
                        last = nc.tensor.matmul(pk[b][:, m * P:m * P + rows], wk[:, q, m * P:(m + 1) * P],
                                                k.xnT[:, q, ds(t * P, rows)], start=q == 0, stop=q == DK - 1)
                last.then_inc(key_done, 1)

            def turn(t, b, rows, i):
                pe.wait_ge(exp_done, done(t))
                pe.wait_ge(e2_done, freed(t))
                for m in range(DK):
                    last = nc.tensor.transpose(pe_[b][:rows, m * P:(m + 1) * P], es[:, b, m, 0:rows], k.ident[:, :])
                last.then_inc(et_done, 1)

            def accumulate(t, b, rows, i):
                pe.wait_ge(e2_done, done(t))
                for m in range(DK):
                    nc.tensor.matmul(pp[m][:, 0:D], e2[:rows, b, m * P:(m + 1) * P], k.xn[:rows, ds(t, 1), :],
                                     start=False, stop=False)
                    last = nc.tensor.matmul(pp[m][:, D:D + 1], e2[:rows, b, m * P:(m + 1) * P], k.ones[:rows, 0:1],
                                            start=False, stop=False)
                last.then_inc(acc_done, 1)

            def count_dst(s, b, rows, i):
                pe.wait_ge(oh_done, done(s))
                for c in range(COLS):
                    last = nc.tensor.matmul(ph[:, 0:NT], oh_lo[:, b, c, :], oh_hi[:, b, c, :], start=False, stop=False)
                last.then_inc(hist_mm, 1)

            pe.sem_inc(hist_mm, CREDIT)
            pipeline(pe, (0, key), (1, turn), (2, accumulate), (2, count_dst))
            for m in range(DK):
                last = nc.tensor.matmul(pp[m][:, 0:D + 1], zf[:, 0:P], zf[:, 0:D + 1], start=False, stop=True)
            last.then_inc(tail_pe, 1)
            nc.tensor.matmul(ph[:, 0:NT], zb[:, :], zb[:, 0:NT], start=False, stop=True).then_inc(hist_mm, 1)
            pe.wait_ge(tail_v, 1)
            for m in range(DK):
                for c in range(DK):
                    nc.tensor.transpose(pk[m][:, c * P:(c + 1) * P], pn[:, m, c * P:(c + 1) * P], k.ident[:, :])
                    last = nc.tensor.transpose(pe_[m][:, c * P:(c + 1) * P], wq[:, m, c * P:(c + 1) * P], k.ident[:, :])
            last.then_inc(tail_pe, 1)
            pe.wait_ge(tail_v, 2)
            for m in range(DK):
                for c in range(DK):
                    last = nc.tensor.matmul(pp[m][:, 0:D], pnT[:, c, m * P:(m + 1) * P], wv[:, c, :],
                                            start=c == 0, stop=c == DK - 1)
            last.then_inc(tail_pe, 1)
            pe.wait_ge(tail_v, 4)
            for m in range(DK):
                for c in range(DK):
                    nc.tensor.matmul(pk[m][:, 0:D], wqT[:, c, m * P:(m + 1) * P], bn[:, c, :],
                                     start=c == 0, stop=c == DK - 1)
            for c in range(DK):
                last = nc.tensor.matmul(px[:, 0:D], bq_rep[:, c, :], bn[:, c, :], start=c == 0, stop=c == DK - 1)
            last.then_inc(tail_pe, 1)
            pe.sem_inc(o_tr, 6)
            pe.sem_inc(o_mm, COLS)
            pe.wait_ge(o_start, 1)

            def turn_hots(b, q, n, x):
                a, w = W[q]
                pe.wait_ge(o_hot, n + 1)
                pe.wait_ge(o_ev, n + 1)
                for j in range(w):
                    nc.tensor.transpose(turned(pk[x], P, w)[:, j, :], oh_lo[:, b, a + j, :], identb[:, :])
                    last = nc.tensor.transpose(turned(pe_[x], NT, w)[:, j, :], oh_hi[:, b, a + j, :], identb[:, :])
                last.then_inc(o_tr, 1)

            def products(g, b, q, n, x):
                a, w = W[q]
                if q < 2:
                    turn_hots(b, q + 1, n + 1, 1 - x)
                else:
                    turn_hots(1 - b, 0, n + 1, 1 - x)
                pe.wait_ge(o_ev, n + 3)
                for c in range(a, a + w):
                    m = COLS * g + c
                    out, ago = bank(b, c)
                    out = out[:, 0:HT]
                    pe.wait_ge(o_red, m + 6 - ago)
                    for j in range(3):
                        nc.tensor.matmul(out, loT[:, x, c - a, :], tab[:, j, :, :].rearrange("p h t -> p (h t)"),
                                         start=j == 0, stop=False)
                    nc.tensor.matmul(out, hiT[:, x, c - a, :], mask[:, :, :].rearrange("p h t -> p (h t)"),
                                     start=False, stop=True).then_inc(o_mm, 1)

            turn_hots(0, 0, 0, 0)
            batches(pe, products)
    st.close()


def scan(k):
    nc, ins = k.nc, k.ins
    st = ExitStack()
    sb = lambda *a: k.sb(st, *a)
    R = H + 2
    prev, src = sb("dst_before", [P, STRIP], I32), sb("src_strips", [P, STRIP], I32)
    neg, negr, pcont, zero = (sb(n, [P, STRIP]) for n in ("run_starts", "run_ends_reversed", "run_from_before", "zero_strip"))
    run, fl = sb("running_max", [P, STRIP, H]), sb("er_of_edge", [P, STRIP, H])
    rec = sb("records", [P, STRIP, R])
    rev = rec[:, :, 0:H]
    tail = sb("tail_records", [P, (EROWS - E) // P, R])
    flip = sb("flip", [P, P])
    carry = [[sb(f"{n}{j}", s) for n, s in (("strip", [P, 2 * H]), ("stripT", [H, P]), ("lastT", [H, P]),
                                            ("carryT", [H, P + 1]), ("carry", [P, H]))] for j in range(3)]
    carry_r = sb("carry_reversed", [P, H])
    T1 = NT + 1
    total, base, gk, gkf, val = (sb(n, [P, T1]) for n in ("tile_edges", "tile_start", "group_start", "groups", "offset"))
    gi = sb("groups_int", [P, T1], I32)
    start, has, node, t1, t2 = (sb(n, [P, NT]) for n in ("node_start", "has_edges", "node_number", "tmp1", "tmp2"))
    node_i, sidx = sb("node_int", [P, NT], I32), sb("first_edge", [P, NT], I32)
    G4 = TABLE // P
    gno_i, gno = sb("group_int", [P, G4], I32), sb("group_number", [P, G4])
    cmp_ = sb("group_compare", [P, G4, T1])
    tg, bs = sb("group_tile", [P, G4, 1]), sb("group_base", [P, G4, 1])
    table = sb("table", [P, 2, G4], I32)
    pa, pb = k.ps(st, "pA", [P, 512]), k.ps(st, "pB", [P, 512])
    pc = [[k.ps(st, f"pC{j}_{n}", [P, 512]) for n in range(2)] for j in range(3)]
    (ld, ld_e, pad, own, pe_s, v_s, t_s, stored, cons, sc, ex, half, fill_in) = (k.sem("p3_" + n) for n in (
        "loaded", "records_loaded", "padded", "dve", "pe", "dve_to_pe", "table", "stored", "const", "scattered", "exp", "scores", "er_in"))
    turned = [k.sem(f"p3_turned{j}") for j in range(3)]
    given = [k.sem(f"p3_given{j}") for j in range(3)]
    body = (P - 1) * STRIP
    halves = ((0, STRIP // 2), (STRIP // 2, STRIP))
    with nc.Block() as block:
        @block.sync
        def _(sp):
            dst = ins["dst"]
            sp.wait_ge(pad, 1)
            sp.dma_start(k.dst_i[0:P - 1, :], dst[0:body].rearrange("(p c) -> p c", c=STRIP)).then_inc(ld, 16)
            sp.dma_start(k.dst_i[P - 1:P, 0:EL_LAST], dst[body:E].rearrange("(p c) -> p c", p=1)).then_inc(ld, 16)
            sp.dma_start(prev[0:1, 1:STRIP], dst[0:STRIP - 1].rearrange("(p c) -> p c", p=1)).then_inc(ld, 16)
            sp.dma_start(prev[1:P - 1, :], dst[STRIP - 1:body - 1].rearrange("(p c) -> p c", c=STRIP)).then_inc(ld, 16)
            sp.dma_start(prev[P - 1:P, 0:EL_LAST + 1], dst[body - 1:E].rearrange("(p c) -> p c", p=1)).then_inc(ld, 16)
            sp.dma_start(src[0:P - 1, :], ins["src"][0:body].rearrange("(p c) -> p c", c=STRIP)).then_inc(ld_e, 16)
            sp.dma_start(src[P - 1:P, 0:EL_LAST], ins["src"][body:E].rearrange("(p c) -> p c", p=1)).then_inc(ld_e, 16)
            sp.wait_ge(t_s, 2)
            with nc.allow_non_contiguous_dma("a small table, once"):
                for j in range(2):
                    sp.dma_start(k.table_d[j, :].rearrange("(c p) -> p c", p=P), table[:, j, :]).then_inc(stored, 16)
            sp.wait_ge(sc, 16 * NT)
            sp.wait_ge(half, 1)
            sp.dma_start(fl[:, :, :].rearrange("p c h -> p (c h)"), k.fill_d[0:ES, :].rearrange("(p c) h -> p (c h)", p=P)).then_inc(fill_in, 16)
            sp.wait_ge(half, 3)
            sp.dma_start(k.edge_d[E:EROWS, :].rearrange("(p c) r -> p (c r)", p=P), tail[:, :, :].rearrange("p c r -> p (c r)")).then_inc(stored, 16)
            for n, (a, z) in enumerate(halves):
                sp.wait_ge(ex, n + 1)
                z2 = min(z, EL_LAST)
                sp.dma_start(k.edge_d[0:body, :].rearrange("(p c) r -> p c r", c=STRIP)[:, a:z, :], rec[0:P - 1, a:z, :]).then_inc(stored, 16)
                sp.dma_start(k.edge_d[body:E, :].rearrange("(p c) r -> p c r", p=1)[:, a:z2, :], rec[P - 1:P, a:z2, :]).then_inc(stored, 16)
            sp.wait_ge(stored, 16 * 7)

        @block.gpsimd
        def _(pool):
            pool.iota(node_i[:, :], [[P, NT]], base=0, channel_multiplier=1).then_inc(cons, 1)
            pool.iota(gno_i[:, :], [[P, G4]], base=0, channel_multiplier=1).then_inc(cons, 1)
            pool.memset(flip[:, :], 0.0).then_inc(cons, 1)
            pool.wait_ge(cons, 3)
            pool.affine_select(out=flip[:, :], in_=flip[:, :], compare_op=ALU.not_equal, fill=1.0, base=1 - P,
                               pattern=[[1, P]], channel_multiplier=1).then_inc(cons, 1)
            pool.wait_ge(t_s, 1)
            for t in range(NT):
                pool.indirect_dma_start(k.fill_d[:, :], IndexOn(ap=sidx[:, t:t + 1], axis=0), k.elr[:, t, H:2 * H], None).then_inc(sc, 16)
            pool.wait_ge(sc, 16 * NT)

        @block.scalar
        def _(act):
            for n, (a, z) in enumerate(halves):
                act.wait_ge(half, n + 4)
                nc.scalar.activation(rec[:, a:z, 0:H], k.el_e[:, a:z, :], ACT.Exp).then_inc(ex, 1)

        @block.vector
        def _(dve):
            link = Chain(dve, own)
            link(dve.memset(k.dst_i[:, :], PAD_DST))
            link(dve.memset(prev[:, :], -1))
            link(dve.memset(src[:, :], 0))
            dve.sem_inc(pad, 1)
            dve.wait_ge(pe_s, 1)
            link(dve.memset(total[:, :], 0.0))
            link(dve.tensor_copy(total[:, 0:NT], pb[:, 0:NT]))
            link(dve.memset(base[:, :], 0.0))
            link(dve.memset(gk[:, :], 0.0))
            link(dve.tensor_tensor_scan(base[:, 1:T1], k.ones[:, 0:NT], total[:, 0:NT], 0.0, ALU.mult, ALU.add))
            link(dve.tensor_tensor(start[:, :], pa[:, 0:NT], base[:, 0:NT], ALU.add))
            dve.wait_ge(cons, 4)
            link(dve.tensor_copy(node[:, :], node_i[:, :]))
            link(dve.tensor_scalar(has[:, :], k.count[:, :], 0.0, None, ALU.is_gt))
            link(dve.tensor_tensor(t1[:, :], start[:, :], has[:, :], ALU.mult))
            link(dve.tensor_scalar(node[:, :], node[:, :], float(ES), None, ALU.add))
            link(dve.tensor_tensor(t2[:, :], node[:, :], has[:, :], ALU.mult))
            link(dve.tensor_tensor(t2[:, :], node[:, :], t2[:, :], ALU.subtract))
            link(dve.tensor_tensor(sidx[:, :], t1[:, :], t2[:, :], ALU.add))
            dve.sem_inc(t_s, 1)
            link(dve.tensor_copy(gno[:, :], gno_i[:, :]))
            link(dve.tensor_scalar(t1[:, :], total[:, 0:NT], float(GE - 1), None, ALU.add))
            link(dve.tensor_copy(gi[:, 0:NT], t1[:, :]))
            link(dve.tensor_single_scalar(gi[:, 0:NT], gi[:, 0:NT], GE.bit_length() - 1, ALU.logical_shift_right))
            link(dve.tensor_copy(gkf[:, 0:NT], gi[:, 0:NT]))
            link(dve.tensor_tensor_scan(gk[:, 1:T1], k.ones[:, 0:NT], gkf[:, 0:NT], 0.0, ALU.mult, ALU.add))
            link(dve.scalar_tensor_tensor(val[:, :], gk[:, :], -float(GE), base[:, :], ALU.mult, ALU.add))
            b3 = lambda a, n: a.unsqueeze(1).broadcast_to([P, G4, n])
            link(dve.tensor_tensor(cmp_[:, :, 0:NT], b3(gk[:, 1:T1], NT), gno[:, :].unsqueeze(2).broadcast_to([P, G4, NT]), ALU.is_le))
            link(dve.tensor_reduce(tg[:, :, 0], cmp_[:, :, 0:NT], AX.X, ALU.add))
            link(dve.tensor_tensor(cmp_[:, :, :], b3(k.iota[:, 0:T1], T1), tg[:, :, :].broadcast_to([P, G4, T1]), ALU.is_equal))
            link(dve.tensor_tensor(cmp_[:, :, :], cmp_[:, :, :], b3(val[:, :], T1), ALU.mult))
            link(dve.tensor_reduce(bs[:, :, 0], cmp_[:, :, :], AX.X, ALU.add))
            link(dve.scalar_tensor_tensor(bs[:, :, 0], gno[:, :], float(GE), bs[:, :, 0], ALU.mult, ALU.add))
            link(dve.tensor_scalar(table[:, 0, :], bs[:, :, 0], float(E), None, ALU.min))
            link(dve.tensor_scalar(table[:, 1, :], tg[:, :, 0], float(NT - 1), None, ALU.min))
            dve.sem_inc(t_s, 1)
            dve.wait_ge(ld, 80)
            link(dve.memset(zero[:, :], 0.0))
            link(dve.tensor_tensor(k.cont[:, :], k.dst_i[:, :], prev[:, :], ALU.is_equal))
            link(dve.tensor_scalar(neg[:, :], k.cont[:, :], 1.0, BIG, ALU.subtract, ALU.mult))
            link(dve.memset(negr[:, 0:1], 0.0))
            link(dve.tensor_tensor(negr[:, 1:STRIP], neg[:, STRIP - 1:0:-1], zero[:, 1:STRIP], ALU.add))
            link(dve.tensor_tensor(rev, k.el_e[:, ::-1, :], k.el_e[:, ::-1, :], ALU.max))
            link(dve.tensor_tensor_scan(pcont[:, :], k.cont[:, :], zero[:, :], 1.0, ALU.mult, ALU.add))
            for h in range(H):
                link(dve.tensor_tensor_scan(run[:, :, h], neg[:, :], k.el_e[:, :, h], -BIG, ALU.add, ALU.max))

            def give(j, across, last):
                link(dve.tensor_copy(carry[j][0][:, 0:H], across.broadcast_to([P, H])))
                link(dve.tensor_copy(carry[j][0][:, H:2 * H], last))
                dve.sem_inc(given[j], 1)

            def across(j, op0, op1, first):
                _, bA, bB, ci, _ = carry[j]
                dve.wait_ge(turned[j], 1)
                link(dve.tensor_copy(bA[:, :], pc[j][0][0:H, 0:P]))
                link(dve.tensor_copy(bB[:, :], pc[j][1][0:H, 0:P]))
                link(dve.memset(ci[:, :], first))
                link(dve.tensor_tensor_scan(ci[:, 1:P + 1], bA[:, :], bB[:, :], first, op0, op1))
                dve.sem_inc(given[j], 1)

            link(dve.tensor_reduce(t1[:, 0:1], neg[:, :], AX.X, ALU.min))
            give(0, t1[:, 0:1], run[:, STRIP - 1, :])
            for h in range(H):
                link(dve.tensor_tensor_scan(fl[:, :, h], negr[:, :], rev[:, :, h], -BIG, ALU.add, ALU.max))
            across(0, ALU.add, ALU.max, -BIG)
            link(dve.tensor_reduce(t1[:, 0:1], negr[:, :], AX.X, ALU.min))
            link(dve.tensor_tensor(t1[:, 0:1], t1[:, 0:1], neg[:, 0:1], ALU.add))
            link(dve.tensor_tensor(t2[:, 0:H], fl[:, STRIP - 1, :], neg[:, 0:1].broadcast_to([P, H]), ALU.add))
            give(1, t1[:, 0:1], t2[:, 0:H])
            dve.sem_inc(half, 1)
            dve.wait_ge(turned[0], 2)
            link(dve.tensor_copy(carry[0][4][:, :], pc[0][0][:, 0:H]))
            for h in range(H):
                link(dve.tensor_tensor_scan(run[:, :, h], neg[:, :], k.el_e[:, :, h], carry[0][4][:, h:h + 1], ALU.add, ALU.max))
            across(1, ALU.add, ALU.max, -BIG)
            dve.wait_ge(turned[1], 2)
            link(dve.tensor_copy(carry_r[:, :], pc[1][0][:, 0:H]))
            dve.sem_inc(given[1], 1)
            dve.wait_ge(turned[1], 3)
            link(dve.tensor_copy(carry[1][4][:, :], pc[1][1][:, 0:H]))
            for h in range(H):
                link(dve.tensor_tensor_scan(rev[:, :, h], negr[:, :], rev[:, :, h], carry[1][4][:, h:h + 1], ALU.add, ALU.max))
            link(dve.tensor_tensor(run[:, :, :], run[:, :, :], rev[:, ::-1, :], ALU.max))
            dve.wait_ge(ld_e, 32)
            link(dve.memset(tail[:, :, :], 0.0))
            link(dve.memset(tail[:, :, H:H + 1], float(PAD_DST)))
            link(dve.tensor_copy(rec[:, :, H], k.dst_i[:, :]))
            link(dve.tensor_copy(rec[:, :, H + 1].bitcast(I32), src[:, :]))
            dve.sem_inc(half, 2)
            dve.wait_ge(fill_in, 16)
            for h in range(H):
                link(dve.tensor_tensor_scan(fl[:, :, h], k.cont[:, :], fl[:, :, h], 0.0, ALU.mult, ALU.add))
            give(2, pcont[:, STRIP - 1:STRIP], fl[:, STRIP - 1, :])
            across(2, ALU.mult, ALU.add, 0.0)
            dve.wait_ge(turned[2], 2)
            link(dve.tensor_copy(carry[2][4][:, :], pc[2][0][:, 0:H]))
            for h in range(H):
                link(dve.scalar_tensor_tensor(fl[:, :, h], pcont[:, :], carry[2][4][:, h:h + 1], fl[:, :, h], ALU.mult, ALU.add))
            for a, z in halves:
                for v in (run, k.el_e):
                    link(dve.tensor_tensor(v[:, a:z, :], v[:, a:z, :], fl[:, a:z, :], ALU.add))
                    link(dve.scalar_tensor_tensor(v[:, a:z, :], v[:, a:z, :], 0.2, v[:, a:z, :], ALU.mult, ALU.max))
                link(dve.tensor_tensor(k.el_e[:, a:z, :], k.el_e[:, a:z, :], run[:, a:z, :], ALU.subtract))
                dve.sem_inc(half, 1)

        @block.tensor
        def _(pe):
            nc.tensor.matmul(pa[:, 0:NT], k.upper[:, :], k.count[:, :], start=True, stop=True)
            nc.tensor.matmul(pb[:, 0:NT], k.ones[:, :], k.count[:, :], start=True, stop=True).then_inc(pe_s, 1)
            pe.wait_ge(cons, 4)

            def turn(j, order):
                strip = carry[j][0]
                pe.wait_ge(given[j], 1)
                nc.tensor.matmul(pc[j][0][0:H, 0:P], strip[:, 0:H], order[:, :], start=True, stop=True)
                nc.tensor.matmul(pc[j][1][0:H, 0:P], strip[:, H:2 * H], order[:, :], start=True, stop=True).then_inc(turned[j], 1)

            def turn_back(j):
                pe.wait_ge(given[j], 2)
                nc.tensor.transpose(pc[j][0][:, 0:H], carry[j][3][:, 0:P], k.ident[0:H, 0:H]).then_inc(turned[j], 1)

            turn(0, k.ident)
            turn_back(0)
            turn(1, flip)
            turn_back(1)
            pe.wait_ge(given[1], 3)
            nc.tensor.matmul(pc[1][1][:, 0:H], flip[:, :], carry_r[:, :], start=True, stop=True).then_inc(turned[1], 1)
            turn(2, k.ident)
            turn_back(2)
    st.close()


def message(k):
    nc, ins = k.nc, k.ins
    st = ExitStack()
    sb = lambda *a: k.sb(st, *a)
    U, R = 8, H + 2
    first_i, first, nodes = sb("tile_first_int", [P, NT], I32), sb("tile_first", [P, NT, 1]), sb("node_numbers", [P, NP])
    tabs = sb("table_row", [1, 2 * TABLE], I32)
    rec = sb("group_records", [P, U, GJ * R])
    feat = sb("group_feat", [P, U, GJ, D])
    oh, wt = sb("group_onehot", [P, U, GJ, P]), sb("group_weighted", [P, U, GJ, GF])
    ps = [k.ps(st, f"pSum{u}", [P, 512]) for u in range(U)]
    rec_in = [k.sem(f"p5_record{u}") for u in range(U)]
    feat_in = [k.sem(f"p5_feat{u}") for u in range(U)]
    zero, tab_in, made, ex_done, mm_done, sum_done, ip = (k.sem("p5_" + n) for n in ("zero", "table", "weighted",
                                                          "weights", "products", "sums", "nodes"))
    with nc.Block() as block:
        @block.sync
        def _(sp):
            sp.dma_start(tabs[:, :], k.table_d.rearrange("a g -> (a g)").rearrange("(o g) -> o g", o=1)).then_inc(tab_in, 16)
            sp.wait_ge(tab_in, 16)
            with sp.Fori(0, NG // U) as i:
                for u in range(U):
                    g = U * i + u
                    base = sp.value_load(tabs[0:1, ds(g, 1)], min_val=0, max_val=E)
                    sp.wait_ge(made, g + 1)
                    sp.wait_ge(ex_done, g + 1)
                    sp.dma_start(rec[:, u, :], k.edge_d[ds(base, GE), :].rearrange("(p j) r -> p (j r)", j=GJ)).then_inc(rec_in[u], 16)

        @block.gpsimd
        def _(pool):
            pool.iota(first_i[:, :], [[P, NT]], base=0, channel_multiplier=0).then_inc(ip, 1)
            pool.wait_ge(ip, 1)
            pool.tensor_copy(first[:, :, 0], first_i[:, :]).then_inc(ip, 1)
            with pool.Fori(0, NG // U) as i:
                for u in range(U):
                    pool.wait_ge(rec_in[u], 16 * i + 16)
                    settle(pool, k.passed)
                    for j in range(GJ):
                        at = j * R + H + 1
                        pool.indirect_dma_start(feat[:, u, j, :], None, k.feat_d[:, :],
                                                IndexOn(ap=rec[:, u, at:at + 1].bitcast(I32), axis=0)).then_inc(feat_in[u], 16)

        @block.scalar
        def _(act):
            act.sem_inc(ex_done, U)
            with act.Fori(0, NG // U) as i:
                for u in range(U):
                    act.wait_ge(rec_in[u], 16 * i + 16)
                    act.wait_ge(mm_done, U * i + u + 1)
                    r = rec[:, u, :].rearrange("p (j r) -> p j r", j=GJ)
                    nc.scalar.activation(wt[:, u, :, D:GF], r[:, :, 0:H], ACT.Copy).then_inc(ex_done, 1)

        @block.vector
        def _(dve):
            dve.memset(k.agg[:, :, :], 0.0).then_inc(zero, 1)
            dve.wait_ge(zero, 1)
            dve.wait_ge(ip, 2)
            dve.tensor_tensor(nodes[:, :].rearrange("p (t n) -> p t n", n=P), k.iota[:, :].unsqueeze(1).broadcast_to([P, NT, P]),
                              first[:, :, :].broadcast_to([P, NT, P]), ALU.add).then_inc(zero, 1)
            dve.wait_ge(zero, 2)
            dve.wait_ge(tab_in, 16)
            dve.sem_inc(made, U)
            dve.sem_inc(sum_done, U)
            with dve.Fori(0, NG // U) as i:
                tile = {}

                def weigh(u):
                    g = U * i + u
                    tile[u] = dve.value_load(tabs[0:1, ds(TABLE + g, 1)], min_val=0, max_val=NT - 1)
                    dve.wait_ge(rec_in[u], 16 * i + 16)
                    dve.wait_ge(mm_done, g + 1)
                    for j in range(GJ):
                        dve.tensor_scalar(oh[:, u, j, :], nodes[:, ds(tile[u] * P, P)], rec[:, u, j * R + H:j * R + H + 1],
                                          None, ALU.is_equal)
                    dve.wait_ge(feat_in[u], 16 * GJ * (i + 1))
                    last = dve.tensor_tensor(wt[:, u, :, 0:D].rearrange("p j (h c) -> p j h c", h=H),
                                             feat[:, u, :, :].rearrange("p j (h c) -> p j h c", h=H),
                                             rec[:, u, :].rearrange("p (j r) -> p j r", j=GJ)[:, :, 0:H].unsqueeze(3).broadcast_to([P, GJ, H, HD]),
                                             ALU.mult)
                    last.then_inc(made, 1)

                def add(u):
                    g = U * i + u
                    dve.wait_ge(mm_done, g + 1 + U)
                    dve.wait_ge(sum_done, g + U)
                    dve.tensor_tensor(k.agg[:, ds(tile[u], 1), :], k.agg[:, ds(tile[u], 1), :],
                                      ps[u][:, 0:GF].unsqueeze(1), ALU.add).then_inc(sum_done, 1)

                weigh(0)
                for u in range(1, U):
                    weigh(u)
                    add(u - 1)
                add(U - 1)

        @block.tensor
        def _(pe):
            pe.sem_inc(mm_done, U)
            with pe.Fori(0, NG // U) as i:
                for u in range(U):
                    g = U * i + u
                    pe.wait_ge(made, g + 1 + U)
                    pe.wait_ge(ex_done, g + 1 + U)
                    pe.wait_ge(sum_done, g + 1)
                    for j in range(GJ):
                        last = nc.tensor.matmul(ps[u][:, 0:GF], oh[:, u, j, :], wt[:, u, j, :], start=j == 0, stop=j == GJ - 1)
                    last.then_inc(mm_done, 1)
    st.close()


def update(k):
    nc, ins = k.nc, k.ins
    st = ExitStack()
    sb = lambda *a: k.sb(st, *a)
    gb, wr = sb("gat_bias_rows", [P, D]), sb("w_router", [P, DK, X])
    xs, xn = sb("x_in", [P, 2, D]), sb("x2n_stage", [P, 2, D])
    xt, x2t = sb("xT_stage", [P, 2, DK, P]), sb("x2T_stage", [P, 2, DK, P])
    s1, g1 = sb("weight_sum", [P, NT, H]), sb("messages", [P, 2, D])
    stats, mv, sd, rs = (sb(n, [P, 2, w]) for n, w in (("stats", 6), ("mv", 2), ("sd", 1), ("rs", 1)))
    pu = [k.ps(st, f"pU{b}", [P, 512]) for b in range(2)]
    pt = [k.ps(st, f"pT{b}", [P, 512]) for b in range(2)]
    pl = [k.ps(st, f"pL{b}", [P, 512]) for b in range(2)]
    x_in = [k.sem(f"p6_x_in{b}") for b in range(2)]
    stored = [k.sem(f"p6_stored{b}") for b in range(2)]
    (ld, xt_done, mm_done, u_done, mv_done, sd_done, xn_done, tr_done, x2t_done, lg_mm, lg_done, own, own_r, g_own, g_done, x2_st, z) = (
        k.sem("p6_" + n) for n in ("loaded", "xT", "products", "x2", "mv", "sd", "x2n", "transposed", "x2T",
                                   "logits_mm", "logits", "dve", "dve_rs", "pool", "messages", "x2_stored", "zero"))
    s1_done = k.sem("p6_weight_sums")
    LINKS = 2
    with nc.Block() as block:
        @block.sync
        def _(sp):
            sp.dma_start(gb[:, :], ins["L0_gnn_gat_bias"].partition_broadcast(P)).then_inc(ld, 16)
            sp.dma_start(wr[:, :, :], ins["L0_ffn_Wr"].rearrange("(k p) n -> p k n", p=P)).then_inc(ld, 16)
            prime(k, sp, stored)

            def load(t, b, rows, i):
                sp.wait_ge(mm_done, freed(t))
                sp.dma_start(xs[:rows, b, :], ins["x"][ds(t * P, rows), :]).then_inc(x_in[b], 16)

            def store(t, b, rows, i):
                sp.wait_ge(xn_done, done(t))
                sp.dma_start(k.x2_d[ds(t * P, rows), :].unsqueeze(1), k.agg[:rows, ds(t, 1), 0:D]).then_inc(x2_st, 16)
                sp.dma_start(k.x2n_d[ds(t * P, rows), :], xn[:rows, b, :]).then_inc(stored[b], 16)

            pipeline(sp, (0, load), (2, store))
            for b in range(2):
                sp.wait_ge(stored[b], 16 * (NT // 2 + 2 - b))
            sp.wait_ge(x2_st, 16 * NT)

        @block.gpsimd
        def _(pool):
            pool.wait_ge(ld, 32)
            pool.wait_ge(z, 2)

            def mean(t, b, rows, i):
                pool.wait_ge(u_done, freed(t))
                Chain(pool, g_own, t)(pool.tensor_tensor(
                    g1[:rows, b, :].rearrange("p (h c) -> p h c", h=H), k.agg[:rows, ds(t, 1), 0:D].rearrange("p a (h c) -> p (a h) c", h=H),
                    s1[:rows, ds(t, 1), :].rearrange("p a h -> p (a h)").unsqueeze(2).broadcast_to([rows, H, HD]), ALU.mult))
                pool.tensor_tensor(g1[:rows, b, :], g1[:rows, b, :], gb[:rows, :], ALU.add).then_inc(g_done, 1)

            pipeline(pool, (0, mean))

        @block.vector
        def _(dve):
            dve.memset(k.logits[:, :, :], 0.0).then_inc(z, 1)
            dve.sem_inc(u_done, CREDIT)
            dve.sem_inc(xn_done, CREDIT)
            dve.wait_ge(ld, 32)
            dve.tensor_scalar(s1[:, :, :], k.agg[:, :, D:GF], 1.0e-30, None, ALU.max).then_inc(s1_done, 1)
            dve.wait_ge(s1_done, 1)
            dve.reciprocal(s1[:, :, :], s1[:, :, :]).then_inc(z, 1)

            def residual(t, b, rows, i):
                link = Chain(dve, own, LINKS * t)
                dve.wait_ge(g_done, t + 1)
                link(dve.scalar_tensor_tensor(g1[:rows, b, :], g1[:rows, b, :], 0.01, g1[:rows, b, :], ALU.mult, ALU.max))
                dve.wait_ge(mm_done, done(t))
                x2 = k.agg[:rows, ds(t, 1), 0:D].rearrange("p a d -> p (a d)")
                dve.tensor_tensor(x2, pu[b][:rows, 0:D], g1[:rows, b, :], ALU.add).then_inc(u_done, 1)
                dve.wait_ge(u_done, done(t))
                settle(dve, k.passed)
                link(dve.bn_stats(stats[:rows, b, :], x2))
                settle(dve, k.passed)
                dve.bn_aggr(mv[:rows, b, :], stats[:rows, b, :]).then_inc(mv_done, 1)
                assert link.n == LINKS

            def normalise(t, b, rows, i):
                dve.wait_ge(sd_done, t + 1)
                Chain(dve, own_r, t)(dve.reciprocal(rs[:rows, b, :], sd[:rows, b, :]))
                dve.wait_ge(tr_done, freed(t))
                dve.wait_ge(stored[b], 16 * i + 16)
                dve.tensor_scalar(xn[:rows, b, :], k.agg[:rows, ds(t, 1), 0:D].rearrange("p a d -> p (a d)"), mv[:rows, b, 0:1], rs[:rows, b, :],
                                  ALU.subtract, ALU.mult).then_inc(xn_done, 1)

            pipeline(dve, (1, normalise), (0, residual))

        @block.scalar
        def _(act):
            act.sem_inc(xt_done, CREDIT)
            act.sem_inc(x2t_done, CREDIT)
            act.sem_inc(lg_done, CREDIT)
            act.wait_ge(z, 1)

            def stage_xT(t, b, rows, i):
                act.wait_ge(mm_done, freed(t))
                nc.scalar.activation(xt[:, b, :, 0:rows], k.xnT[:, :, ds(t * P, rows)], ACT.Copy).then_inc(xt_done, 1)

            def deviation(t, b, rows, i):
                act.wait_ge(mv_done, t + 1)
                nc.scalar.activation(sd[:rows, b, :], mv[:rows, b, 1:2], ACT.Sqrt, bias=k.eps[:rows, :]).then_inc(sd_done, 1)

            def turned(t, b, rows, i):
                act.wait_ge(tr_done, done(t))
                act.wait_ge(lg_mm, freed(t))
                nc.scalar.activation(x2t[:, b, :, 0:rows], pt[b][:, 0:DK * P].rearrange("p (k n) -> p k n", k=DK)[:, :, 0:rows],
                                     ACT.Copy).then_inc(x2t_done, 1)

            def keep_logits(t, b, rows, i):
                act.wait_ge(lg_mm, done(t))
                nc.scalar.activation(k.logits[:rows, ds(t, 1), :], pl[b][:rows, 0:X].unsqueeze(1), ACT.Copy).then_inc(lg_done, 1)

            pipeline(act, (0, stage_xT), (3, turned), (4, keep_logits), (2, deviation))

        @block.tensor
        def _(pe):
            for s in (mm_done, tr_done, lg_mm):
                pe.sem_inc(s, CREDIT)
            pe.wait_ge(ld, 32)

            def product(t, b, rows, i):
                pe.wait_ge(xt_done, done(t))
                pe.wait_ge(u_done, freed(t))
                for c in range(DK):
                    nc.tensor.matmul(pu[b][:rows, 0:D], xt[:, b, c, 0:rows], k.w_lin[:, c, :], start=c == 0, stop=False)
                nc.tensor.matmul(pu[b][:rows, 0:D], k.ones[0:1, 0:rows], k.cb[0:1, :], start=False, stop=False)
                pe.wait_ge(x_in[b], 16 * i + 16)
                nc.tensor.matmul(pu[b][:rows, 0:D], k.ident[:rows, :rows], xs[:rows, b, :], start=False, stop=True).then_inc(mm_done, 1)

            def turn(t, b, rows, i):
                pe.wait_ge(xn_done, done(t))
                pe.wait_ge(x2t_done, freed(t))
                for c in range(DK):
                    last = nc.tensor.transpose(pt[b][:, c * P:c * P + rows], xn[:rows, b, c * P:(c + 1) * P], k.ident[:rows, :rows])
                last.then_inc(tr_done, 1)

            def router(t, b, rows, i):
                pe.wait_ge(x2t_done, done(t))
                pe.wait_ge(lg_done, freed(t))
                for c in range(DK):
                    last = nc.tensor.matmul(pl[b][:rows, 0:X], x2t[:, b, c, 0:rows], wr[:, c, :], start=c == 0, stop=c == DK - 1)
                last.then_inc(lg_mm, 1)

            pipeline(pe, (3, router), (2, turn), (0, product))
    st.close()


def load_weights(k, queue, experts):
    shared = ("L0_ffn_W1s", "L0_ffn_b1s", "L0_ffn_W2s", "L0_ffn_b2s")
    routed = ("L0_ffn_W1p", "L0_ffn_b1p", "L0_ffn_W2p", "L0_ffn_b2p")
    for e in experts:
        u, c1, d, c2 = (k.ins[n] if e == X else k.ins[n][e] for n in (shared if e == X else routed))
        landed = k.shared_in if e == X else k.routed_in
        queue.dma_start(k.w_up[:, e, :, :], u.rearrange("(c p) f -> p c f", p=P)).then_inc(landed, 16)
        queue.dma_start(k.w_down[:, e, :, :], d.rearrange("(c p) n -> p c n", p=P)).then_inc(landed, 16)
        with k.nc.allow_non_contiguous_dma("short bias columns"):
            queue.dma_start(k.b_up[:, e, :], c1.rearrange("(c p) -> p c", p=P)).then_inc(landed, 16)
        queue.dma_start(k.b_down[:, e, :], c2.partition_broadcast(P)).then_inc(landed, 16)


def route(k):
    nc = k.nc
    st = ExitStack()
    sb = lambda *a: k.sb(st, *a)
    T1 = NT + 1
    node_i, node, valid, spare = sb("node_int", [P, NT], I32), sb("node_number", [P, NT]), sb("valid", [P, NT]), sb("spare_row", [P, NT])
    rev = sb("reversed", [P, 1, X])
    m1, m2, mt, dw = (sb(n, [P, NT, 1]) for n in ("best", "second", "first_index", "difference"))
    l2, t8, oh1, oh2, sel, slot = (sb(n, [P, NT, X]) for n in ("logits2", "tmp8", "choice1", "choice2", "selected", "slot"))
    tb = sb("before_tile", [P, T1, X])
    nbf, be = sb("expert_blocks", [P, X]), sb("block_end", [P, X + 1])
    nbi = sb("expert_blocks_int", [P, X], I32)
    bno_i, bno, cmp_, eb, ebi = (sb("block_int", [P, 2], I32), sb("block_number", [P, 2]), sb("block_compare", [P, 2, X]),
                                 sb("block_expert", [P, 2, 1]), sb("block_expert_int", [P, 2], I32))
    pos = sb("choice_slot", [P, NT])
    gate = sb("gates", [P, 2, NT])
    pr, pq = k.ps(st, "pRank", [P, 512]), k.ps(st, "pSum", [P, 512])
    own, cons, pe_s, v_s, ex, stored = (k.sem("p7_" + n) for n in ("dve", "const", "pe", "dve_done", "exp", "stored"))
    with nc.Block() as block:
        @block.sync
        def _(sp):
            load_weights(k, sp, (X,))
            sp.wait_ge(v_s, 3)
            with nc.allow_non_contiguous_dma("a small table, once"):
                sp.dma_start(k.block_d[0, :].rearrange("(c p) -> p c", p=P), ebi[:, :]).then_inc(stored, 16)
            sp.wait_ge(stored, 16)

        @block.gpsimd
        def _(pool):
            pool.iota(node_i[:, :], [[P, NT]], base=0, channel_multiplier=1).then_inc(cons, 1)
            pool.iota(bno_i[:, :], [[P, 2]], base=0, channel_multiplier=1).then_inc(cons, 1)

        @block.scalar
        def _(act):
            act.wait_ge(v_s, 1)
            nc.scalar.activation(dw[:, :, :], dw[:, :, :], ACT.Exp).then_inc(ex, 1)

        @block.vector
        def _(dve):
            link = Chain(dve, own)
            over_e = lambda a: a.broadcast_to([P, NT, X])
            dve.wait_ge(cons, 2)
            link(dve.tensor_copy(node[:, :], node_i[:, :]))
            link(dve.tensor_copy(bno[:, :], bno_i[:, :]))
            link(dve.tensor_scalar(valid[:, :], node[:, :], float(N), None, ALU.is_lt))
            link(dve.tensor_scalar(rev[:, 0, :], k.iota[:, 0:X], -1.0, float(X), ALU.mult, ALU.add))

            def choose(logits, best, out):
                link(dve.tensor_reduce(best[:, :, 0], logits[:, :, :], AX.X, ALU.max))
                link(dve.tensor_tensor(t8[:, :, :], logits[:, :, :], over_e(best[:, :, :]), ALU.is_equal))
                link(dve.tensor_tensor(t8[:, :, :], t8[:, :, :], rev[:, :, :].broadcast_to([P, NT, X]), ALU.mult))
                link(dve.tensor_reduce(mt[:, :, 0], t8[:, :, :], AX.X, ALU.max))
                link(dve.tensor_tensor(out[:, :, :], t8[:, :, :], over_e(mt[:, :, :]), ALU.is_equal))

            choose(k.logits, m1, oh1)
            link(dve.scalar_tensor_tensor(l2[:, :, :], oh1[:, :, :], -BIG, k.logits[:, :, :], ALU.mult, ALU.add))
            choose(l2, m2, oh2)
            link(dve.tensor_tensor(dw[:, :, :], m2[:, :, :], m1[:, :, :], ALU.subtract))
            dve.sem_inc(v_s, 1)
            for oh in (oh1, oh2):
                link(dve.tensor_tensor(oh[:, :, :], oh[:, :, :], over_e(valid[:, :].unsqueeze(2)), ALU.mult))
            link(dve.tensor_tensor(sel[:, :, :], oh1[:, :, :], oh2[:, :, :], ALU.add))
            dve.sem_inc(v_s, 1)
            dve.wait_ge(ex, 1)
            link(dve.tensor_scalar(gate[:, 0, :], dw[:, :, 0], 1.0, None, ALU.add))
            link(dve.reciprocal(gate[:, 0, :], gate[:, 0, :]))
            link(dve.tensor_tensor(gate[:, 1, :], gate[:, 0, :], dw[:, :, 0], ALU.mult))
            link(dve.tensor_copy(k.choice[:, :, :, 1], gate[:, :, :]))
            for j in range(2):
                link(dve.tensor_copy(k.choice[:, j, :, 0].bitcast(I32), node_i[:, :]))
            dve.wait_ge(pe_s, 1)
            link(dve.memset(tb[:, 0:1, :], 0.0))
            q3 = pq[:, 0:NT * X].rearrange("p (t e) -> p t e", e=X)
            for e in range(X):
                link(dve.tensor_tensor_scan(tb[:, 1:T1, e], k.ones[:, 0:NT], q3[:, :, e], 0.0, ALU.mult, ALU.add))
            link(dve.tensor_scalar(nbf[:, :], tb[:, NT, :], float(BLK - 1), None, ALU.add))
            link(dve.tensor_copy(nbi[:, :], nbf[:, :]))
            link(dve.tensor_single_scalar(nbi[:, :], nbi[:, :], BLK.bit_length() - 1, ALU.logical_shift_right))
            link(dve.tensor_copy(nbf[:, :], nbi[:, :]))
            link(dve.memset(be[:, 0:1], 0.0))
            link(dve.tensor_tensor_scan(be[:, 1:X + 1], k.ones[:, 0:X], nbf[:, :], 0.0, ALU.mult, ALU.add))
            link(dve.tensor_tensor(slot[:, :, :], pr[:, 0:NT * X].rearrange("p (t e) -> p t e", e=X), tb[:, 0:NT, :], ALU.add))
            link(dve.tensor_scalar(nbf[:, :], be[:, 0:X], float(BLK), None, ALU.mult))
            link(dve.tensor_tensor(slot[:, :, :], slot[:, :, :], nbf[:, :].unsqueeze(1).broadcast_to([P, NT, X]), ALU.add))
            for j, oh in enumerate((oh1, oh2)):
                link(dve.tensor_tensor(t8[:, :, :], oh[:, :, :], slot[:, :, :], ALU.mult))
                link(dve.tensor_reduce(pos[:, :], t8[:, :, :], AX.X, ALU.add))
                link(dve.tensor_scalar(spare[:, :], valid[:, :], 1.0, -1.0, ALU.subtract, ALU.mult))
                link(dve.tensor_scalar(t8[:, :, 0], node[:, :], float(SLOTS + j * NP), None, ALU.add))
                link(dve.tensor_tensor(spare[:, :], spare[:, :], t8[:, :, 0], ALU.mult))
                link(dve.tensor_tensor(k.slot[:, j, :], spare[:, :], pos[:, :], ALU.add))
            link(dve.tensor_scalar(bno[:, :], bno[:, :], float(NT), None, ALU.subtract))
            link(dve.tensor_tensor(cmp_[:, :, :], be[:, 1:X + 1].unsqueeze(1).broadcast_to([P, 2, X]),
                                   bno[:, :].unsqueeze(2).broadcast_to([P, 2, X]), ALU.is_le))
            link(dve.tensor_reduce(eb[:, :, 0], cmp_[:, :, :], AX.X, ALU.add))
            link(dve.tensor_scalar(eb[:, :, 0], eb[:, :, 0], float(X - 1), None, ALU.min))
            link(dve.tensor_scalar(bno[:, :], bno[:, :], 0.0, float(X), ALU.is_lt, ALU.mult))
            link(dve.tensor_tensor(ebi[:, :], eb[:, :, 0], bno[:, :], ALU.add))
            dve.sem_inc(v_s, 1)

        @block.tensor
        def _(pe):
            pe.wait_ge(v_s, 2)
            s2 = sel[:, :, :].rearrange("p t e -> p (t e)")
            nc.tensor.matmul(pr[:, 0:NT * X], k.upper[:, :], s2, start=True, stop=True)
            nc.tensor.matmul(pq[:, 0:NT * X], k.ones[:, :], s2, start=True, stop=True).then_inc(pe_s, 1)
    st.close()


def experts(k):
    nc, ins = k.nc, k.ins
    st = ExitStack()
    sb = lambda *a: k.sb(st, *a)
    XA = X + 1
    w1, w2, b1, b2, sh_in, all_in = k.w_up, k.w_down, k.b_up, k.b_down, k.shared_in, k.routed_in
    tabs = sb("block_row", [1, 2 * P], I32)
    idx, sidx, xg = sb("token_index", [P, 2, 1], I32), sb("sum_index", [P, 2, 1], I32), sb("tokens", [P, 2, D])
    RB = NB - NT
    rows_i, rows_f = sb("slot_rows", [P, BLK, 2]), sb("slot_rows_f", [P, 2, BLK])
    tokens, gates = sb("tokens_of_block", [P, RB], I32), sb("gates_of_block", [P, RB, 1])
    x2, yb = sb("x2_in", [P, 2, D]), sb("result_plus_bias", [P, 2, D])
    xt, hp, ht, y = (sb(n, [P, 2, w]) for n, w in (("tokensT", DK * P), ("hidden", F), ("hiddenT", FK * P), ("result", D)))
    HF = F // 2
    px, pw = k.ps(st, "pX", [P, 512]), k.ps(st, "pSlots", [P, 512])
    ph = [k.ps(st, f"pH{j}", [P, 512]) for j in range(2)]
    pg = [k.ps(st, f"pG{j}", [P, 512]) for j in range(2)]
    py = [k.ps(st, f"pY{j}", [P, 512]) for j in range(2)]
    x_in, x2_in, x_got, stored, added = ([k.sem(f"p8_{n}{b}") for b in range(2)] for n in (
        "tokens", "x2", "tokens_gathered", "stored", "added"))
    filled, tok_in, tok_s, tok_pe, x_own, own = (k.sem("p8_" + n) for n in (
        "slots_filled", "slot_rows", "slot_columns", "slots_turned", "index", "dve"))
    tab_in, tx, xt_s, up, hp_s, th, gl, dn, y_s = (k.sem("p8_" + n) for n in (
        "table", "turned", "tokensT", "up", "hidden", "hidden_turned", "gelu", "down", "result"))
    SLOTS_AT, FIRST = NT // 2 - 6, NT // 2 - 1
    assert NT % 2 == 1 and NB % 2 == 0

    def steps(eng, head, body, tail, slots=None, routed=None):
        head()

        def pairs(a, z):
            with eng.Fori(a, z) as i:
                for b in range(2):
                    body(2 * i + b, b, i)

        pairs(0, SLOTS_AT)
        if slots:
            slots()
        pairs(SLOTS_AT, FIRST)
        if routed:
            routed()
        for i in (FIRST, FIRST + 1):
            for b in range(2):
                body(2 * i + b, b, i)
        pairs(FIRST + 2, NB // 2 - 1)
        body(NB - 2, 0, NB // 2 - 1)
        tail()

    with nc.Block() as block:
        @block.sync
        def _(sp):
            sp.dma_start(tabs[:, :], k.block_d).then_inc(tab_in, 16)
            prime(k, sp, stored)

            def load(t, b, rows, i):
                sp.wait_ge(tx, freed(t))
                sp.dma_start(xg[:, b, :], k.x2n_d[ds(t * P, P), :]).then_inc(x_in[b], 16)

            def load_x2(t, b, rows, i):
                sp.wait_ge(y_s, freed(t))
                sp.dma_start(x2[:rows, b, :], k.x2_d[ds(t * P, rows), :]).then_inc(x2_in[b], 16)

            def store(t, b, rows, i):
                sp.wait_ge(y_s, done(t))
                sp.dma_start(k.acc_d[ds(t * P, rows), :], y[:rows, b, :]).then_inc(stored[b], 16)

            pipeline(sp, (0, load), (4, store), (2, load_x2))

        @block.gpsimd
        def _(pool):
            pool.sem_inc(x_own, CREDIT)
            prime(k, pool, added)
            for t in range(NT):
                for j in range(2):
                    pool.indirect_dma_start(k.token_d[:, :], IndexOn(ap=k.slot[:, j, t:t + 1], axis=0), k.choice[:, j, t, :], None).then_inc(filled, 16)
            pool.wait_ge(filled, 32 * NT)
            pool.dma_start(rows_i[0:RB, :, :].rearrange("p s o -> p (s o)"), k.token_d[0:SLOTS, :].rearrange("(b s) o -> b (s o)", s=BLK)).then_inc(tok_in, 16)
            pool.wait_ge(tok_s, 2)

            def gather(s, b):
                pool.wait_ge(tx, freed(s))
                pool.tensor_copy(idx[:, b, :], tokens[:, ds(s - NT, 1)]).then_inc(x_own, 1)
                pool.wait_ge(x_own, seen(s, 0))
                settle(pool, k.passed)
                pool.indirect_dma_start(xg[:, b, :], None, k.x2n_d[:, :], IndexOn(ap=idx[:, b, :], axis=0)).then_inc(x_got[b], 16)

            def add(s, b, i):
                pool.tensor_copy(sidx[:, b, :], tokens[:, ds(s - NT, 1)]).then_inc(x_own, 1)
                pool.wait_ge(x_own, seen(s + 4, 1))
                settle(pool, k.passed)
                pool.wait_ge(added[1 - b], 16 * (i - NT // 2 + 1))
                settle(pool, k.passed)
                pool.wait_ge(y_s, done(s))
                settle(pool, k.passed)
                pool.indirect_dma_start(k.acc_d[:, :], IndexOn(ap=sidx[:, b, :], axis=0), y[:, b, :], None,
                                        compute_op=ALU.add).then_inc(added[b], 16)

            def seen(s, adds):
                if isinstance(s, int):
                    return CREDIT + min(s - NT + 1, RB) + max(s - NT - 4 + adds, 0)
                return CREDIT + 2 * s - 2 * NT - 3 + adds

            for s in range(NT, NT + 5):
                gather(s, s % 2)
            for b in range(2):
                pool.wait_ge(stored[b], 16 * (NT // 2 + 2 - b))
            add(NT, 1, NT // 2)
            with pool.Fori((NT + 5) // 2, NB // 2) as i:
                for b in range(2):
                    gather(2 * i + b, b)
                    add(2 * i + b - 4, b, i - 2)
            for s in range(NB - 4, NB):
                add(s, s % 2, s // 2)
            for b in range(2):
                pool.wait_ge(added[b], 16 * (NB // 2 - NT // 2 + b))
            for a in range(0, N, OUT_ROWS):
                pool.dma_start(k.out[a:a + OUT_ROWS, :], k.acc_d[a:a + OUT_ROWS, :]).then_inc(tok_in, 16)
            pool.wait_ge(tok_in, 16 * (1 + N // OUT_ROWS))

        @block.vector
        def _(dve):
            def turn(s, b):
                dve.wait_ge(tx, done(s))
                dve.tensor_copy(xt[:, b, :], px[:, 0:DK * P]).then_inc(xt_s, 1)

            def hidden(s, b):
                dve.wait_ge(th, 2 * freed(s))
                for j in range(2):
                    dve.wait_ge(up, 2 * s + j + 1)
                    dve.tensor_copy(hp[:, b, j * HF:(j + 1) * HF], ph[j][:, :]).then_inc(hp_s, 1)

            def result(s, b, i, shared):
                e = dve.value_load(tabs[0:1, ds(s, 1)], min_val=0, max_val=X)
                dve.wait_ge(dn, done(s))
                Chain(dve, own, s)(dve.tensor_tensor(yb[:, b:b + 1, :], py[b][:, 0:D].unsqueeze(1), b2[:, ds(e, 1), :], ALU.add))
                if shared:
                    dve.wait_ge(stored[b], 16 * i + 16)
                    dve.wait_ge(x2_in[b], 16 * i + 16)
                    dve.tensor_tensor(y[:, b, :], yb[:, b, :], x2[:, b, :], ALU.add).then_inc(y_s, 1)
                else:
                    if isinstance(s, int) and s == NT:
                        for c in range(2):
                            dve.wait_ge(stored[c], 16 * (NT // 2 + 2 - c))
                    dve.wait_ge(added[b], 16 * (i - NT // 2 + b))
                    dve.tensor_tensor(y[:, b:b + 1, :], yb[:, b:b + 1, :], gates[:, ds(s - NT, 1), :].broadcast_to([P, 1, D]),
                                      ALU.mult).then_inc(y_s, 1)

            def head():
                dve.sem_inc(y_s, CREDIT)
                dve.wait_ge(sh_in, 64)
                dve.wait_ge(tab_in, 16)
                turn(0, 0)
                turn(1, 1)
                hidden(0, 0)

            def body(s, b, i):
                shared = s < NT if isinstance(s, int) else not phase
                if not (isinstance(s, int) and s == NB - 2):
                    turn(s + 2, b)
                hidden(s + 1, 1 - b)
                result(s, b, i, shared)

            phase = []

            def slots():
                dve.wait_ge(tok_in, 16)
                dve.tensor_copy(rows_f[0:RB, 0, :], rows_i[0:RB, :, 0].bitcast(I32))
                dve.tensor_copy(rows_f[0:RB, 1, :], rows_i[0:RB, :, 1]).then_inc(tok_s, 1)
                dve.wait_ge(tok_pe, 1)
                dve.tensor_copy(gates[:, :, 0], pw[:, P:P + RB])
                dve.tensor_copy(tokens[:, :], pw[:, 0:RB]).then_inc(tok_s, 1)

            def routed():
                phase.append("routed")
                dve.wait_ge(all_in, 64 * X)

            steps(dve, head, body, lambda: result(NB - 1, 1, NB // 2 - 1, False), slots, routed)

        @block.scalar
        def _(act):
            def gelu(s, b):
                e = act.value_load(tabs[0:1, ds(s, 1)], min_val=0, max_val=X)
                act.wait_ge(dn, freed(s))
                for c in range(FK):
                    if c % 4 == 0:
                        act.wait_ge(th, 2 * CREDIT + 2 * s + c // 4 + 1)
                    nc.scalar.activation(ht[:, b, c * P:(c + 1) * P], pg[c // 4][:, c % 4 * P:(c % 4 + 1) * P], ACT.Gelu,
                                         bias=b1[:, ds(e, 1), c]).then_inc(gl, 1)

            act.sem_inc(gl, FK)
            act.wait_ge(sh_in, 64)
            load_weights(k, act, range(X))
            act.wait_ge(tab_in, 16)
            steps(act, lambda: None, lambda s, b, i: gelu(s, b), lambda: gelu(NB - 1, 1),
                  routed=lambda: act.wait_ge(all_in, 64 * X))

        @block.tensor
        def _(pe):
            def turn(s, b, i, shared):
                if shared:
                    pe.wait_ge(x_in[b], 16 * i + 16)
                else:
                    pe.wait_ge(x_got[b], 16 * (i - NT // 2 + b))
                if not (isinstance(s, int) and s == 0):
                    pe.wait_ge(xt_s, s)
                for c in range(DK):
                    last = nc.tensor.transpose(px[:, c * P:(c + 1) * P], xg[:, b, c * P:(c + 1) * P], k.ident[:, :])
                last.then_inc(tx, 1)

            def first_layer(s, b, e, j):
                pe.wait_ge(xt_s, s + 1)
                if not (isinstance(s, int) and s == 0):
                    pe.wait_ge(hp_s, 2 * s)
                for c in range(DK):
                    last = nc.tensor.matmul(ph[j][:, :], xt[:, b, c * P:(c + 1) * P],
                                            w1[:, ds(e, 1), c, j * HF:(j + 1) * HF], start=c == 0, stop=c == DK - 1)
                last.then_inc(up, 1)

            def turn_hidden(s, b):
                pe.wait_ge(hp_s, 2 * s + 2)
                pe.wait_ge(gl, FK * s + FK)
                for c in range(FK):
                    last = nc.tensor.transpose(pg[c // 4][:, c % 4 * P:(c % 4 + 1) * P], hp[:, b, c * P:(c + 1) * P], k.ident[:, :])
                    if c % 4 == 3:
                        last.then_inc(th, 1)

            def second_layer(s, b, e):
                pe.wait_ge(y_s, freed(s))
                for c in range(FK):
                    pe.wait_ge(gl, FK * s + FK + c + 1)
                    last = nc.tensor.matmul(py[b][:, 0:D], ht[:, b, c * P:(c + 1) * P], w2[:, ds(e, 1), c, :],
                                            start=c == 0, stop=c == FK - 1)
                last.then_inc(dn, 1)

            def expert(s):
                return pe.value_load(tabs[0:1, ds(s, 1)], min_val=0, max_val=X)

            def head():
                pe.sem_inc(tx, CREDIT)
                pe.sem_inc(dn, CREDIT)
                pe.sem_inc(th, 2 * CREDIT)
                pe.wait_ge(sh_in, 64)
                pe.wait_ge(tab_in, 16)
                turn(0, 0, 0, True)
                turn(1, 1, 0, True)
                e = expert(0)
                first_layer(0, 0, e, 0)
                first_layer(0, 0, e, 1)

            def body(s, b, i):
                e0, e1 = expert(s), expert(s + 1)
                if not (isinstance(s, int) and s == NB - 2):
                    turn(s + 2, b, i + 1, s + 2 < NT if isinstance(s, int) else not phase)
                first_layer(s + 1, 1 - b, e1, 0)
                turn_hidden(s, b)
                first_layer(s + 1, 1 - b, e1, 1)
                second_layer(s, b, e0)

            def slots():
                pe.wait_ge(tok_s, 1)
                for c in range(2):
                    last = nc.tensor.transpose(pw[:, c * P:c * P + RB], rows_f[0:RB, c, :], k.ident[0:RB, 0:RB])
                last.then_inc(tok_pe, 1)

            phase = []

            def routed():
                phase.append("routed")
                pe.wait_ge(all_in, 64 * X)

            def tail():
                turn_hidden(NB - 1, 1)
                second_layer(NB - 1, 1, expert(NB - 1))

            steps(pe, head, body, tail, slots, routed)
    st.close()




def build(nc, ins, out):
    k = Kernel(nc, ins, out)
    k.outer = outer = ExitStack()
    sb = lambda *a: k.sb(outer, *a)
    k.ident, k.upper, k.ones, k.iota = (sb(n, [P, P]) for n in ("ident", "upper", "ones", "iota_row"))
    k.eps = sb("eps", [P, 1])
    k.elr = sb("el_er", [P, NT, 2 * H])
    k.cb = sb("update_bias", [P, D])
    k.w_lin = sb("w_lin", [P, DK, D])
    k.logits = sb("router_logits", [P, NT, X])
    k.choice, k.slot = sb("choices", [P, 2, NT, 2]), sb("slots_of_choices", [P, 2, NT], I32)
    wide, edges, nodes = ExitStack(), ExitStack(), ExitStack()
    k.w_feat, k.b_feat = k.sb(wide, "w_feat", [P, DK, D + 2 * H]), k.sb(wide, "b_feat", [P, D + 2 * H])
    k.xnT = k.sb(wide, "xnT", [P, DK, NP])
    k.count = k.sb(edges, "edges_of_node", [P, NT])
    k.el_e = k.sb(edges, "el_of_edge", [P, STRIP, H])
    k.dst_i = k.sb(edges, "dst_strips", [P, STRIP], I32)
    k.cont = k.sb(edges, "run_continues", [P, STRIP])
    k.xn = k.sb(nodes, "xn", [P, NT, D])
    k.x_in = k.sem("x_in")
    prepare(k)
    project(k)
    collect(k)
    nodes.close()
    scan(k)
    edges.close()
    k.agg = k.sb(wide, "node_sums", [P, NT, GF])
    message(k)
    update(k)
    wide.close()
    k.w_up, k.w_down = sb("w_up", [P, X + 1, DK, F]), sb("w_down", [P, X + 1, FK, D])
    k.b_up, k.b_down = sb("b_up", [P, X + 1, FK]), sb("b_down_rows", [P, X + 1, D])
    k.shared_in, k.routed_in = k.sem("shared_weights_in"), k.sem("routed_weights_in")
    route(k)
    experts(k)
    outer.close()
    k.stack.close()


_INS = ['x', 'src', 'dst', 'L0_gnn_W_lin', 'L0_gnn_b_lin', 'L0_gnn_W_gat', 'L0_gnn_attn_l', 'L0_gnn_attn_r',
        'L0_gnn_gat_bias', 'L0_mix_W_qk', 'L0_mix_b_qk', 'L0_mix_W_v', 'L0_mix_b_v', 'L0_mix_gamma',
        'L0_mix_beta', 'L0_ffn_Wr', 'L0_ffn_W1s', 'L0_ffn_b1s', 'L0_ffn_W2s', 'L0_ffn_b2s', 'L0_ffn_W1p',
        'L0_ffn_b1p', 'L0_ffn_W2p', 'L0_ffn_b2p']


def kernel(**inputs):
    import numpy as _np
    import concourse.bacc as _bacc
    from concourse import mybir as _mybir
    from concourse.bass_utils import run_bass_kernel_spmd as _run

    nc = _bacc.Bacc("TRN2", target_bir_lowering=False, num_devices=1)
    arrays, ins = {}, {}
    for name in _INS:
        a = _np.ascontiguousarray(inputs[name])
        arrays[f"in_{name}"] = a
        ins[name] = nc.dram_tensor(f"in_{name}", a.shape, _mybir.dt.from_np(a.dtype), kind="ExternalInput").ap()
    out = nc.dram_tensor("out_0", (N, D), _mybir.dt.float32, kind="ExternalOutput").ap()
    build(nc, ins, out)
    r = _run(nc, [arrays], core_ids=[0])
    return r.results[0]["out_0"]
```
